# Optimizing a Trainium2 kernel written in Bass

```python
import numpy as np
import jax
import jax.numpy as jnp

def _softmax(x, axis=-1):
    return jax.nn.softmax(x, axis=axis)

def _gelu(x):
    return jax.nn.gelu(x, approximate=True)

def _silu(x):
    return jax.nn.silu(x)

def _sigmoid(x):
    return jax.nn.sigmoid(x)

def _layernorm(x, axis=-1, eps=1e-05):
    m = jnp.mean(x, axis=axis, keepdims=True)
    v = jnp.var(x, axis=axis, keepdims=True)
    return (x - m) / jnp.sqrt(v + eps)

def _scatter_add(tgt, idx, src, axis=0):
    return tgt.at[idx].add(src)

def _segment_sum(src, seg, n):
    return jax.ops.segment_sum(src, seg, n)
kernel_name = 'mk_early_fusion_embed_d1_tok_img512_r4_985651'

def setup_inputs(seed: int=0):
    np.random.seed(seed)
    _w = jnp.asarray

    def _rec_inputs():
        import jax
        import jax.numpy as jnp
        _rk = jax.random.key(seed)
        x = 7.22013e-05 + 1.00017 * jax.random.normal(jax.random.fold_in(_rk, 1), (4, 512, 64, 2), jnp.float32)
        x_txt = jax.random.randint(jax.random.fold_in(_rk, 51), (4, 77), 0, 24997, jnp.int32)
        mask_BS_f1_0 = jnp.where(jnp.ones((4, 77), dtype=bool), 1.0, 0.0).astype(jnp.float32)
        return (x, x_txt, mask_BS_f1_0)
    x, x_txt, mask_BS_f1_0 = _rec_inputs()

    def _L0_tok_setup():
        import jax, jax.numpy as jnp
        import numpy as np
        B, L, C = (8, 512, 64)
        D = C // 8

        def _attn(q, k, v, scale):
            scores = jnp.einsum('bld,bmd->blm', q, k) / scale
            w = jax.nn.softmax(scores, axis=-1)
            return jnp.einsum('blm,bmd->bld', w, v)
        key = jax.random.key(seed)
        ks = jax.random.split(key, 16)
        he = lambda k, cin, cout: jax.random.normal(k, (cin, cout), jnp.float32) * np.sqrt(2.0 / cin)
        inp = {'x': jax.random.normal(ks[0], (B, L, C, 2), jnp.float32)}
        dims = [D, D, C, D, D, C, D, D, C, D, D, C]
        for i, dout in enumerate(dims):
            inp[f'w{i + 1}'] = he(ks[i + 1], C, dout)
        inp['alpha'] = jnp.zeros((1,), jnp.float32)
        inp['gamma'] = jnp.zeros((1,), jnp.float32)
        return inp
    _L0_tok_all = _L0_tok_setup()
    _L0_tok_in = {k: v for k, v in _L0_tok_all.items() if k in ('w1', 'w2', 'w3', 'w4', 'w5', 'w6', 'w7', 'w8', 'w9', 'w10', 'w11', 'w12', 'alpha', 'gamma')}
    del _L0_tok_all

    def _L0_txt_setup():
        import jax, jax.numpy as jnp
        import numpy as np
        B, S, D, H, L, F, V = (128, 200, 128, 8, 4, 512, 100001)
        HD = D // H

        def layer_norm(x, g, b, eps=1e-05):
            mu = jnp.mean(x, axis=-1, keepdims=True)
            var = jnp.mean((x - mu) ** 2, axis=-1, keepdims=True)
            return (x - mu) / jnp.sqrt(var + eps) * g + b
        key = jax.random.key(seed)
        ks = jax.random.split(key, 12)
        r = lambda k, shape: jax.random.normal(k, shape, jnp.float32) * 0.02
        item_seq = jax.random.randint(ks[0], (B, S), 1, V)
        attention_mask = jnp.ones((B, S), jnp.float32)
        item_emb = r(ks[1], (V, D)).at[0].set(0.0)
        pos_emb = r(ks[2], (S, D))
        return {'item_seq': item_seq, 'attention_mask': attention_mask, 'item_emb': item_emb, 'pos_emb': pos_emb, 'Wq': r(ks[3], (L, D, D)), 'bq': jnp.zeros((L, D)), 'Wk': r(ks[4], (L, D, D)), 'bk': jnp.zeros((L, D)), 'Wv': r(ks[5], (L, D, D)), 'bv': jnp.zeros((L, D)), 'Wo': r(ks[6], (L, D, D)), 'bo': jnp.zeros((L, D)), 'ln1_g': jnp.ones((L, D)), 'ln1_b': jnp.zeros((L, D)), 'ln2_g': jnp.ones((L, D)), 'ln2_b': jnp.zeros((L, D)), 'W1': r(ks[7], (L, D, F)), 'b1': jnp.zeros((L, F)), 'W2': r(ks[8], (L, F, D)), 'b2': jnp.zeros((L, D)), 'lnf_g': jnp.ones((D,)), 'lnf_b': jnp.zeros((D,))}
    _L0_txt_all = _L0_txt_setup()
    _L0_txt_in = {k: v for k, v in _L0_txt_all.items() if k in ('item_emb', 'pos_emb', 'Wq', 'bq', 'Wk', 'bk', 'Wv', 'bv', 'Wo', 'bo', 'ln1_g', 'ln1_b', 'ln2_g', 'ln2_b', 'W1', 'b1', 'W2', 'b2', 'lnf_g', 'lnf_b')}
    del _L0_txt_all

    def _L0_attn_setup():
        import jax, jax.numpy as jnp
        import numpy as np
        D_MODEL, N_HEADS, D_VALUE = (128, 8, 64)
        D_HEAD = D_MODEL // N_HEADS

        def _elu_feature_map(t):
            return jax.nn.elu(t) + 1.0
        key = jax.random.key(seed)
        ks = jax.random.split(key, 5)
        B, T = (2, 512)
        x = jax.random.normal(ks[0], (B, T, D_MODEL), dtype=jnp.float32)
        scale = 0.02
        W_q = jax.random.normal(ks[1], (N_HEADS * D_HEAD, D_MODEL), dtype=jnp.float32) * scale
        W_k = jax.random.normal(ks[2], (N_HEADS * D_HEAD, D_MODEL), dtype=jnp.float32) * scale
        W_v = jax.random.normal(ks[3], (N_HEADS * D_VALUE, D_MODEL), dtype=jnp.float32) * scale
        W_out = jax.random.normal(ks[4], (D_MODEL, N_HEADS * D_VALUE), dtype=jnp.float32) * scale
        return {'x': x, 'W_q': W_q, 'W_k': W_k, 'W_v': W_v, 'W_out': W_out}
    _L0_attn_all = _L0_attn_setup()
    _L0_attn_in = {k: v for k, v in _L0_attn_all.items() if k in ('W_q', 'W_k', 'W_v', 'W_out')}
    del _L0_attn_all

    def _L0_ffn_setup():
        import jax, jax.numpy as jnp
        import numpy as np
        B, N, DIM = (1, 512, 128)
        DH, H = (64, 8)
        E, FF = (8, 512)

        def _layernorm(x, g, b, eps=1e-05):
            mu = jnp.mean(x, axis=-1, keepdims=True)
            var = jnp.mean(jnp.square(x - mu), axis=-1, keepdims=True)
            return (x - mu) * jax.lax.rsqrt(var + eps) * g + b

        def _l2norm(x, eps=1e-12):
            return x / jnp.sqrt(jnp.sum(jnp.square(x), axis=-1, keepdims=True) + eps)
        key = jax.random.key(seed)
        ks = jax.random.split(key, 12)
        g = lambda k, shape: jax.random.normal(k, shape, jnp.float32) * 0.02
        return {'x': jax.random.normal(ks[0], (B, N, DIM), jnp.float32), 'ln_g': jnp.ones((DIM,), jnp.float32), 'ln_b': jnp.zeros((DIM,), jnp.float32), 'Wq': g(ks[1], (DIM, DIM)), 'Wk': g(ks[2], (DIM, DIM)), 'Wv': g(ks[3], (DIM, DIM)), 'Wo': g(ks[4], (DIM, DIM)), 'qn_g': jnp.ones((DH,), jnp.float32), 'kn_g': jnp.ones((DH,), jnp.float32), 'gate_W': g(ks[5], (DIM, E)), 'gate_b': jnp.zeros((E,), jnp.float32), 'W1': g(ks[6], (E, DIM, FF)), 'b1': jnp.zeros((E, FF), jnp.float32), 'W2': g(ks[7], (E, FF, DIM)), 'b2': jnp.zeros((E, DIM), jnp.float32)}
    _L0_ffn_all = _L0_ffn_setup()
    _L0_ffn_in = {k: v for k, v in _L0_ffn_all.items() if k in ('ln_g', 'ln_b', 'Wq', 'Wk', 'Wv', 'Wo', 'qn_g', 'kn_g', 'gate_W', 'gate_b', 'W1', 'b1', 'W2', 'b2')}
    del _L0_ffn_all
    return {'x': x, 'x_txt': x_txt, 'mask_BS_f1_0': mask_BS_f1_0, 'L0_tok_w1': _L0_tok_in['w1'], 'L0_tok_w2': _L0_tok_in['w2'], 'L0_tok_w3': _L0_tok_in['w3'], 'L0_tok_w4': _L0_tok_in['w4'], 'L0_tok_w5': _L0_tok_in['w5'], 'L0_tok_w6': _L0_tok_in['w6'], 'L0_tok_w7': _L0_tok_in['w7'], 'L0_tok_w8': _L0_tok_in['w8'], 'L0_tok_w9': _L0_tok_in['w9'], 'L0_tok_w10': _L0_tok_in['w10'], 'L0_tok_w11': _L0_tok_in['w11'], 'L0_tok_w12': _L0_tok_in['w12'], 'L0_tok_alpha': _L0_tok_in['alpha'], 'L0_tok_gamma': _L0_tok_in['gamma'], 'L0_txt_item_emb': _L0_txt_in['item_emb'], 'L0_txt_pos_emb': _L0_txt_in['pos_emb'], 'L0_txt_Wq': _L0_txt_in['Wq'], 'L0_txt_bq': _L0_txt_in['bq'], 'L0_txt_Wk': _L0_txt_in['Wk'], 'L0_txt_bk': _L0_txt_in['bk'], 'L0_txt_Wv': _L0_txt_in['Wv'], 'L0_txt_bv': _L0_txt_in['bv'], 'L0_txt_Wo': _L0_txt_in['Wo'], 'L0_txt_bo': _L0_txt_in['bo'], 'L0_txt_ln1_g': _L0_txt_in['ln1_g'], 'L0_txt_ln1_b': _L0_txt_in['ln1_b'], 'L0_txt_ln2_g': _L0_txt_in['ln2_g'], 'L0_txt_ln2_b': _L0_txt_in['ln2_b'], 'L0_txt_W1': _L0_txt_in['W1'], 'L0_txt_b1': _L0_txt_in['b1'], 'L0_txt_W2': _L0_txt_in['W2'], 'L0_txt_b2': _L0_txt_in['b2'], 'L0_txt_lnf_g': _L0_txt_in['lnf_g'], 'L0_txt_lnf_b': _L0_txt_in['lnf_b'], 'L0_attn_W_q': _L0_attn_in['W_q'], 'L0_attn_W_k': _L0_attn_in['W_k'], 'L0_attn_W_v': _L0_attn_in['W_v'], 'L0_attn_W_out': _L0_attn_in['W_out'], 'L0_ffn_ln_g': _L0_ffn_in['ln_g'], 'L0_ffn_ln_b': _L0_ffn_in['ln_b'], 'L0_ffn_Wq': _L0_ffn_in['Wq'], 'L0_ffn_Wk': _L0_ffn_in['Wk'], 'L0_ffn_Wv': _L0_ffn_in['Wv'], 'L0_ffn_Wo': _L0_ffn_in['Wo'], 'L0_ffn_qn_g': _L0_ffn_in['qn_g'], 'L0_ffn_kn_g': _L0_ffn_in['kn_g'], 'L0_ffn_gate_W': _L0_ffn_in['gate_W'], 'L0_ffn_gate_b': _L0_ffn_in['gate_b'], 'L0_ffn_W1': _L0_ffn_in['W1'], 'L0_ffn_b1': _L0_ffn_in['b1'], 'L0_ffn_W2': _L0_ffn_in['W2'], 'L0_ffn_b2': _L0_ffn_in['b2']}

def reference(x, x_txt, mask_BS_f1_0, L0_tok_w1, L0_tok_w2, L0_tok_w3, L0_tok_w4, L0_tok_w5, L0_tok_w6, L0_tok_w7, L0_tok_w8, L0_tok_w9, L0_tok_w10, L0_tok_w11, L0_tok_w12, L0_tok_alpha, L0_tok_gamma, L0_txt_item_emb, L0_txt_pos_emb, L0_txt_Wq, L0_txt_bq, L0_txt_Wk, L0_txt_bk, L0_txt_Wv, L0_txt_bv, L0_txt_Wo, L0_txt_bo, L0_txt_ln1_g, L0_txt_ln1_b, L0_txt_ln2_g, L0_txt_ln2_b, L0_txt_W1, L0_txt_b1, L0_txt_W2, L0_txt_b2, L0_txt_lnf_g, L0_txt_lnf_b, L0_attn_W_q, L0_attn_W_k, L0_attn_W_v, L0_attn_W_out, L0_ffn_ln_g, L0_ffn_ln_b, L0_ffn_Wq, L0_ffn_Wk, L0_ffn_Wv, L0_ffn_Wo, L0_ffn_qn_g, L0_ffn_kn_g, L0_ffn_gate_W, L0_ffn_gate_b, L0_ffn_W1, L0_ffn_b1, L0_ffn_W2, L0_ffn_b2):
    import jax
    import jax.numpy as jnp

    def _L0_tok_ref(x, w1, w2, w3, w4, w5, w6, w7, w8, w9, w10, w11, w12, alpha, gamma):
        import jax, jax.numpy as jnp
        import numpy as np
        B, L, C = (8, 512, 64)
        D = C // 8

        def _attn(q, k, v, scale):
            scores = jnp.einsum('bld,bmd->blm', q, k) / scale
            w = jax.nn.softmax(scores, axis=-1)
            return jnp.einsum('blm,bmd->bld', w, v)
        ecg = x[:, :, :, 0]
        pcg = x[:, :, :, 1]
        proj = lambda f, w: jnp.einsum('blc,cd->bld', f, w)
        scale = jnp.sqrt(jnp.asarray(D, x.dtype))
        qkv_ecg_intra = _attn(proj(ecg, w1), proj(ecg, w2), proj(ecg, w3), scale)
        qkv_ecg_inter = _attn(proj(ecg, w4), proj(pcg, w5), proj(pcg, w6), scale)
        ecg_out = qkv_ecg_inter + alpha * qkv_ecg_intra
        qkv_pcg_intra = _attn(proj(pcg, w7), proj(pcg, w8), proj(pcg, w9), scale)
        qkv_pcg_inter = _attn(proj(pcg, w10), proj(ecg, w11), proj(ecg, w12), scale)
        pcg_out = qkv_pcg_inter + gamma * qkv_pcg_intra
        return jnp.concatenate([ecg_out, pcg_out], axis=-1)

    def _L0_txt_ref(item_seq, attention_mask, item_emb, pos_emb, Wq, bq, Wk, bk, Wv, bv, Wo, bo, ln1_g, ln1_b, ln2_g, ln2_b, W1, b1, W2, b2, lnf_g, lnf_b):
        import jax, jax.numpy as jnp
        import numpy as np
        B, S, D, H, L, F, V = (128, 200, 128, 8, 4, 512, 100001)
        HD = D // H

        def layer_norm(x, g, b, eps=1e-05):
            mu = jnp.mean(x, axis=-1, keepdims=True)
            var = jnp.mean((x - mu) ** 2, axis=-1, keepdims=True)
            return (x - mu) / jnp.sqrt(var + eps) * g + b
        b, s = item_seq.shape
        x = item_emb[item_seq] + pos_emb[None, :s, :]
        causal = jnp.triu(jnp.ones((s, s), bool), 1)
        pad = attention_mask[:, None, None, :] == 0
        mask = causal[None, None, :, :] | pad
        scale = 1.0 / np.sqrt(HD)
        for l in range(L):
            h = layer_norm(x, ln1_g[l], ln1_b[l])
            q = (h @ Wq[l] + bq[l]).reshape(b, s, H, HD)
            k = (h @ Wk[l] + bk[l]).reshape(b, s, H, HD)
            v = (h @ Wv[l] + bv[l]).reshape(b, s, H, HD)
            scores = jnp.einsum('bqhd,bkhd->bhqk', q, k) * scale
            scores = jnp.where(mask, -jnp.inf, scores)
            attn = jax.nn.softmax(scores, axis=-1)
            ctx = jnp.einsum('bhqk,bkhd->bqhd', attn, v).reshape(b, s, D)
            x = x + ctx @ Wo[l] + bo[l]
            h2 = layer_norm(x, ln2_g[l], ln2_b[l])
            x = x + jax.nn.gelu(h2 @ W1[l] + b1[l], approximate=False) @ W2[l] + b2[l]
        return layer_norm(x, lnf_g, lnf_b)

    def _L0_attn_ref(x, W_q, W_k, W_v, W_out):
        import jax, jax.numpy as jnp
        import numpy as np
        D_MODEL, N_HEADS, D_VALUE = (128, 8, 64)
        D_HEAD = D_MODEL // N_HEADS

        def _elu_feature_map(t):
            return jax.nn.elu(t) + 1.0
        B, T, D = x.shape
        H, dh, dv = (N_HEADS, D_HEAD, D_VALUE)
        Q = _elu_feature_map((x @ W_q.T).reshape(B, T, H, dh)).transpose(0, 2, 1, 3)
        K = _elu_feature_map((x @ W_k.T).reshape(B, T, H, dh)).transpose(0, 2, 1, 3)
        V = (x @ W_v.T).reshape(B, T, H, dv).transpose(0, 2, 1, 3)
        KV = jnp.einsum('bhti,bhtj->bhtij', K, V)
        S = jnp.cumsum(KV, axis=2)
        z = jnp.cumsum(K, axis=2)
        num = jnp.einsum('bhti,bhtij->bhtj', Q, S)
        den = jnp.maximum(jnp.einsum('bhti,bhti->bht', Q, z), 1e-06)[..., None]
        out = (num / den).transpose(0, 2, 1, 3).reshape(B, T, H * dv)
        return out @ W_out.T

    def _L0_ffn_ref(x, ln_g, ln_b, Wq, Wk, Wv, Wo, qn_g, kn_g, gate_W, gate_b, W1, b1, W2, b2):
        import jax, jax.numpy as jnp
        import numpy as np
        B, N, DIM = (1, 512, 128)
        DH, H = (64, 8)
        E, FF = (8, 512)

        def _layernorm(x, g, b, eps=1e-05):
            mu = jnp.mean(x, axis=-1, keepdims=True)
            var = jnp.mean(jnp.square(x - mu), axis=-1, keepdims=True)
            return (x - mu) * jax.lax.rsqrt(var + eps) * g + b

        def _l2norm(x, eps=1e-12):
            return x / jnp.sqrt(jnp.sum(jnp.square(x), axis=-1, keepdims=True) + eps)
        b, n, d = x.shape
        dh = qn_g.shape[0]
        h = d // dh
        hx = _layernorm(x, ln_g, ln_b)
        q = (hx @ Wq).reshape(b, n, h, dh).transpose(0, 2, 1, 3)
        k = (hx @ Wk).reshape(b, n, h, dh).transpose(0, 2, 1, 3)
        v = (hx @ Wv).reshape(b, n, h, dh).transpose(0, 2, 1, 3)
        scale = jnp.sqrt(jnp.float32(dh))
        q = _l2norm(q) * scale * qn_g
        k = _l2norm(k) * scale * kn_g
        scores = jnp.einsum('bhqd,bhkd->bhqk', q, k) * dh ** (-0.5)
        causal = jnp.tril(jnp.ones((n, n), bool))
        scores = jnp.where(causal, scores, jnp.finfo(scores.dtype).min)
        attn = jax.nn.softmax(scores, axis=-1)
        o = jnp.einsum('bhqk,bhkd->bhqd', attn, v)
        y = o.transpose(0, 2, 1, 3).reshape(b, n, d) @ Wo
        gate = jax.nn.softmax(y @ gate_W + gate_b, axis=-1)
        hid = jax.nn.gelu(jnp.einsum('bnd,edf->bnef', y, W1) + b1)
        eo = jnp.einsum('bnef,efd->bned', hid, W2) + b2
        out = jnp.einsum('bned,bne->bnd', eo, gate)
        return out
    h = _L0_tok_ref(x, L0_tok_w1, L0_tok_w2, L0_tok_w3, L0_tok_w4, L0_tok_w5, L0_tok_w6, L0_tok_w7, L0_tok_w8, L0_tok_w9, L0_tok_w10, L0_tok_w11, L0_tok_w12, L0_tok_alpha, L0_tok_gamma)
    h = jnp.concatenate([h, _L0_txt_ref(x_txt, mask_BS_f1_0, L0_txt_item_emb, L0_txt_pos_emb, L0_txt_Wq, L0_txt_bq, L0_txt_Wk, L0_txt_bk, L0_txt_Wv, L0_txt_bv, L0_txt_Wo, L0_txt_bo, L0_txt_ln1_g, L0_txt_ln1_b, L0_txt_ln2_g, L0_txt_ln2_b, L0_txt_W1, L0_txt_b1, L0_txt_W2, L0_txt_b2, L0_txt_lnf_g, L0_txt_lnf_b)], axis=1)
    h = h + _L0_attn_ref(_layernorm(h, axis=-1), L0_attn_W_q, L0_attn_W_k, L0_attn_W_v, L0_attn_W_out)
    h = h + _L0_ffn_ref(_layernorm(h, axis=-1), L0_ffn_ln_g, L0_ffn_ln_b, L0_ffn_Wq, L0_ffn_Wk, L0_ffn_Wv, L0_ffn_Wo, L0_ffn_qn_g, L0_ffn_kn_g, L0_ffn_gate_W, L0_ffn_gate_b, L0_ffn_W1, L0_ffn_b1, L0_ffn_W2, L0_ffn_b2)
    return h

_drawn_inputs = setup_inputs


def setup_inputs(seed=0):
    import zlib

    import numpy as np

    out = dict(_drawn_inputs(seed))
    spreads = {'L0_txt_bq': (0.0, 0.8),
     'L0_txt_bk': (0.0, 2.0),
     'L0_txt_bv': (0.0, 0.1),
     'L0_txt_bo': (0.0, 0.1),
     'L0_txt_ln1_g': (1.0, 0.2),
     'L0_txt_ln1_b': (0.0, 0.376),
     'L0_txt_ln2_g': (1.0, 0.6),
     'L0_txt_ln2_b': (0.0, 0.369),
     'L0_txt_b1': (0.0, 0.1),
     'L0_txt_b2': (0.0, 0.1),
     'L0_txt_lnf_g': (1.0, 0.2),
     'L0_txt_lnf_b': (0.0, 0.1),
     'L0_ffn_ln_g': (1.0, 0.6),
     'L0_ffn_ln_b': (0.0, 0.8),
     'L0_ffn_qn_g': (1.0, 0.6),
     'L0_ffn_kn_g': (1.0, 0.6),
     'L0_ffn_gate_b': (0.0, 0.8),
     'L0_ffn_b1': (0.0, 0.598),
     'L0_ffn_b2': (0.0, 0.601)}
    factors = {'L0_txt_Wq': 8.0,
     'L0_txt_Wk': 8.0,
     'L0_attn_W_q': 8.0,
     'L0_attn_W_k': 8.0,
     'L0_ffn_Wq': 8.0,
     'L0_ffn_Wk': 8.0,
     'L0_ffn_Wv': 8.0,
     'L0_ffn_Wo': 8.0,
     'L0_ffn_gate_W': 8.0,
     'L0_ffn_W1': 8.0,
     'L0_ffn_W2': 3.898}
    for name, (base, spread) in spreads.items():
        noise = np.random.default_rng([zlib.crc32(name.encode()), seed]).standard_normal(out[name].shape)
        drawn = base * np.exp(spread * noise) if base else spread * noise
        out[name] = jnp.asarray(drawn.astype(out[name].dtype))
    for name, factor in factors.items():
        out[name] = (out[name] * factor).astype(out[name].dtype)
    return out
```

```python
from contextlib import ExitStack

import concourse.bass as bass
from concourse import mybir

F32 = mybir.dt.float32
BF16 = mybir.dt.bfloat16
I32 = mybir.dt.int32
U32 = mybir.dt.uint32
ALU = mybir.AluOpType
ACT = mybir.ActivationFunctionType
AX = mybir.AxisListType

P = 128
BATCH, TOK, CH = 4, 512, 64
TXT = 77
D = 2 * CH
TT = TOK // P
TILES = TT + 1
T = TOK + TXT
ROWS = [P] * TT + [TXT]
NEG = -1.0e30

DQ = CH // 8
UNITS = 4 * TT

LAYERS, HEADS, HD, FF = 4, 8, 16, 512
SEQ4 = BATCH * TXT
KT = FF // P

LH, LD, LV = 8, 16, 64
LVA = LV + 1
FH, FD = 2, 64
E, EF = 8, 512
EK = EF // P


def fusion_kernel(nc, A, out):
    ctx = ExitStack()
    with ctx:
        def sb(name, shape, dt=F32):
            return ctx.enter_context(nc.sbuf_tensor(name, shape, dt))

        def sem(name):
            return ctx.enter_context(nc.semaphore(name))

        TP = TILES * P
        vec_names = [("bq", LAYERS), ("bk", LAYERS), ("g1", LAYERS), ("c1", LAYERS), ("g2", LAYERS),
                     ("c2", LAYERS), ("b1", LAYERS * KT), ("eb", E * EK), ("fg", 1), ("fc", 1),
                     ("qn", 1), ("kn", 1)]
        VEC, at = {}, 0
        for n, c in vec_names:
            VEC[n] = at
            at += c
        NVEC = at
        seq = sb("seq", [P, BATCH * TILES, D])
        ident = sb("ident", [P, P])
        neghalf = sb("neghalf", [P, 4 * TILES])
        eps = sb("eps", [P, TILES])
        tiny = sb("tiny", [P, 4 * TILES])
        mix = sb("mix", [P, 2])
        hmask = sb("hmask", [P, HEADS])
        vrow = sb("vrow", [NVEC, D])
        vcol = sb("vcol", [P, NVEC])
        bq4 = sb("bq4", [P, LAYERS])
        qkg = sb("qkg", [P, 1])
        sT = sb("sT", [P, TP])
        w_lraw = sb("w_lraw", [P, 6, D])
        w_loraw = sb("w_loraw", [P, LH * LV])
        w_lT = sb("w_lT", [P, 6 * P])
        w_loT = sb("w_loT", [P, 4, D])
        ones = sb("ones", [P, T])
        hblock = sb("hblock", [P, P])
        lsbd = sb("lsbd", [P, LH * LV])
        causal01 = sb("causal01", [P, P])
        w_fqkv = sb("w_fqkv", [P, 3 * D])
        w_fo = sb("w_fo", [P, D])
        w_gate = sb("w_gate", [P, E])
        gb_r = sb("gb_r", [P, E])
        b2_e = sb("b2_e", [E, D])
        identb = sb("identb", [P, P], BF16)
        causalb = sb("causalb", [P, P], BF16)
        yT = sb("yT", [P, TP])
        w1_e = sb("w1_e", [P, E, EF])
        w2_e = sb("w2_e", [P, E * EK, D])

        first_half = ExitStack()

        def sb1(name, shape, dt=F32):
            return first_half.enter_context(nc.sbuf_tensor(name, shape, dt))

        x_in = sb1("x_in", [P, TT, D])
        w_qk = sb1("w_qk", [P, 2 * P])
        w_tv = sb1("w_tv", [P, 4 * CH])
        xT = sb1("xT", [P, TOK])
        qT = sb1("qT", [P, TOK])
        kT = sb1("kT", [P, TOK])
        v_tok = sb1("v_tok", [P, TT, 4 * CH])
        prob = sb1("prob", [P, 2, TOK])
        probT = sb1("probT", [P, 2, TOK])
        nmax = sb1("nmax", [P, UNITS])
        psum_e = sb1("psum_e", [P, UNITS])
        rsum = sb1("rsum", [P, UNITS])
        intra = sb1("intra", [P, 2, CH])
        tx = sb1("tx", [TXT, BATCH, D])
        tx_res = sb1("tx_res", [TXT, BATCH, D])
        tx_n = sb1("tx_n", [TXT, BATCH, D])
        tx_st = sb1("tx_st", [TXT, BATCH, 6])
        tx_mv = sb1("tx_mv", [TXT, BATCH, 2])
        tx_ve = sb1("tx_ve", [TXT, BATCH])
        tx_rs = sb1("tx_rs", [TXT, BATCH])
        tok_idx = sb1("tok_idx", [TXT, BATCH], I32)
        pos = sb1("pos", [TXT, D])
        padrow = sb1("padrow", [TXT, BATCH, TXT])
        causal_t = sb1("causal_t", [TXT, TXT])
        tmask = sb1("tmask", [TXT, BATCH, TXT])
        w_q = sb1("w_q", [D, D])
        w_k = sb1("w_k", [D, D])
        w_v = sb1("w_v", [D, D])
        w_o = sb1("w_o", [D, D])
        w_1 = sb1("w_1", [D, FF])
        w_2 = sb1("w_2", [P, KT, D])
        bv_r = sb1("bv_r", [TXT, LAYERS, D])
        bo_r = sb1("bo_r", [TXT, LAYERS, D])
        b2_r = sb1("b2_r", [TXT, LAYERS, D])
        lnf_g = sb1("lnf_g", [TXT, D])
        lnf_b = sb1("lnf_b", [TXT, D])
        hT = sb1("hT", [P, SEQ4])
        tqT = sb1("tqT", [P, SEQ4])
        kbd = sb1("kbd", [P, BATCH, HEADS * TXT])
        tv = sb1("tv", [TXT, BATCH, HEADS, HD + 1])
        ts = sb1("ts", [TXT, BATCH, HEADS * TXT])
        tpT = sb1("tpT", [TXT, BATCH, HEADS * TXT])
        tnm = sb1("tnm", [TXT, BATCH, HEADS])
        trs = sb1("trs", [TXT, BATCH, HEADS])
        tctx = sb1("tctx", [TXT, BATCH, D])
        cT = sb1("cT", [P, SEQ4])
        gact = sb1("gact", [P, KT, SEQ4])
        first_half.close()

        qkv = sb("qkv", [P, TILES, 3 * D])
        sq = sb("sq", [P, TILES, 2 * D])
        ss = sb("ss", [P, TILES, 2 * FH])
        ssr = sb("ssr", [P, TILES, 2 * FH])
        fp = sb("fp", [P, 2, T])
        fpn = sb("fpn", [P, 2, T])
        fpT = sb("fpT", [P, 2, 512])
        fnm = sb("fnm", [P, FH * TILES])
        fsum = sb("fsum", [P, FH * TILES])
        frs = sb("frs", [P, FH * TILES])
        foT = sb("foT", [P, T])
        fq = sb("fq", [P, T])
        fk = sb("fk", [P, T])
        hid = sb("hid", [P, 2, EK, T])
        acc = sb("acc", [P, TILES, D])
        lv = sb("lv", [P, TILES, LH * LV])
        lqbd = sb("lqbd", [P, 2, LH, P])
        la = sb("la", [P, 2, LH, P])
        lktok = sb("lktok", [P, TT, P])
        lo = sb("lo", [P, 2, 4, P])
        xn = sb("xn", [P, TILES, D])
        lt1 = sb("lt1", [P, T])
        lt2 = sb("lt2", [P, T])
        lz = sb("lz", [P, T])
        lq = sb("lq", [P, T])
        lk = sb("lk", [P, T])
        st5 = sb("st5", [P, TILES, 6])
        mv5 = sb("mv5", [P, TILES, 2])
        va5 = sb("va5", [P, TILES])
        vb5 = sb("vb5", [P, TILES])
        rs5 = sb("rs5", [P, TILES])
        lg = sb("lg", [P, TILES, E])
        lgm = sb("lgm", [P, TILES])
        gate = sb("gate", [P, TILES, E])
        gateT = sb("gateT", [E, T])

        ps = ctx.enter_context(nc.psum_tensor("ps", [P, 8, 512], F32))
        psf = ps[:, :, :].rearrange("p b n -> p (b n)")

        def banks(first, width, rows_=P):
            return psf[0:rows_, first * 512:first * 512 + width]

        S = {}
        for n in ("""const_pool x_loaded qk_weights params txt_ids txt_embed setup_psum setup_done
                  proj_full xT_ready q_ready k_ready va_ready vb_ready
                  score_full max_ready prob_ready probT_full probT_act probT_dve out_full out_done
                  wq_loaded wk_loaded wv_loaded wo_loaded w1_loaded w2_loaded
                  tx_stat tx_rstd tx_resid tx_norm tx_normT tx_hT tx_k tx_q tx_v tx_kbd tx_qs tx_vs
                  tx_score tx_masked tx_shift tx_exp tx_pt tx_pT tx_pv tx_ctx tx_ct tx_cT tx_o tx_x
                  tx_f1 tx_g tx_f2 seq_tok seq_txt
                  block_params l_weights e_weights l_wT l_wT_done
                  stat5 rstd5 norm5 normT5 hT5
                  la_qk la_min la_exp la_feat la_vfull la_vdone la_qz la_den la_q la_ktps la_ktok la_qbd
                  la_at la_masked la_ot la_lo la_state la_sbd la_y seq_tile seq_lin
                  fa_qkv fa_qkv_sb fa_ss fa_rs fa_norm fa_T fa_qT fa_kT fa_s fa_max fa_exp fa_pn fa_pt fa_pT_act fa_pT_dve fa_o fa_oT
                  y_ps y_done g_ps g_shift g_exp g_done g_tps g_T b2_ps acc_init
                  up up_done down acc_done stored""").split():
            S[n] = sem(n)

        block = ctx.enter_context(nc.Block())

        def nth(turn, per_turn, k):
            return turn * per_turn + k

        def add_bias(pool, rows_, l):
            pool.tensor_tensor(tx_res[:, :, :], tx[:, :, :],
                               rows_[:, bass.ds(l, 1), :].broadcast_to([TXT, BATCH, D]), ALU.add).then_inc(S["tx_resid"], 1)

        @block.sync
        def _(sp):
            tokw = [("w1", 0, 0), ("w4", 0, 1), ("w7", 1, 2), ("w10", 1, 3)]
            tokk = [("w2", 0, 0), ("w5", 1, 1), ("w8", 1, 2), ("w11", 0, 3)]
            tokv = [("w3", 0, 0), ("w6", 1, 1), ("w9", 1, 2), ("w12", 0, 3)]
            sp.dma_start(x_in[:, :, :], A["x"][0].rearrange("(t p) c s -> p t (c s)", p=P)).then_inc(S["x_loaded"], 16)
            sp.dma_start(tok_idx[:, :], A["x_txt"].rearrange("b s -> s b"), allow_slow_non_contiguous=True).then_inc(S["txt_ids"], 16)
            sp.wait_ge(S["const_pool"], 1)
            for name, chan, a in tokw:
                sp.dma_start(w_qk[chan:D:2, 32 * a:32 * a + DQ], A[f"L0_tok_{name}"]).then_inc(S["qk_weights"], 16)
            for name, chan, a in tokk:
                sp.dma_start(w_qk[chan:D:2, P + 32 * a:P + 32 * a + DQ], A[f"L0_tok_{name}"]).then_inc(S["qk_weights"], 16)
            for name, chan, a in tokv:
                sp.dma_start(w_tv[chan:D:2, CH * a:CH * (a + 1)], A[f"L0_tok_{name}"]).then_inc(S["qk_weights"], 16)
            def param(dst, src):
                sp.dma_start(dst, src).then_inc(S["params"], 16)
            param(mix[:, 0:1], A["L0_tok_alpha"].partition_broadcast(P))
            param(mix[:, 1:2], A["L0_tok_gamma"].partition_broadcast(P))
            for n, src in (("bq", "txt_bq"), ("bk", "txt_bk"), ("g1", "txt_ln1_g"), ("c1", "txt_ln1_b"),
                           ("g2", "txt_ln2_g"), ("c2", "txt_ln2_b")):
                param(vrow[VEC[n]:VEC[n] + LAYERS, :], A[f"L0_{src}"])
            param(vrow[VEC["b1"]:VEC["b1"] + LAYERS * KT, :], A["L0_txt_b1"].rearrange("l (j p) -> (l j) p", p=P))
            param(vrow[VEC["eb"]:VEC["eb"] + E * EK, :], A["L0_ffn_b1"].rearrange("e (j p) -> (e j) p", p=P))
            param(vrow[VEC["fg"]:VEC["fg"] + 1, :], A["L0_ffn_ln_g"].unsqueeze(0))
            param(vrow[VEC["fc"]:VEC["fc"] + 1, :], A["L0_ffn_ln_b"].unsqueeze(0))
            for h in range(FH):
                param(vrow[VEC["qn"]:VEC["qn"] + 1, h * FD:(h + 1) * FD], A["L0_ffn_qn_g"].unsqueeze(0))
                param(vrow[VEC["kn"]:VEC["kn"] + 1, h * FD:(h + 1) * FD], A["L0_ffn_kn_g"].unsqueeze(0))
            param(pos[:, :], A["L0_txt_pos_emb"][0:TXT, :])
            for b in range(BATCH):
                param(padrow[:, b, :], A["mask_BS_f1_0"][b].partition_broadcast(TXT))
            param(bv_r[:, :, :], A["L0_txt_bv"].partition_broadcast(TXT))
            param(bo_r[:, :, :], A["L0_txt_bo"].partition_broadcast(TXT))
            param(b2_r[:, :, :], A["L0_txt_b2"].partition_broadcast(TXT))
            param(lnf_g[:, :], A["L0_txt_lnf_g"].partition_broadcast(TXT))
            param(lnf_b[:, :], A["L0_txt_lnf_b"].partition_broadcast(TXT))

            with sp.Fori(1, BATCH) as b:
                sp.wait_ge(S["proj_full"], nth(b, 5, -4))
                sp.dma_start(x_in[:, :, :], A["x"][b, :, :, :].rearrange("(t p) c s -> p t (c s)", p=P)).then_inc(S["x_loaded"], 16)

            def layer_weights(l, first=False):
                for dst, src, loaded, used, per in (
                        (w_k[:, :], "Wk", "wk_loaded", "tx_k", 1),
                        (w_q[:, :], "Wq", "wq_loaded", "tx_q", 1),
                        (w_v[:, :], "Wv", "wv_loaded", "tx_v", 1),
                        (w_o[:, :], "Wo", "wo_loaded", "tx_o", 1),
                        (w_1[:, :], "W1", "w1_loaded", "tx_f1", KT),
                        (w_2[:, :, :], "W2", "w2_loaded", "tx_f2", 1)):
                    if not first:
                        sp.wait_ge(S[used], l * per)
                    t = A[f"L0_txt_{src}"]
                    s = t[l, :, :]
                    if src == "W2":
                        s = s.rearrange("(j p) n -> p j n", p=P)
                    sp.dma_start(dst, s).then_inc(S[loaded], 16)

            layer_weights(0, first=True)
            with sp.Fori(1, LAYERS) as l:
                layer_weights(l)

            def load(signal, dst, src):
                sp.dma_start(dst, src).then_inc(S[signal], 16)
            for k, n in enumerate(("q", "k")):
                load("l_weights", w_lraw[:, k, :], A[f"L0_attn_W_{n}"])
            load("l_weights", w_lraw[:, 2:6, :], A["L0_attn_W_v"].rearrange("(j p) n -> p j n", p=P))
            load("l_weights", w_loraw[:, :], A["L0_attn_W_out"])
            for k, n in enumerate(("q", "k", "v")):
                load("block_params", w_fqkv[:, k * D:(k + 1) * D], A[f"L0_ffn_W{n}"])
            load("block_params", w_fo[:, :], A["L0_ffn_Wo"])
            load("block_params", w_gate[:, :], A["L0_ffn_gate_W"])
            load("block_params", gb_r[:, :], A["L0_ffn_gate_b"].partition_broadcast(P))
            load("block_params", b2_e[:, :], A["L0_ffn_b2"])
            load("e_weights", w1_e[:, :, :], A["L0_ffn_W1"].rearrange("e p n -> p e n"))
            for e in range(E):
                load("e_weights", w2_e[:, e * EK:(e + 1) * EK, :], A["L0_ffn_W2"][e].rearrange("(j p) n -> p j n", p=P))

            with sp.Fori(0, BATCH) as b:
                sp.wait_ge(S["acc_done"], nth(b, E, 2 * E))
                sp.dma_start(out[b, 0:TOK, :].rearrange("(t p) c -> p t c", p=P), acc[:, 0:TT, :]).then_inc(S["stored"], 16)
                sp.dma_start(out[b, TOK:T, :], acc[0:TXT, TT, :]).then_inc(S["stored"], 16)
            sp.wait_ge(S["stored"], 32 * BATCH + 32)
        @block.gpsimd
        def _(pool):
            pool.memset(w_qk[:, :], 0.0)
            pool.memset(w_tv[:, :], 0.0)
            pool.memset(ident[:, :], 0.0)
            pool.memset(neghalf[:, :], -0.5)
            pool.memset(eps[:, :], 1e-5)
            pool.memset(tiny[:, :], 1e-12)
            pool.memset(hmask[:, :], 1.0)
            pool.memset(causal_t[:, :], 0.0)
            pool.memset(hblock[:, :], 1.0)
            pool.memset(ones[:, :], 1.0)
            pool.memset(causal01[:, :], 1.0)
            pool.memset(identb[:, :], 0.0)
            pool.memset(causalb[:, :], 0.0)
            pool.memset(sT[:, :], 0.0)
            pool.memset(yT[:, :], 0.0)
            pool.drain().then_inc(S["const_pool"], 1)
            pool.wait_ge(S["txt_ids"], 16)
            for b in range(BATCH):
                pool.indirect_dma_start(
                    out=tx[:, b, :], out_offset=None, in_=A["L0_txt_item_emb"],
                    in_offset=bass.IndirectOffsetOnAxis(ap=tok_idx[:, b:b + 1].bitcast(U32), axis=0),
                ).then_inc(S["txt_embed"], 16)
            pool.affine_select(out=ident[:, :], in_=ident[:, :], compare_op=ALU.not_equal, fill=1.0,
                               base=0, pattern=[[-1, P]], channel_multiplier=1)
            pool.affine_select(out=causal_t[:, :], in_=causal_t[:, :], compare_op=ALU.is_ge, fill=NEG,
                               base=0, pattern=[[-1, TXT]], channel_multiplier=1)
            pool.affine_select(out=identb[:, :], in_=identb[:, :], compare_op=ALU.not_equal, fill=1.0,
                               base=0, pattern=[[-1, P]], channel_multiplier=1)
            pool.affine_select(out=causalb[:, :], in_=causalb[:, :], compare_op=ALU.is_ge, fill=NEG,
                               base=0, pattern=[[-1, P]], channel_multiplier=1)
            pool.affine_select(out=causal01[:, :], in_=causal01[:, :], compare_op=ALU.is_ge, fill=0.0,
                               base=0, pattern=[[1, P]], channel_multiplier=-1)
            pool.affine_select(out=hblock[:, :], in_=hblock[:, :], compare_op=ALU.is_ge, fill=0.0,
                               base=0, pattern=[[-LD, LH], [0, LD]], channel_multiplier=1)
            pool.drain()
            pool.affine_select(out=hblock[:, :], in_=hblock[:, :], compare_op=ALU.is_gt, fill=0.0,
                               base=LD, pattern=[[LD, LH], [0, LD]], channel_multiplier=-1)
            pool.affine_select(out=hmask[:, :], in_=hmask[:, :], compare_op=ALU.is_ge, fill=0.0,
                               base=0, pattern=[[-HD, HEADS]], channel_multiplier=1)
            pool.drain()
            pool.affine_select(out=hmask[:, :], in_=hmask[:, :], compare_op=ALU.is_gt, fill=0.0,
                               base=HD, pattern=[[HD, HEADS]], channel_multiplier=-1)
            pool.drain().then_inc(S["const_pool"], 1)

            def rstd_txt(turn, k):
                pool.wait_ge(S["tx_stat"], nth(turn, 2, k))
                pool.tensor_tensor(tx_ve[:, :], tx_mv[:, :, 1], eps[0:TXT, 0:BATCH], ALU.add)
                pool.drain()
                pool.tensor_tensor(tx_rs[:, :], tx_ve[:, :], neghalf[0:TXT, 0:BATCH], ALU.pow).then_inc(S["tx_rstd"], 1)

            pool.wait_ge(S["setup_done"], 1)
            with pool.Fori(0, LAYERS) as l:
                rstd_txt(l, 1)
                add_bias(pool, bo_r, l)
                rstd_txt(l, 2)
                add_bias(pool, b2_r, l)
            rstd_txt(LAYERS, 1)

            with pool.Fori(0, BATCH) as b:
                pool.wait_ge(S["stat5"], nth(b, 1, 1))
                pool.tensor_tensor(va5[:, :], mv5[:, :, 1], eps[:, 0:TILES], ALU.add)
                pool.drain()
                pool.tensor_tensor(rs5[:, :], va5[:, :], neghalf[:, 0:TILES], ALU.pow).then_inc(S["rstd5"], 1)
                pool.wait_ge(S["la_q"], nth(b, 1, 1))
                for i in range(TILES):
                    if i >= 2:
                        pool.wait_ge(S["la_at"], nth(b, TILES, i - 1))
                    r = ROWS[i]
                    pool.tensor_tensor(lqbd[:, i % 2, :, 0:r], lq[:, i * P:i * P + r].unsqueeze(1).broadcast_to([P, LH, r]),
                                       hmask[:, :].unsqueeze(2).broadcast_to([P, LH, r]), ALU.mult).then_inc(S["la_qbd"], 1)
            with pool.Fori(0, BATCH) as b:
                pool.wait_ge(S["stat5"], nth(b, 1, BATCH + 1))
                pool.tensor_tensor(va5[:, :], mv5[:, :, 1], eps[:, 0:TILES], ALU.add)
                pool.drain()
                pool.tensor_tensor(rs5[:, :], va5[:, :], neghalf[:, 0:TILES], ALU.pow)
                pool.drain()
                pool.tensor_tensor(vb5[:, :], rs5[:, :], rs5[:, :], ALU.mult)
                pool.drain()
                pool.tensor_tensor(vb5[:, :], vb5[:, :], mv5[:, :, 1], ALU.mult)
                pool.drain()
                pool.tensor_tensor(vb5[:, :], vb5[:, :], eps[:, 0:TILES], ALU.add)
                pool.drain()
                pool.tensor_tensor(va5[:, :], vb5[:, :], neghalf[:, 0:TILES], ALU.pow)
                pool.drain()
                pool.tensor_tensor(rs5[:, :], rs5[:, :], va5[:, :], ALU.mult).then_inc(S["rstd5"], 1)
                pool.wait_ge(S["fa_ss"], nth(b, 1, 1))
                pool.tensor_tensor(ss[:, :, :], ss[:, :, :], tiny[:, :].rearrange("p (t h) -> p t h", t=TILES), ALU.add)
                pool.drain()
                pool.tensor_tensor(ssr[:, :, :], ss[:, :, :], neghalf[:, :].rearrange("p (t h) -> p t h", t=TILES), ALU.pow).then_inc(S["fa_rs"], 1)

        @block.tensor
        def _(pe):
            def transpose(dst, src, rows_in):
                return pe.transpose(dst, src, ident[0:rows_in, 0:rows_in])

            pe.wait_ge(S["const_pool"], 2)
            pe.wait_ge(S["params"], 16 * N_PARAMS)
            transpose(ps[:, 7, 0:NVEC], vrow[:, :], NVEC).then_inc(S["setup_psum"], 1)
            pe.wait_ge(S["qk_weights"], 16 * 12)

            BANK_S, BANK_T, BANK_O, BANK_P = 0, 2, 4, 6

            def tok_project(b):
                pe.wait_ge(S["x_loaded"], nth(b, 16, 16))
                pe.wait_ge(S["vb_ready"], nth(b, 1, 1))
                for t in range(TT):
                    mm = transpose(ps[:, 6, t * P:(t + 1) * P], x_in[:, t, :], P)
                mm.then_inc(S["proj_full"], 1)
                pe.wait_ge(S["xT_ready"], nth(b, 1, 1))
                pe.wait_ge(S["va_ready"], nth(b, 1, 1))
                for bank, w0 in ((7, 0), (6, P)):
                    pe.matmul(ps[:, bank, :], w_qk[:, w0:w0 + P], xT[:, :], start=True, stop=True).then_inc(S["proj_full"], 1)
                for bank, read, first in ((7, "q_ready", 0), (6, "k_ready", 2)):
                    pe.wait_ge(S[read], nth(b, 1, 1))
                    for t in range(2):
                        tile_ = first + t
                        mm = pe.matmul(ps[:, bank, t * 256:(t + 1) * 256], xT[:, tile_ * P:(tile_ + 1) * P],
                                       w_tv[:, :], start=True, stop=True)
                    mm.then_inc(S["proj_full"], 1)

            def tok_scores(b, n):
                i, a = divmod(n, 4)
                pe.wait_ge(S["prob_ready"], nth(b, UNITS, n + 1))
                pe.matmul(ps[:, BANK_S + n % 2, :], qT[32 * a:32 * a + DQ, i * P:(i + 1) * P],
                          kT[32 * a:32 * a + DQ, :], start=True, stop=True).then_inc(S["score_full"], 1)

            def tok_turn(b, n):
                pe.wait_ge(S["prob_ready"], nth(b, UNITS, n + 3))
                if n % 2 == 0:
                    pe.wait_ge(S["probT_act"], nth(b, UNITS // 2, n // 2 + 1))
                else:
                    pe.wait_ge(S["probT_dve"], nth(b, UNITS // 2, n // 2 + 1))
                for j in range(TT):
                    mm = transpose(ps[:, BANK_T + n % 2, j * P:(j + 1) * P], prob[:, n % 2, j * P:(j + 1) * P], P)
                mm.then_inc(S["probT_full"], 1)

            def tok_values(b, n):
                a = n % 4
                if n % 2 == 0:
                    pe.wait_ge(S["probT_act"], nth(b, UNITS // 2, n // 2 + 2))
                else:
                    pe.wait_ge(S["probT_dve"], nth(b, UNITS // 2, n // 2 + 2))
                pe.wait_ge(S["out_done"], nth(b, UNITS, n + 1))
                for j in range(TT):
                    mm = pe.matmul(ps[:, BANK_O + n % 2, 0:CH], probT[:, n % 2, j * P:(j + 1) * P],
                                   v_tok[:, j, a * CH:(a + 1) * CH], start=(j == 0), stop=(j == TT - 1))
                mm.then_inc(S["out_full"], 1)

            with pe.Fori(0, BATCH) as b:
                tok_project(b)
                for n in range(UNITS + 2):
                    if n < UNITS:
                        tok_scores(b, n)
                    if 1 <= n <= UNITS:
                        tok_turn(b, n - 1)
                    if n == 2:
                        pe.wait_ge(S["va_ready"], nth(b, 1, 2))
                        pe.wait_ge(S["vb_ready"], nth(b, 1, 2))
                    if n >= 2:
                        tok_values(b, n - 2)

            pe.wait_ge(S["seq_tok"], BATCH)

            def turn_norm(l, k):
                pe.wait_ge(S["tx_norm"], nth(l, 2, k))
                for b in range(BATCH):
                    mm = transpose(ps[:, 0, b * TXT:(b + 1) * TXT], tx_n[:, b, :], TXT)
                mm.then_inc(S["tx_normT"], 1)
                pe.wait_ge(S["tx_hT"], nth(l, 2, k))

            def txt_layer(l):
                turn_norm(l, 1)
                pe.wait_ge(S["wk_loaded"], nth(l, 16, 16))
                pe.matmul(ps[:, 2, 0:SEQ4], w_k[:, :], hT[:, :], start=True, stop=True).then_inc(S["tx_k"], 1)
                pe.wait_ge(S["wq_loaded"], nth(l, 16, 16))
                pe.matmul(ps[:, 1, 0:SEQ4], w_q[:, :], hT[:, :], start=True, stop=True).then_inc(S["tx_q"], 1)
                pe.wait_ge(S["wv_loaded"], nth(l, 16, 16))
                for b in range(BATCH):
                    mm = pe.matmul(ps[0:TXT, 3, b * D:(b + 1) * D], hT[:, b * TXT:(b + 1) * TXT], w_v[:, :], start=True, stop=True)
                mm.then_inc(S["tx_v"], 1)
                pe.wait_ge(S["tx_qs"], nth(l, 1, 1))
                HALF = HEADS * TXT // 2

                def scores(b):
                    pe.wait_ge(S["tx_kbd"], nth(l, BATCH, b + 1))
                    pe.wait_ge(S["tx_masked"], nth(l, BATCH, b + 1))
                    for g in range(2):
                        mm = pe.matmul(ps[0:TXT, 4 + g, 0:HALF], tqT[:, b * TXT:(b + 1) * TXT],
                                       kbd[:, b, g * HALF:(g + 1) * HALF], start=True, stop=True)
                    mm.then_inc(S["tx_score"], 1)

                def turn_probs(b):
                    pe.wait_ge(S["tx_exp"], nth(l, BATCH, b + 1))
                    pe.wait_ge(S["tx_pT"], nth(l, BATCH, b + 1))
                    for h in range(HEADS):
                        g, k = divmod(h, HEADS // 2)
                        mm = transpose(ps[0:TXT, 6 + g, k * TXT:(k + 1) * TXT], ts[:, b, h * TXT:(h + 1) * TXT], TXT)
                    mm.then_inc(S["tx_pt"], 1)

                def values(b):
                    pe.wait_ge(S["tx_pT"], nth(l, BATCH, b + 2))
                    pe.wait_ge(S["tx_ctx"], nth(l, BATCH, b + 1))
                    if b == 0:
                        pe.wait_ge(S["tx_vs"], nth(l, 1, 1))
                    for h in range(HEADS):
                        mm = pe.matmul(ps[0:TXT, 2 + b % 2, h * (HD + 1):(h + 1) * (HD + 1)],
                                       tpT[:, b, h * TXT:(h + 1) * TXT], tv[:, b, h, :], start=True, stop=True)
                    mm.then_inc(S["tx_pv"], 1)

                for n in range(BATCH + 2):
                    if n < BATCH:
                        scores(n)
                    if 1 <= n <= BATCH:
                        turn_probs(n - 1)
                    if n >= 2:
                        values(n - 2)
                pe.wait_ge(S["tx_ctx"], nth(l, BATCH, BATCH + 2))
                for b in range(BATCH):
                    mm = transpose(ps[:, 0, b * TXT:(b + 1) * TXT], tctx[:, b, :], TXT)
                mm.then_inc(S["tx_ct"], 1)
                pe.wait_ge(S["tx_cT"], nth(l, 1, 1))
                pe.wait_ge(S["wo_loaded"], nth(l, 16, 16))
                for b in range(BATCH):
                    mm = pe.matmul(ps[0:TXT, 1, b * D:(b + 1) * D], cT[:, b * TXT:(b + 1) * TXT], w_o[:, :], start=True, stop=True)
                mm.then_inc(S["tx_o"], 1)
                turn_norm(l, 2)
                pe.wait_ge(S["w1_loaded"], nth(l, 16, 16))
                for j in range(KT):
                    pe.matmul(ps[:, 4 + j, 0:SEQ4], w_1[:, j * P:(j + 1) * P], hT[:, :], start=True, stop=True).then_inc(S["tx_f1"], 1)
                pe.wait_ge(S["tx_g"], nth(l, KT, KT))
                pe.wait_ge(S["w2_loaded"], nth(l, 16, 16))
                for b in range(BATCH):
                    for j in range(KT):
                        mm = pe.matmul(ps[0:TXT, 1, b * D:(b + 1) * D], gact[:, j, b * TXT:(b + 1) * TXT],
                                       w_2[:, j, :], start=(j == 0), stop=(j == KT - 1))
                mm.then_inc(S["tx_f2"], 1)

            with pe.Fori(0, LAYERS) as l:
                txt_layer(l)

            pe.wait_ge(S["seq_txt"], 1)
            pe.wait_ge(S["l_weights"], 16 * 4)
            for k in range(6):
                mm = transpose(ps[:, k // 4, k % 4 * P:(k % 4 + 1) * P], w_lraw[:, k, :], P)
            for k in range(4):
                mm = transpose(ps[:, 2, k * P:(k + 1) * P], w_loraw[:, k * P:(k + 1) * P], P)
            mm.then_inc(S["l_wT"], 1)
            pe.wait_ge(S["l_wT_done"], 1)

            def wide(bank, lhsT, rhs, width=T):
                pe.matmul(banks(bank, 512), lhsT, rhs[:, 0:512], start=True, stop=True)
                return pe.matmul(ps[:, bank + 1, 0:width - 512], lhsT, rhs[:, 512:width], start=True, stop=True)

            def turn_tiles(n):
                pe.wait_ge(S["norm5"], n)
                for i in range(TILES):
                    r = ROWS[i]
                    mm = transpose(psf[:, i * P:i * P + r], xn[0:r, i, :], r)
                mm.then_inc(S["normT5"], 1)
                pe.wait_ge(S["hT5"], n)

            def linear(b):
                pe.wait_ge(S["seq_lin"], nth(b, 1, 1))
                turn_tiles(nth(b, 1, 1))
                wide(4, w_lT[:, P:2 * P], sT).then_inc(S["la_qk"], 1)
                wide(2, w_lT[:, 0:P], sT).then_inc(S["la_qk"], 1)
                for i in range(TILES):
                    if i >= 2:
                        pe.wait_ge(S["la_vdone"], nth(b, TILES, i - 1))
                    pe.matmul(ps[:, 6 + i % 2, :], sT[:, i * P:(i + 1) * P], w_lT[:, 2 * P:6 * P], start=True, stop=True).then_inc(S["la_vfull"], 1)
                pe.wait_ge(S["la_feat"], nth(b, 2, 1))
                for i in range(TT):
                    mm = transpose(ps[:, 0, i * P:(i + 1) * P], lk[:, i * P:(i + 1) * P], P)
                mm.then_inc(S["la_ktps"], 1)
                pe.wait_ge(S["la_qz"], nth(b, 1, 1))
                wide(2, hblock[:, :], lz).then_inc(S["la_den"], 1)
                pe.wait_ge(S["la_q"], nth(b, 1, 1))
                pe.wait_ge(S["la_vdone"], nth(b, TILES, TILES))

                def scores(i):
                    r = ROWS[i]
                    pe.wait_ge(S["la_qbd"], nth(b, TILES, i + 1))
                    if i >= 2:
                        pe.wait_ge(S["la_masked"], nth(b, TILES, i - 1))
                    for g in range(2):
                        mm = pe.matmul(ps[0:r, 2 + 2 * (i % 2) + g, 0:4 * r], lk[:, i * P:i * P + r],
                                       lqbd[:, i % 2, 4 * g:4 * g + 4, 0:r], start=True, stop=True)
                    mm.then_inc(S["la_at"], 1)

                def state(i):
                    if i >= 1:
                        pe.wait_ge(S["la_sbd"], nth(b, TT, i))
                    pe.matmul(ps[:, 1, :], lktok[:, i, :], lv[:, i, :], start=(i == 0), stop=(i == TT - 1),
                              skip_group_check=True).then_inc(S["la_state"], 1)

                def outputs(i):
                    r = ROWS[i]
                    pe.wait_ge(S["la_masked"], nth(b, TILES, i + 1))
                    if i >= 1:
                        pe.wait_ge(S["la_sbd"], nth(b, TT, i))
                    if i >= 2:
                        pe.wait_ge(S["la_lo"], nth(b, TILES, i - 1))
                    bank = 6 + i % 2
                    for g in range(4):
                        if i >= 1:
                            pe.matmul(ps[:, bank, g * r:(g + 1) * r], lsbd[:, g * P:(g + 1) * P], lq[:, i * P:i * P + r],
                                      start=True, stop=False, skip_group_check=True)
                        for h in (2 * g, 2 * g + 1):
                            p0 = LV * (h % 2)
                            mm = pe.matmul(ps[p0:p0 + LV, bank, g * r:(g + 1) * r], lv[0:r, i, h * LV:(h + 1) * LV],
                                           la[0:r, i % 2, h, 0:r], start=(i == 0), stop=True, skip_group_check=True)
                    mm.then_inc(S["la_ot"], 1)

                def project(i):
                    r = ROWS[i]
                    pe.wait_ge(S["la_lo"], nth(b, TILES, i + 1))
                    if i >= 1:
                        pe.wait_ge(S["seq_tile"], nth(b, TILES, i))
                    for g in range(4):
                        mm = pe.matmul(ps[0:r, 0, i % 4 * P:(i % 4 + 1) * P], lo[:, i % 2, g, 0:r], w_loT[:, g, :],
                                       start=(g == 0), stop=(g == 3))
                    mm.then_inc(S["la_y"], 1)

                pe.wait_ge(S["la_ktok"], nth(b, 1, 1))
                scores(0)
                for i in range(TILES):
                    if i < TT:
                        scores(i + 1)
                    if i >= 1:
                        project(i - 1)
                    outputs(i)
                    if i < TT:
                        state(i)
                project(TT)

            with pe.Fori(0, BATCH) as b:
                linear(b)

            pe.wait_ge(S["seq_lin"], BATCH + 1)
            pe.wait_ge(S["block_params"], 16 * 7)
            pe.wait_ge(S["e_weights"], 16 * (1 + E))

            def attention(b):
                pe.wait_ge(S["acc_done"], nth(b, E, E))
                turn_tiles(nth(b, 1, BATCH + 1))
                for i in range(TILES):
                    mm = pe.matmul(ps[:, 2 + i, 0:3 * D], sT[:, i * P:(i + 1) * P], w_fqkv[:, :], start=True, stop=True)
                    mm.then_inc(S["fa_qkv"], 1)
                pe.wait_ge(S["fa_norm"], nth(b, 1, 1))
                for part in range(2):
                    for i in range(TILES):
                        r = ROWS[i]
                        mm = transpose(psf[:, part * 1024 + i * P:part * 1024 + i * P + r], qkv[0:r, i, part * D:(part + 1) * D], r)
                    mm.then_inc(S["fa_T"], 1)
                pe.wait_ge(S["fa_qT"], nth(b, 1, 1))
                pe.wait_ge(S["fa_kT"], nth(b, 1, 1))

                units = [(i, h) for i in range(TILES) for h in range(FH)]
                U = len(units)

                def scores(n):
                    i, h = units[n]
                    r, width = ROWS[i], min((i + 1) * P, T)
                    bank = 4 + 2 * (n % 2)
                    if n >= 2:
                        pe.wait_ge(S["fa_exp"], nth(b, U, n - 1))
                    lhsT = fq[h * FD:(h + 1) * FD, i * P:i * P + r]
                    for c, w in ((0, min(width, 512)), (512, width - 512)):
                        if w > 0:
                            pe.matmul(ps[0:r, bank + c // 512, 0:w], lhsT, fk[h * FD:(h + 1) * FD, c:c + w],
                                      start=True, stop=False, skip_group_check=True)
                    mm = pe.matmul(psf[0:r, bank * 512 + i * P:bank * 512 + i * P + r], identb[0:r, 0:r], causalb[0:r, 0:r],
                                   start=False, stop=True, skip_group_check=True)
                    mm.then_inc(S["fa_s"], 1)

                def turn(n):
                    i, h = units[n]
                    r = ROWS[i]
                    pe.wait_ge(S["fa_pn"], nth(b, U, n + 1))
                    wait_pT(n - 2)
                    for j in range(i + 1):
                        c = ROWS[j]
                        mm = transpose(ps[0:c, n % 2, j * r:(j + 1) * r], fpn[0:r, n % 2, j * P:j * P + c], r)
                    mm.then_inc(S["fa_pt"], 1)

                def wait_pT(n):
                    if n >= 0:
                        if n % 2 == 0:
                            pe.wait_ge(S["fa_pT_act"], nth(b, U // 2, n // 2 + 1))
                        else:
                            pe.wait_ge(S["fa_pT_dve"], nth(b, U // 2, n // 2 + 1))

                def values(n):
                    i, h = units[n]
                    r = ROWS[i]
                    wait_pT(n)
                    for j in range(i + 1):
                        c = ROWS[j]
                        mm = pe.matmul(psf[h * FD:(h + 1) * FD, 1024 + i * P:1024 + i * P + r],
                                       qkv[0:c, j, 2 * D + h * FD:2 * D + (h + 1) * FD], fpT[0:c, n % 2, j * r:(j + 1) * r],
                                       start=(j == 0), stop=(j == i))
                    mm.then_inc(S["fa_o"], 1)

                for n in range(U + 3):
                    if n < U:
                        scores(n)
                    if 2 <= n <= U + 1:
                        turn(n - 2)
                    if n >= 3:
                        values(n - 3)
                pe.wait_ge(S["fa_oT"], nth(b, 1, 1))
                wide(0, w_fo[:, :], foT).then_inc(S["y_ps"], 1)
                pe.wait_ge(S["y_done"], nth(b, 1, 1))
                for i in range(TILES):
                    mm = pe.matmul(ps[:, 4, i * E:(i + 1) * E], yT[:, i * P:(i + 1) * P], w_gate[:, :], start=True, stop=True)
                mm.then_inc(S["g_ps"], 1)

            def experts(b):
                def up(e):
                    for f in range(EK):
                        n = e * EK + f
                        if n >= 2:
                            pe.wait_ge(S["up_done"], nth(b, E * EK, n - 1))
                        bank = 2 * (n % 2)
                        wide(bank, w1_e[:, e, f * P:(f + 1) * P], yT).then_inc(S["up"], 1)

                def down(e):
                    pe.wait_ge(S["up_done"], nth(b, E * EK, (e + 1) * EK))
                    if e >= 2:
                        pe.wait_ge(S["acc_done"], nth(b, E, E + e - 1))
                    for i in range(TILES):
                        r = ROWS[i]
                        c0 = (4 + 2 * (e % 2)) * 512 + i * P
                        for f in range(EK):
                            mm = pe.matmul(psf[0:r, c0:c0 + P], hid[:, e % 2, f, i * P:i * P + r], w2_e[:, e * EK + f, :],
                                           start=(f == 0), stop=(f == EK - 1))
                    mm.then_inc(S["down"], 1)

                up(0)
                pe.wait_ge(S["g_done"], nth(b, 1, 1))
                for i in range(TILES):
                    r = ROWS[i]
                    mm = transpose(psf[0:E, 5 * 512 + i * P:5 * 512 + i * P + r], gate[0:r, i, :], r)
                mm.then_inc(S["g_tps"], 1)
                pe.wait_ge(S["g_T"], nth(b, 1, 1))
                for i in range(TILES):
                    r = ROWS[i]
                    mm = pe.matmul(psf[0:r, 6 * 512 + i * P:6 * 512 + (i + 1) * P], gateT[:, i * P:i * P + r], b2_e[:, :], start=True, stop=True)
                mm.then_inc(S["b2_ps"], 1)
                for e in range(E):
                    if e + 1 < E:
                        up(e + 1)
                    if e == 0:
                        pe.wait_ge(S["acc_init"], nth(b, 1, 1))
                    down(e)

            with pe.Fori(0, BATCH) as b:
                attention(b)
                experts(b)

        @block.vector
        def _(dve):
            dve.sem_inc(S["vb_ready"], 1)
            dve.sem_inc(S["out_done"], 2)
            dve.sem_inc(S["probT_dve"], 1)
            dve.sem_inc(S["tx_masked"], 1)
            dve.sem_inc(S["tx_ctx"], 2)
            dve.sem_inc(S["seq_lin"], 1)
            dve.sem_inc(S["acc_done"], E)
            dve.sem_inc(S["stored"], 32)
            dve.memset(tv[:, :, :, HD:HD + 1], 1.0)
            dve.memset(seq[:, :, :], 0.0)
            dve.wait_ge(S["setup_psum"], 1)
            dve.tensor_copy(vcol[:, :], ps[:, 7, 0:NVEC])
            dve.tensor_scalar(tmask[:, :, :], padrow[:, :, :], 0.0, NEG, ALU.is_equal, ALU.mult)
            dve.drain()
            dve.tensor_tensor(tmask[:, :, :], tmask[:, :, :], causal_t[:, :].unsqueeze(1).broadcast_to([TXT, BATCH, TXT]), ALU.add)
            dve.tensor_scalar(bq4[:, :], vcol[:, VEC["bq"]:VEC["bq"] + LAYERS], HD ** -0.5, None, ALU.mult)
            dve.scalar_tensor_tensor(qkg[:, :], vcol[:, VEC["qn"]:VEC["qn"] + 1], FD ** 0.5,
                                     vcol[:, VEC["kn"]:VEC["kn"] + 1], ALU.mult, ALU.mult)
            dve.wait_ge(S["txt_embed"], 16 * BATCH)
            dve.tensor_tensor(tx[:, :, :], tx[:, :, :], pos[:, :].unsqueeze(1).broadcast_to([TXT, BATCH, D]), ALU.add)
            dve.drain().then_inc(S["setup_done"], 1)

            def tok_prologue(b):
                dve.wait_ge(S["proj_full"], nth(b, 5, 1))
                dve.tensor_copy(xT[:, :], ps[:, 6, :]).then_inc(S["xT_ready"], 1)
                dve.wait_ge(S["proj_full"], nth(b, 5, 3))
                dve.tensor_copy(kT[:, :], ps[:, 6, :]).then_inc(S["k_ready"], 1)
                dve.wait_ge(S["proj_full"], nth(b, 5, 5))
                dve.tensor_copy(v_tok[:, 2:4, :], ps[:, 6, :]).then_inc(S["vb_ready"], 1)

            def tok_max(b, n):
                dve.wait_ge(S["score_full"], nth(b, UNITS, n + 1))
                dve.tensor_reduce(nmax[:, n:n + 1], ps[:, n % 2, :], AX.X, ALU.max, negate=True).then_inc(S["max_ready"], 1)

            def tok_probT(b, n):
                dve.wait_ge(S["probT_full"], nth(b, UNITS, n + 1))
                dve.tensor_copy(probT[:, n % 2, :], ps[:, 2 + n % 2, :]).then_inc(S["probT_dve"], 1)

            def tok_rsum(b, n):
                dve.wait_ge(S["prob_ready"], nth(b, UNITS, n + 3))
                dve.reciprocal(rsum[:, n:n + 1], psum_e[:, n:n + 1])

            def tok_out(b, n):
                i, a = divmod(n, 4)
                s = a // 2
                dve.wait_ge(S["out_full"], nth(b, UNITS, n + 1))
                o = ps[:, 4 + n % 2, 0:CH]
                if a % 2 == 0:
                    dve.tensor_scalar(intra[:, s, :], o, rsum[:, n:n + 1], mix[:, s:s + 1], ALU.mult, ALU.mult).then_inc(S["out_done"], 1)
                else:
                    dst = seq[:, bass.ds(b * TILES + i, 1), s * CH:(s + 1) * CH]
                    dve.scalar_tensor_tensor(dst, o.unsqueeze(1), rsum[:, n:n + 1], intra[:, s, :].unsqueeze(1), ALU.mult, ALU.add).then_inc(S["out_done"], 1)

            dve.wait_ge(S["params"], 16 * N_PARAMS)
            with dve.Fori(0, BATCH) as b:
                tok_prologue(b)
                for n in range(UNITS + 2):
                    if n < UNITS:
                        tok_max(b, n)
                    dve.drain()
                    if 1 <= n <= UNITS:
                        tok_rsum(b, n - 1)
                        if (n - 1) % 2 == 1:
                            tok_probT(b, n - 1)
                    if n >= 2:
                        tok_out(b, n - 2)
                dve.drain().then_inc(S["seq_tok"], 1)

            def norm_stats(l, k):
                for b in range(BATCH):
                    dve.bn_stats(tx_st[:, b, :], tx[:, b, :])
                dve.drain()
                for b in range(BATCH):
                    mm = dve.bn_aggr(tx_mv[:, b, :], tx_st[:, b, :])
                mm.then_inc(S["tx_stat"], 1)

            def normalise(l, k, done=True):
                dve.wait_ge(S["tx_rstd"], nth(l, 2, k))
                for b in range(BATCH):
                    mm = dve.tensor_scalar(tx_n[:, b, :], tx[:, b, :], tx_mv[:, b, 0:1], tx_rs[:, b:b + 1], ALU.subtract, ALU.mult)
                if done:
                    mm.then_inc(S["tx_norm"], 1)

            def scale_turned(l, k, g, c):
                dve.wait_ge(S["tx_normT"], nth(l, 2, k))
                dve.tensor_scalar(hT[:, :], ps[:, 0, 0:SEQ4], vcol[:, bass.ds(VEC[g] + l, 1)], vcol[:, bass.ds(VEC[c] + l, 1)],
                                  ALU.mult, ALU.add).then_inc(S["tx_hT"], 1)

            def txt_layer(l):
                norm_stats(l, 1)
                normalise(l, 1)
                scale_turned(l, 1, "g1", "c1")
                dve.wait_ge(S["tx_k"], nth(l, 1, 1))
                for b in range(BATCH):
                    dve.scalar_tensor_tensor(
                        kbd[:, b, :].rearrange("p (h t) -> p h t", h=HEADS),
                        ps[:, 2, b * TXT:(b + 1) * TXT].unsqueeze(1).broadcast_to([P, HEADS, TXT]),
                        vcol[:, bass.ds(VEC["bk"] + l, 1)],
                        hmask[:, :].unsqueeze(2).broadcast_to([P, HEADS, TXT]), ALU.add, ALU.mult).then_inc(S["tx_kbd"], 1)
                dve.wait_ge(S["tx_v"], nth(l, 1, 1))
                for b in range(BATCH):
                    mm = dve.tensor_tensor(tv[:, b, :, 0:HD], ps[0:TXT, 3, b * D:(b + 1) * D].rearrange("p (h d) -> p h d", h=HEADS),
                                           bv_r[:, bass.ds(l, 1), :].rearrange("p a (h d) -> p (a h) d", h=HEADS), ALU.add)
                mm.then_inc(S["tx_vs"], 1)

                def mask(b):
                    dve.wait_ge(S["tx_score"], nth(l, BATCH, b + 1))
                    dve.tensor_tensor(ts[:, b, :].rearrange("p (g h t) -> p g h t", g=2, h=HEADS // 2),
                                      ps[0:TXT, 4:6, 0:HEADS // 2 * TXT].rearrange("p g (h t) -> p g h t", t=TXT),
                                      tmask[:, b, :].unsqueeze(1).unsqueeze(1).broadcast_to([TXT, 2, HEADS // 2, TXT]),
                                      ALU.add).then_inc(S["tx_masked"], 1)

                def shift(b):
                    s3 = ts[:, b, :].rearrange("p (h t) -> p h t", h=HEADS)
                    dve.drain()
                    dve.tensor_reduce(tnm[:, b, :], s3, AX.X, ALU.max, negate=True)
                    dve.drain()
                    dve.tensor_tensor(s3, s3, tnm[:, b, :].unsqueeze(2).broadcast_to([TXT, HEADS, TXT]), ALU.add).then_inc(S["tx_shift"], 1)

                def context(b):
                    dve.wait_ge(S["tx_pv"], nth(l, BATCH, b + 1))
                    o = ps[0:TXT, 2 + b % 2, 0:HEADS * (HD + 1)].rearrange("p (h d) -> p h d", h=HEADS)
                    dve.reciprocal(trs[:, b, :], o[:, :, HD])
                    dve.drain()
                    dve.tensor_tensor(tctx[:, b, :].rearrange("p (h d) -> p h d", h=HEADS), o[:, :, 0:HD],
                                      trs[:, b, :].unsqueeze(2).broadcast_to([TXT, HEADS, HD]), ALU.mult).then_inc(S["tx_ctx"], 1)

                mask(0)
                for b in range(BATCH):
                    shift(b)
                    if b + 1 < BATCH:
                        mask(b + 1)
                    if b >= 2:
                        context(b - 2)
                context(BATCH - 2)
                context(BATCH - 1)

                def residual(bank_full, k, turn_value):
                    dve.wait_ge(S[bank_full], turn_value)
                    dve.wait_ge(S["tx_resid"], nth(l, 2, k))
                    dve.tensor_tensor(tx[:, :, :], ps[0:TXT, 1, :].rearrange("p (b d) -> p b d", b=BATCH), tx_res[:, :, :], ALU.add).then_inc(S["tx_x"], 1)
                    dve.drain()

                residual("tx_o", 1, nth(l, 1, 1))
                norm_stats(l, 2)
                normalise(l, 2)
                scale_turned(l, 2, "g2", "c2")
                residual("tx_f2", 2, nth(l, 1, 1))

            with dve.Fori(0, LAYERS) as l:
                txt_layer(l)
            norm_stats(LAYERS, 1)
            normalise(LAYERS, 1, done=False)
            dve.drain()
            dve.tensor_tensor(tx_n[:, :, :], tx_n[:, :, :], lnf_g[:, :].unsqueeze(1).broadcast_to([TXT, BATCH, D]), ALU.mult)
            dve.drain()
            dve.tensor_tensor(seq[0:TXT, TT::TILES, :], tx_n[:, :, :], lnf_b[:, :].unsqueeze(1).broadcast_to([TXT, BATCH, D]), ALU.add).then_inc(S["seq_txt"], 1)

            dve.drain()
            dve.wait_ge(S["l_wT"], 1)
            dve.tensor_copy(w_lT[:, :], banks(0, 6 * P))
            dve.tensor_copy(w_loT[:, :, :], ps[:, 2, :].rearrange("p (g n) -> p g n", g=4)).then_inc(S["l_wT_done"], 1)

            def norm5(b, n, g=None, c=None):
                src = [seq[:, bass.ds(b * TILES + i, 1), :].rearrange("p a d -> p (a d)") for i in range(TILES)]
                for i in range(TILES):
                    dve.bn_stats(st5[:, i, :], src[i])
                dve.drain()
                for i in range(TILES):
                    op = dve.bn_aggr(mv5[:, i, :], st5[:, i, :])
                op.then_inc(S["stat5"], 1)
                dve.wait_ge(S["rstd5"], n)
                for i in range(TILES):
                    op = dve.tensor_scalar(xn[:, i, :], src[i], mv5[:, i, 0:1], rs5[:, i:i + 1], ALU.subtract, ALU.mult)
                op.then_inc(S["norm5"], 1)
                dve.wait_ge(S["normT5"], n)
                if g is None:
                    dve.tensor_copy(sT[:, 0:T], banks(0, T)).then_inc(S["hT5"], 1)
                else:
                    dve.tensor_scalar(sT[:, 0:T], banks(0, T), g, c, ALU.mult, ALU.add).then_inc(S["hT5"], 1)

            def linear(b):
                norm5(b, nth(b, 1, 1))
                for k, (bank, part) in enumerate(((4, lt1), (2, lt2))):
                    dve.wait_ge(S["la_qk"], nth(b, 2, k + 1))
                    dve.tensor_scalar(part[:, :], banks(bank, T), 0.0, None, ALU.min).then_inc(S["la_min"], 1)
                for k, (bank, part, feat) in enumerate(((4, lt1, lk), (2, lt2, lq))):
                    dve.wait_ge(S["la_exp"], nth(b, 2, k + 1))
                    dve.scalar_tensor_tensor(feat[:, :], banks(bank, T), 0.0, part[:, :], ALU.max, ALU.add).then_inc(S["la_feat"], 1)
                dve.drain()
                dve.tensor_tensor_scan(lz[:, :], ones[:, :], lk[:, :], 0.0, ALU.mult, ALU.add)
                dve.drain()
                dve.tensor_tensor(lz[:, :], lz[:, :], lq[:, :], ALU.mult).then_inc(S["la_qz"], 1)
                dve.wait_ge(S["la_den"], nth(b, 1, 1))
                dve.tensor_scalar(lt1[:, :], banks(2, T), 1e-6, None, ALU.max)
                dve.drain()
                dve.reciprocal(lt2[:, :], lt1[:, :])
                dve.drain()
                dve.tensor_tensor(lq[:, :], lq[:, :], lt2[:, :], ALU.mult).then_inc(S["la_q"], 1)

                def mask(i):
                    r = ROWS[i]
                    dve.wait_ge(S["la_at"], nth(b, TILES, i + 1))
                    if i >= 2:
                        dve.wait_ge(S["la_ot"], nth(b, TILES, i - 1))
                    bank = 2 + 2 * (i % 2)
                    dve.tensor_tensor(la[0:r, i % 2, :, 0:r].rearrange("p (g h) t -> p g h t", g=2),
                                      ps[0:r, bank:bank + 2, 0:4 * r].rearrange("p g (h t) -> p g h t", h=4),
                                      causal01[0:r, 0:r].unsqueeze(1).unsqueeze(1).broadcast_to([r, 2, 4, r]),
                                      ALU.mult).then_inc(S["la_masked"], 1)

                def keep_state(i):
                    dve.wait_ge(S["la_state"], nth(b, TT, i + 1))
                    if i >= 1:
                        dve.wait_ge(S["la_ot"], nth(b, TILES, i + 1))
                    dve.tensor_tensor(lsbd[:, :].rearrange("p (h v) -> p h v", h=LH), ps[:, 1, :].rearrange("p (h v) -> p h v", h=LH),
                                      hmask[:, :].unsqueeze(2).broadcast_to([P, LH, LV]), ALU.mult).then_inc(S["la_sbd"], 1)

                def residual(i):
                    r = ROWS[i]
                    dve.wait_ge(S["la_y"], nth(b, TILES, i + 1))
                    at_ = seq[0:r, bass.ds(b * TILES + i, 1), :]
                    dve.tensor_tensor(at_, ps[0:r, 0, i % 4 * P:(i % 4 + 1) * P].unsqueeze(1), at_, ALU.add).then_inc(S["seq_tile"], 1)

                mask(0)
                for i in range(TILES):
                    if i < TT:
                        mask(i + 1)
                        keep_state(i)
                    if i >= 1:
                        residual(i - 1)
                residual(TT)
                dve.drain().then_inc(S["seq_lin"], 1)

            with dve.Fori(0, BATCH) as b:
                linear(b)

            dve.wait_ge(S["block_params"], 16 * 7)

            def attention(b):
                norm5(b, nth(b, 1, BATCH + 1), vcol[:, VEC["fg"]:VEC["fg"] + 1], vcol[:, VEC["fc"]:VEC["fc"] + 1])
                dve.wait_ge(S["fa_qkv_sb"], nth(b, TILES, TILES))
                dve.tensor_tensor(sq[:, :, :], qkv[:, :, 0:2 * D], qkv[:, :, 0:2 * D], ALU.mult)
                dve.drain()
                dve.tensor_reduce(ss[:, :, :], sq[:, :, :].rearrange("p t (h d) -> p t h d", d=FD), AX.X, ALU.add).then_inc(S["fa_ss"], 1)
                dve.wait_ge(S["fa_rs"], nth(b, 1, 1))
                qk4 = qkv[:, :, 0:2 * D].rearrange("p t (h d) -> p t h d", d=FD)
                dve.tensor_tensor(qk4, qk4, ssr[:, :, :].unsqueeze(3).broadcast_to([P, TILES, 2 * FH, FD]), ALU.mult).then_inc(S["fa_norm"], 1)
                dve.wait_ge(S["fa_T"], nth(b, 2, 1))
                dve.tensor_scalar(fq[:, :], banks(0, T), qkg[:, 0:1], None, ALU.mult).then_inc(S["fa_qT"], 1)

                units = [(i, h) for i in range(TILES) for h in range(FH)]
                U = len(units)

                def rowmax(n):
                    i, h = units[n]
                    r, width = ROWS[i], min((i + 1) * P, T)
                    dve.wait_ge(S["fa_s"], nth(b, U, n + 1))
                    dve.tensor_reduce(fnm[0:r, n:n + 1], banks(4 + 2 * (n % 2), width, r), AX.X, ALU.max, negate=True).then_inc(S["fa_max"], 1)

                def scale(n):
                    i, h = units[n]
                    r, width = ROWS[i], min((i + 1) * P, T)
                    dve.wait_ge(S["fa_exp"], nth(b, U, n + 1))
                    dve.reciprocal(frs[0:r, n:n + 1], fsum[0:r, n:n + 1])
                    dve.drain()
                    if n >= 2:
                        dve.wait_ge(S["fa_pt"], nth(b, U, n - 1))
                    dve.tensor_scalar(fpn[0:r, n % 2, 0:width], fp[0:r, n % 2, 0:width], frs[0:r, n:n + 1], None, ALU.mult).then_inc(S["fa_pn"], 1)

                def copy_pT(n):
                    i, h = units[n]
                    r = ROWS[i]
                    dve.wait_ge(S["fa_pt"], nth(b, U, n + 1))
                    if n >= 2:
                        dve.wait_ge(S["fa_o"], nth(b, U, n - 1))
                    if i < TT:
                        dve.tensor_copy(fpT[:, n % 2, 0:(i + 1) * r], ps[:, n % 2, 0:(i + 1) * r]).then_inc(S["fa_pT_dve"], 1)
                    else:
                        dve.tensor_copy(fpT[:, n % 2, 0:TT * r], ps[:, n % 2, 0:TT * r])
                        dve.tensor_copy(fpT[0:r, n % 2, TT * r:(TT + 1) * r], ps[0:r, n % 2, TT * r:(TT + 1) * r]).then_inc(S["fa_pT_dve"], 1)

                for n in range(U + 3):
                    if n < U:
                        rowmax(n)
                    if 1 <= n <= U:
                        scale(n - 1)
                    if 2 <= n <= U + 1 and (n - 2) % 2 == 1:
                        copy_pT(n - 2)
                dve.wait_ge(S["fa_o"], nth(b, U, U))
                dve.tensor_copy(foT[:, :], banks(2, T)).then_inc(S["fa_oT"], 1)
                dve.wait_ge(S["g_ps"], nth(b, 1, 1))
                dve.tensor_tensor(lg[:, :, :], ps[:, 4, 0:TILES * E].rearrange("p (t e) -> p t e", t=TILES),
                                  gb_r[:, :].unsqueeze(1).broadcast_to([P, TILES, E]), ALU.add)
                dve.drain()
                dve.tensor_reduce(lgm[:, :], lg[:, :, :], AX.X, ALU.max, negate=True)
                dve.drain()
                dve.tensor_tensor(lg[:, :, :], lg[:, :, :], lgm[:, :].unsqueeze(2).broadcast_to([P, TILES, E]), ALU.add).then_inc(S["g_shift"], 1)
                dve.wait_ge(S["g_exp"], nth(b, 1, 1))
                dve.tensor_reduce(lgm[:, :], lg[:, :, :], AX.X, ALU.add)
                dve.drain()
                dve.reciprocal(lgm[:, :], lgm[:, :])
                dve.drain()
                dve.tensor_tensor(gate[:, :, :], lg[:, :, :], lgm[:, :].unsqueeze(2).broadcast_to([P, TILES, E]), ALU.mult).then_inc(S["g_done"], 1)
                dve.wait_ge(S["g_tps"], nth(b, 1, 1))
                dve.tensor_copy(gateT[:, :], banks(5, T, E)).then_inc(S["g_T"], 1)
                dve.wait_ge(S["b2_ps"], nth(b, 1, 1))
                dve.wait_ge(S["stored"], nth(b, 32, 32))
                at_ = seq[:, bass.ds(b * TILES, TT), :]
                dve.tensor_tensor(acc[:, 0:TT, :], ps[:, 6, :].rearrange("p (t d) -> p t d", t=TT), at_, ALU.add)
                dve.tensor_tensor(acc[0:TXT, TT:TILES, :], ps[0:TXT, 7, 0:D].unsqueeze(1), seq[0:TXT, bass.ds(b * TILES + TT, 1), :], ALU.add).then_inc(S["acc_init"], 1)
                for e in range(E):
                    dve.drain()
                    dve.wait_ge(S["down"], nth(b, E, e + 1))
                    for i in range(TILES):
                        r = ROWS[i]
                        c0 = (4 + 2 * (e % 2)) * 512 + i * P
                        op = dve.scalar_tensor_tensor(acc[0:r, i, :], psf[0:r, c0:c0 + P], gate[0:r, i, e:e + 1], acc[0:r, i, :], ALU.mult, ALU.add)
                    op.then_inc(S["acc_done"], 1)

            with dve.Fori(0, BATCH) as b:
                attention(b)

        @block.scalar
        def _(act):
            act.sem_inc(S["va_ready"], 1)
            act.sem_inc(S["prob_ready"], 2)
            act.sem_inc(S["probT_act"], 1)
            act.sem_inc(S["tx_pT"], 1)
            act.wait_ge(S["setup_done"], 1)

            def tok_exp(b, n):
                act.wait_ge(S["max_ready"], nth(b, UNITS, n + 1))
                if n >= 2:
                    act.wait_ge(S["probT_full"], nth(b, UNITS, n - 1))
                act.activation(prob[:, n % 2, :], ps[:, n % 2, :], ACT.Exp, bias=nmax[:, n:n + 1],
                               accum_out=psum_e[:, n:n + 1]).then_inc(S["prob_ready"], 1)

            def tok_probT(b, n):
                act.wait_ge(S["probT_full"], nth(b, UNITS, n + 1))
                act.activation(probT[:, n % 2, :], ps[:, 2 + n % 2, :], ACT.Copy).then_inc(S["probT_act"], 1)

            with act.Fori(0, BATCH) as b:
                act.wait_ge(S["proj_full"], nth(b, 5, 2))
                act.activation(qT[:, :], ps[:, 7, :], ACT.Copy, scale=DQ ** -0.5).then_inc(S["q_ready"], 1)
                act.wait_ge(S["proj_full"], nth(b, 5, 4))
                act.activation(v_tok[:, 0:2, :], ps[:, 7, :], ACT.Copy).then_inc(S["va_ready"], 1)
                for n in range(UNITS + 1):
                    if n < UNITS:
                        tok_exp(b, n)
                    if n >= 1 and (n - 1) % 2 == 0:
                        tok_probT(b, n - 1)

            with act.Fori(0, LAYERS) as l:
                act.wait_ge(S["tx_q"], nth(l, 1, 1))
                act.activation(tqT[:, :], ps[:, 1, 0:SEQ4], ACT.Identity, bias=bq4[:, bass.ds(l, 1)], scale=HD ** -0.5).then_inc(S["tx_qs"], 1)

                def exp(b):
                    act.wait_ge(S["tx_shift"], nth(l, BATCH, b + 1))
                    act.activation(ts[:, b, :], ts[:, b, :], ACT.Exp).then_inc(S["tx_exp"], 1)

                def copy_pT(b):
                    act.wait_ge(S["tx_pt"], nth(l, BATCH, b + 1))
                    act.activation(tpT[:, b, :].rearrange("p (g t) -> p g t", g=2), ps[0:TXT, 6:8, 0:HEADS // 2 * TXT], ACT.Copy).then_inc(S["tx_pT"], 1)

                exp(0)
                for b in range(BATCH):
                    if b + 1 < BATCH:
                        exp(b + 1)
                    copy_pT(b)
                act.wait_ge(S["tx_ct"], nth(l, 1, 1))
                act.activation(cT[:, :], ps[:, 0, 0:SEQ4], ACT.Copy).then_inc(S["tx_cT"], 1)
                for j in range(KT):
                    act.wait_ge(S["tx_f1"], nth(l, KT, j + 1))
                    act.activation(gact[:, j, :], ps[:, 4 + j, 0:SEQ4], ACT.Gelu,
                                   bias=vcol[:, bass.ds(VEC["b1"] + l * KT + j, 1)]).then_inc(S["tx_g"], 1)

            with act.Fori(0, BATCH) as b:
                for k, part in enumerate((lt1, lt2)):
                    act.wait_ge(S["la_min"], nth(b, 2, k + 1))
                    act.activation(part[:, :], part[:, :], ACT.Exp).then_inc(S["la_exp"], 1)
                for i in range(TILES):
                    act.wait_ge(S["la_vfull"], nth(b, TILES, i + 1))
                    act.activation(lv[:, i, :], ps[:, 6 + i % 2, :], ACT.Copy).then_inc(S["la_vdone"], 1)
                act.wait_ge(S["la_ktps"], nth(b, 1, 1))
                act.activation(lktok[:, :, :], ps[:, 0, :].rearrange("p (t d) -> p t d", t=TT), ACT.Copy).then_inc(S["la_ktok"], 1)
                for i in range(TILES):
                    r = ROWS[i]
                    act.wait_ge(S["la_ot"], nth(b, TILES, i + 1))
                    if i >= 2:
                        act.wait_ge(S["la_y"], nth(b, TILES, i - 1))
                    act.activation(lo[:, i % 2, :, 0:r], ps[:, 6 + i % 2, 0:4 * r].rearrange("p (g t) -> p g t", g=4), ACT.Copy).then_inc(S["la_lo"], 1)

            with act.Fori(0, BATCH) as b:
                for i in range(TILES):
                    act.wait_ge(S["fa_qkv"], nth(b, TILES, i + 1))
                    act.activation(qkv[:, i, :], ps[:, 2 + i, 0:3 * D], ACT.Copy).then_inc(S["fa_qkv_sb"], 1)
                act.wait_ge(S["fa_T"], nth(b, 2, 2))
                act.activation(fk[:, :], banks(2, T), ACT.Copy).then_inc(S["fa_kT"], 1)
                units = [(i, h) for i in range(TILES) for h in range(FH)]
                U = len(units)

                def exp(n):
                    i, h = units[n]
                    r, width = ROWS[i], min((i + 1) * P, T)
                    act.wait_ge(S["fa_max"], nth(b, U, n + 1))
                    if n >= 2:
                        act.wait_ge(S["fa_pn"], nth(b, U, n - 1))
                    act.activation(fp[0:r, n % 2, 0:width], banks(4 + 2 * (n % 2), width, r), ACT.Exp, bias=fnm[0:r, n:n + 1],
                                   accum_out=fsum[0:r, n:n + 1]).then_inc(S["fa_exp"], 1)

                def copy_pT(n):
                    i, h = units[n]
                    r = ROWS[i]
                    act.wait_ge(S["fa_pt"], nth(b, U, n + 1))
                    if n >= 2:
                        act.wait_ge(S["fa_o"], nth(b, U, n - 1))
                    if i < TT:
                        act.activation(fpT[:, n % 2, 0:(i + 1) * r], ps[:, n % 2, 0:(i + 1) * r], ACT.Copy).then_inc(S["fa_pT_act"], 1)
                    else:
                        act.activation(fpT[:, n % 2, 0:TT * r], ps[:, n % 2, 0:TT * r], ACT.Copy)
                        act.activation(fpT[0:r, n % 2, TT * r:(TT + 1) * r], ps[0:r, n % 2, TT * r:(TT + 1) * r], ACT.Copy).then_inc(S["fa_pT_act"], 1)

                for n in range(U + 2):
                    if n < U:
                        exp(n)
                    if n >= 2 and (n - 2) % 2 == 0:
                        copy_pT(n - 2)
                act.wait_ge(S["y_ps"], nth(b, 1, 1))
                act.activation(yT[:, 0:T], banks(0, T), ACT.Copy).then_inc(S["y_done"], 1)
                act.wait_ge(S["g_shift"], nth(b, 1, 1))
                act.activation(lg[:, :, :], lg[:, :, :], ACT.Exp).then_inc(S["g_exp"], 1)
                for n in range(E * EK):
                    e, f = divmod(n, EK)
                    act.wait_ge(S["up"], nth(b, E * EK, n + 1))
                    if f == 0 and e >= 2:
                        act.wait_ge(S["down"], nth(b, E, e - 1))
                    act.activation(hid[:, e % 2, f, :], banks(2 * (n % 2), T), ACT.Gelu_apprx_tanh,
                                   bias=vcol[:, VEC["eb"] + n:VEC["eb"] + n + 1]).then_inc(S["up_done"], 1)


N_PARAMS = 2 + 6 + 2 + 2 + 4 + 1 + BATCH + 5

def kernel(**inputs):
    import numpy as np
    import concourse.bacc as bacc
    from concourse.bass_utils import run_bass_kernel_spmd

    nc = bacc.Bacc("TRN2", target_bir_lowering=False, num_devices=1)
    arrays, aps = {}, {}
    for name, value in inputs.items():
        a = np.ascontiguousarray(value)
        arrays["in_" + name] = a
        aps[name] = nc.dram_tensor("in_" + name, a.shape, mybir.dt.from_np(a.dtype), kind="ExternalInput").ap()
    out = nc.dram_tensor("out", (BATCH, T, D), F32, kind="ExternalOutput").ap()
    fusion_kernel(nc, aps, out)
    r = run_bass_kernel_spmd(nc, [arrays], core_ids=[0])
    return r.results[0]["out"]
```

```python
from contextlib import ExitStack

import concourse.bass as bass
from concourse import mybir

F32 = mybir.dt.float32
F32R = mybir.dt.float32r
BF16 = mybir.dt.bfloat16
I32 = mybir.dt.int32
U32 = mybir.dt.uint32
ALU = mybir.AluOpType
ACT = mybir.ActivationFunctionType
AX = mybir.AxisListType

P = 128
BATCH, TOK, CH = 4, 512, 64
TXT = 77
D = 2 * CH
TT = TOK // P
TILES = TT + 1
T = TOK + TXT
ROWS = [P] * TT + [TXT]
NEG = -1.0e30

DQ = CH // 8
UNITS = 4 * TT

LAYERS, HEADS, HD, FF = 4, 8, 16, 512
SEQ4 = BATCH * TXT
KT = FF // P

LH, LD, LV = 8, 16, 64
LVA = LV + 1
FH, FD = 2, 64
E, EF = 8, 512
EK = EF // P

PAIRS = BATCH // 2
POS = BATCH * T
TILES_ALL = BATCH * TILES


def fusion_kernel(nc, A, out):
    ctx = ExitStack()
    with ctx:
        def sb(name, shape, dt=F32):
            return ctx.enter_context(nc.sbuf_tensor(name, shape, dt))

        def sem(name):
            return ctx.enter_context(nc.semaphore(name))

        TP = TILES * P
        vec_names = [("bq", LAYERS), ("bk", LAYERS), ("g1", LAYERS), ("c1", LAYERS), ("g2", LAYERS),
                     ("c2", LAYERS), ("b1", LAYERS * KT), ("eb", E * EK), ("fg", 1), ("fc", 1),
                     ("qn", 1), ("kn", 1)]
        VEC, at = {}, 0
        for n, c in vec_names:
            VEC[n] = at
            at += c
        NVEC = at
        seq = sb("seq", [P, BATCH * TILES, D])
        ident = sb("ident", [P, P])
        neghalf = sb("neghalf", [P, 4 * TILES])
        eps = sb("eps", [P, TILES_ALL])
        tiny = sb("tiny", [P, 4 * TILES])
        mix = sb("mix", [P, 2])
        hmask = sb("hmask", [P, HEADS])
        vrow = sb("vrow", [NVEC, D])
        vcol = sb("vcol", [P, NVEC])
        bq4 = sb("bq4", [P, LAYERS])
        qkg = sb("qkg", [P, 1])
        mv_l = sb("mv_l", [P, TILES_ALL, 2])
        va_l = sb("va_l", [P, TILES_ALL])
        rs_l = sb("rs_l", [P, TILES_ALL])
        mv_f = sb("mv_f", [P, TILES_ALL, 2])
        va_f = sb("va_f", [P, TILES_ALL])
        vb_f = sb("vb_f", [P, TILES_ALL])
        rs_f = sb("rs_f", [P, TILES_ALL])
        st5 = sb("st5", [P, 2, TILES, 6])
        mv5 = sb("mv5", [P, 2 * TILES, 2])
        xn = sb("xn", [P, 2, TILES, D])
        sT = sb("sT", [P, 2, TP])
        w_lraw = sb("w_lraw", [P, 6, D])
        w_loraw = sb("w_loraw", [P, LH * LV])
        w_lT = sb("w_lT", [P, 6 * P])
        w_loT = sb("w_loT", [P, 4, D])
        ones = sb("ones", [P, T])
        causal01 = sb("causal01", [P, P])
        w_fqkv = sb("w_fqkv", [P, 3 * D])
        w_fo = sb("w_fo", [P, D])
        w_gate = sb("w_gate", [P, E])
        gb_r = sb("gb_r", [P, E])
        b2_e = sb("b2_e", [E, D])
        identb = sb("identb", [P, P], BF16)
        causalb = sb("causalb", [P, P], BF16)
        w1_h = sb("w1_h", [P, E, EF], F32R)
        w1_l = sb("w1_l", [P, E, EF], F32R)
        w2_e = sb("w2_e", [P, E * EK, D])
        y_all = sb("y_all", [P, POS])
        y_h = sb("y_h", [P, POS], F32R)
        y_l = sb("y_l", [P, POS], F32R)
        lg = sb("lg", [P, TILES_ALL, E])
        lgm = sb("lgm", [P, TILES_ALL])
        gate = sb("gate", [P, TILES_ALL, E])

        first_half = ExitStack()

        def sb1(name, shape, dt=F32):
            return first_half.enter_context(nc.sbuf_tensor(name, shape, dt))

        x_in = sb1("x_in", [P, TT, D])
        w_qk = sb1("w_qk", [P, 2 * P])
        w_tv = sb1("w_tv", [P, 4 * CH])
        xT = sb1("xT", [P, TOK])
        qT = sb1("qT", [P, TOK])
        kT = sb1("kT", [P, TOK])
        v_tok = sb1("v_tok", [P, TT, 4 * CH])
        prob = sb1("prob", [P, 2, TOK])
        probT = sb1("probT", [P, 2, TOK])
        nmax = sb1("nmax", [P, UNITS])
        psum_e = sb1("psum_e", [P, UNITS])
        rsum = sb1("rsum", [P, UNITS])
        intra = sb1("intra", [P, 2, CH])
        tx = sb1("tx", [TXT, BATCH, D])
        tx_res = sb1("tx_res", [TXT, BATCH, D])
        tx_n = sb1("tx_n", [TXT, BATCH, D])
        tx_st = sb1("tx_st", [TXT, BATCH, 6])
        tx_mv = sb1("tx_mv", [TXT, BATCH, 2])
        tx_ve = sb1("tx_ve", [TXT, BATCH])
        tx_rs = sb1("tx_rs", [TXT, BATCH])
        tok_idx = sb1("tok_idx", [TXT, BATCH], I32)
        pos = sb1("pos", [TXT, D])
        padrow = sb1("padrow", [TXT, BATCH, TXT])
        causal_t = sb1("causal_t", [TXT, TXT])
        tmask = sb1("tmask", [TXT, BATCH, TXT])
        w_q = sb1("w_q", [D, D])
        w_k = sb1("w_k", [D, D])
        w_v = sb1("w_v", [D, D])
        w_o = sb1("w_o", [D, D])
        w_1 = sb1("w_1", [D, FF])
        w_2 = sb1("w_2", [P, KT, D])
        bv_r = sb1("bv_r", [TXT, LAYERS, D])
        bo_r = sb1("bo_r", [TXT, LAYERS, D])
        b2_r = sb1("b2_r", [TXT, LAYERS, D])
        lnf_g = sb1("lnf_g", [TXT, D])
        lnf_b = sb1("lnf_b", [TXT, D])
        hT = sb1("hT", [P, SEQ4])
        tqT = sb1("tqT", [P, SEQ4])
        kbd = sb1("kbd", [P, BATCH, HEADS * TXT])
        tv = sb1("tv", [TXT, BATCH, HEADS, HD + 1])
        ts = sb1("ts", [TXT, BATCH, HEADS * TXT])
        tpT = sb1("tpT", [TXT, BATCH, HEADS * TXT])
        tnm = sb1("tnm", [TXT, BATCH, HEADS])
        trs = sb1("trs", [TXT, BATCH, HEADS])
        tctx = sb1("tctx", [TXT, BATCH, D])
        cT = sb1("cT", [P, SEQ4])
        gact = sb1("gact", [P, KT, SEQ4])
        w1_raw = sb1("w1_raw", [P, 2, EF])
        first_half.close()

        linear_part = ExitStack()

        def sb2(name, shape, dt=F32):
            return linear_part.enter_context(nc.sbuf_tensor(name, shape, dt))

        lt1 = sb2("lt1", [P, 2, T])
        lt2 = sb2("lt2", [P, 2, T])
        lz = sb2("lz", [P, 2, TP])
        lq = sb2("lq", [P, 2, T])
        lk = sb2("lk", [P, 2, T])
        lv = sb2("lv", [P, 2, TILES, LH * LV])
        lktok = sb2("lktok", [P, 2, TT, P])
        lden = sb2("lden", [P, 2, TILES, LH])
        lrexp = sb2("lrexp", [P, 2, TILES, LH, LD])
        lqbd = sb2("lqbd", [P, 2, LH, P])
        la = sb2("la", [P, 2, LH, P])
        lo = sb2("lo", [P, 2, 4, P])
        lsbd = sb2("lsbd", [P, 2, LH * LV])
        linear_part.close()

        attention_part = ExitStack()

        def sb3(name, shape, dt=F32):
            return attention_part.enter_context(nc.sbuf_tensor(name, shape, dt))

        FU = 2 * FH * TILES
        qkv = sb3("qkv", [P, 2, TILES, 3 * D])
        sq = sb3("sq", [P, 2, TILES, 2 * D])
        ss = sb3("ss", [P, 2, TILES, 2 * FH])
        ssr = sb3("ssr", [P, 2, TILES, 2 * FH])
        fq = sb3("fq", [P, 2, T])
        fk = sb3("fk", [P, 2, T])
        fp = sb3("fp", [P, 2, T])
        fpn = sb3("fpn", [P, 2, T])
        fpT = sb3("fpT", [P, 2, 512])
        fnm = sb3("fnm", [P, FU])
        fsum = sb3("fsum", [P, FU])
        frs = sb3("frs", [P, FU])
        foT = sb3("foT", [P, 2, T])
        attention_part.close()

        hid = sb("hid", [P, 2, EK, TOK])
        gateT = sb("gateT", [E, TOK])
        gate_c = sb("gate_c", [P, 4, E])

        ps = ctx.enter_context(nc.psum_tensor("ps", [P, 8, 512], F32))
        psf = ps[:, :, :].rearrange("p b n -> p (b n)")

        def banks(first, width, rows_=P):
            return psf[0:rows_, first * 512:first * 512 + width]

        S = {}
        for n in ("""const_pool x_loaded qk_weights params txt_ids txt_embed setup_psum setup_done
                  proj_full xT_ready q_ready k_ready va_ready vb_ready
                  score_full max_ready prob_ready probT_full probT_ready out_full out_done
                  wq_loaded wk_loaded wv_loaded wo_loaded w1_loaded w2_loaded
                  tx_stat tx_rstd tx_resid tx_norm tx_normT tx_hT tx_k tx_q tx_v tx_kbd tx_qs tx_vs
                  tx_score tx_masked tx_shift tx_exp tx_pt tx_pT tx_pv tx_ctx tx_ct tx_cT tx_o tx_x
                  tx_f1 tx_g tx_f2 seq_tok seq_txt
                  block_params l_weights e_loaded e_high e_split l_wT l_wT_done
                  stat_tok rstd_lin stat_h rstd_h
                  la_norm la_normT la_hT la_qk la_min la_exp la_feat la_vfull la_vdone la_qz la_den la_rden la_rT la_q
                  la_ktps la_ktok la_qbd la_at la_masked la_ot la_lo la_state la_sbd la_y seq_tile lin_free
                  fa_xn fa_xT fa_hT fa_qkv fa_qkv_sb fa_ss fa_rs fa_norm fa_T fa_qT fa_kT fa_s fa_max fa_exp fa_pn
                  fa_pt fa_pT_act fa_pT_dve fa_o fa_oT y_ps y_done y_high y_split
                  g_ps g_shift g_exp g_chunk g_tps g_T b2_ps acc_init
                  up up_done down acc_done stored""").split():
            S[n] = sem(n)

        AT_SCORES = [0, 2, 4, 6]
        AT_SHIFT = [1, 3, 5, 7]
        AT_TURN = [[2, 3], [4, 5], [6, 7], [8, 9]]
        AT_VALUES = [4, 6, 8, 10]
        AT_CTX_TURN, AT_OUT, AT_NORM2, AT_TURN2, AT_UP, AT_DOWN = 11, 12, 13, 14, 15, 17
        HALF = HEADS * TXT // 2
        BANK_XT, BANK_Q, BANK_K, BANK_V = 2, 0, 1, 2
        BANK_S, BANK_T, BANK_O = 0, 2, 3
        BANK_TX = 4
        BANK_TV, BANK_TQ, BANK_TK = 5, 6, 7
        BANK_TY, BANK_TPT, BANK_TC = 5, 6, 7
        BANKS_UP = [5, 6, 7, 4]

        block = ctx.enter_context(nc.Block())

        def nth(turn, per_turn, k):
            return turn * per_turn + k

        def add_bias(pool, rows_, l):
            pool.tensor_tensor(tx_res[:, :, :], tx[:, :, :],
                               rows_[:, bass.ds(l, 1), :].broadcast_to([TXT, BATCH, D]), ALU.add).then_inc(S["tx_resid"], 1)

        @block.sync
        def _(sp):
            tokw = [("w1", 0, 0), ("w4", 0, 1), ("w7", 1, 2), ("w10", 1, 3)]
            tokk = [("w2", 0, 0), ("w5", 1, 1), ("w8", 1, 2), ("w11", 0, 3)]
            tokv = [("w3", 0, 0), ("w6", 1, 1), ("w9", 1, 2), ("w12", 0, 3)]
            sp.dma_start(x_in[:, :, :], A["x"][0].rearrange("(t p) c s -> p t (c s)", p=P)).then_inc(S["x_loaded"], 16)
            sp.dma_start(tok_idx[:, :], A["x_txt"].rearrange("b s -> s b"), allow_slow_non_contiguous=True).then_inc(S["txt_ids"], 16)
            sp.wait_ge(S["const_pool"], 1)
            for name, chan, a in tokw:
                sp.dma_start(w_qk[chan:D:2, 32 * a:32 * a + DQ], A[f"L0_tok_{name}"]).then_inc(S["qk_weights"], 16)
            for name, chan, a in tokk:
                sp.dma_start(w_qk[chan:D:2, P + 32 * a:P + 32 * a + DQ], A[f"L0_tok_{name}"]).then_inc(S["qk_weights"], 16)
            for name, chan, a in tokv:
                sp.dma_start(w_tv[chan:D:2, CH * a:CH * (a + 1)], A[f"L0_tok_{name}"]).then_inc(S["qk_weights"], 16)
            def param(dst, src):
                sp.dma_start(dst, src).then_inc(S["params"], 16)
            param(mix[:, 0:1], A["L0_tok_alpha"].partition_broadcast(P))
            param(mix[:, 1:2], A["L0_tok_gamma"].partition_broadcast(P))
            for n, src in (("bq", "txt_bq"), ("bk", "txt_bk"), ("g1", "txt_ln1_g"), ("c1", "txt_ln1_b"),
                           ("g2", "txt_ln2_g"), ("c2", "txt_ln2_b")):
                param(vrow[VEC[n]:VEC[n] + LAYERS, :], A[f"L0_{src}"])
            param(vrow[VEC["b1"]:VEC["b1"] + LAYERS * KT, :], A["L0_txt_b1"].rearrange("l (j p) -> (l j) p", p=P))
            param(vrow[VEC["eb"]:VEC["eb"] + E * EK, :], A["L0_ffn_b1"].rearrange("e (j p) -> (e j) p", p=P))
            param(vrow[VEC["fg"]:VEC["fg"] + 1, :], A["L0_ffn_ln_g"].unsqueeze(0))
            param(vrow[VEC["fc"]:VEC["fc"] + 1, :], A["L0_ffn_ln_b"].unsqueeze(0))
            for h in range(FH):
                param(vrow[VEC["qn"]:VEC["qn"] + 1, h * FD:(h + 1) * FD], A["L0_ffn_qn_g"].unsqueeze(0))
                param(vrow[VEC["kn"]:VEC["kn"] + 1, h * FD:(h + 1) * FD], A["L0_ffn_kn_g"].unsqueeze(0))
            param(pos[:, :], A["L0_txt_pos_emb"][0:TXT, :])
            for b in range(BATCH):
                param(padrow[:, b, :], A["mask_BS_f1_0"][b].partition_broadcast(TXT))
            param(bv_r[:, :, :], A["L0_txt_bv"].partition_broadcast(TXT))
            param(bo_r[:, :, :], A["L0_txt_bo"].partition_broadcast(TXT))
            param(b2_r[:, :, :], A["L0_txt_b2"].partition_broadcast(TXT))
            param(lnf_g[:, :], A["L0_txt_lnf_g"].partition_broadcast(TXT))
            param(lnf_b[:, :], A["L0_txt_lnf_b"].partition_broadcast(TXT))

            def layer_weights(l, first=False):
                for dst, src, loaded, used, per in (
                        (w_k[:, :], "Wk", "wk_loaded", "tx_k", 1),
                        (w_q[:, :], "Wq", "wq_loaded", "tx_q", 1),
                        (w_v[:, :], "Wv", "wv_loaded", "tx_v", 1),
                        (w_o[:, :], "Wo", "wo_loaded", "tx_o", 1),
                        (w_1[:, :], "W1", "w1_loaded", "tx_f1", KT),
                        (w_2[:, :, :], "W2", "w2_loaded", "tx_f2", 1)):
                    if not first:
                        sp.wait_ge(S[used], l * per)
                    t = A[f"L0_txt_{src}"]
                    s = t[l, :, :]
                    if src == "W2":
                        s = s.rearrange("(j p) n -> p j n", p=P)
                    sp.dma_start(dst, s).then_inc(S[loaded], 16)

            layer_weights(0, first=True)
            def expert_weights(t):
                for k in range(2):
                    sp.dma_start(w1_raw[:, k, :], A["L0_ffn_W1"][2 * t + k, :, :]).then_inc(S["e_loaded"], 16)

            expert_weights(0)
            with sp.Fori(1, BATCH) as b:
                sp.wait_ge(S["proj_full"], nth(b, 5, -4))
                sp.dma_start(x_in[:, :, :], A["x"][b, :, :, :].rearrange("(t p) c s -> p t (c s)", p=P)).then_inc(S["x_loaded"], 16)
                layer_weights(b)
                sp.wait_ge(S["e_split"], b)
                expert_weights(b)

            def load(signal, dst, src):
                sp.dma_start(dst, src).then_inc(S[signal], 16)
            for k, n in enumerate(("q", "k")):
                load("l_weights", w_lraw[:, k, :], A[f"L0_attn_W_{n}"])
            load("l_weights", w_lraw[:, 2:6, :], A["L0_attn_W_v"].rearrange("(j p) n -> p j n", p=P))
            load("l_weights", w_loraw[:, :], A["L0_attn_W_out"])
            for k, n in enumerate(("q", "k", "v")):
                load("block_params", w_fqkv[:, k * D:(k + 1) * D], A[f"L0_ffn_W{n}"])
            for e in range(E):
                load("block_params", w2_e[:, e * EK:(e + 1) * EK, :], A["L0_ffn_W2"][e].rearrange("(j p) n -> p j n", p=P))
            load("block_params", w_fo[:, :], A["L0_ffn_Wo"])
            load("block_params", w_gate[:, :], A["L0_ffn_gate_W"])
            load("block_params", gb_r[:, :], A["L0_ffn_gate_b"].partition_broadcast(P))
            load("block_params", b2_e[:, :], A["L0_ffn_b2"])
            for b in range(BATCH):
                sp.wait_ge(S["acc_done"], (b + 2) * E)
                sp.dma_start(out[b, 0:TOK, :].rearrange("(t p) c -> p t c", p=P), seq[:, TILES * b:TILES * b + TT, :]).then_inc(S["stored"], 16)
            sp.wait_ge(S["acc_done"], (BATCH + 2) * E)
            sp.dma_start(out[:, TOK:T, :].rearrange("b t c -> t b c"), seq[0:TXT, TT::TILES, :]).then_inc(S["stored"], 16)
            sp.wait_ge(S["stored"], 16 * (BATCH + 1))

        @block.gpsimd
        def _(pool):
            pool.memset(w_qk[:, :], 0.0)
            pool.memset(w_tv[:, :], 0.0)
            pool.memset(ident[:, :], 0.0)
            pool.memset(neghalf[:, :], -0.5)
            pool.memset(eps[:, :], 1e-5)
            pool.memset(tiny[:, :], 1e-12)
            pool.memset(hmask[:, :], 1.0)
            pool.memset(causal_t[:, :], 0.0)
            pool.memset(ones[:, :], 1.0)
            pool.memset(causal01[:, :], 1.0)
            pool.memset(identb[:, :], 0.0)
            pool.memset(causalb[:, :], 0.0)
            pool.memset(sT[:, :, :], 0.0)
            pool.drain().then_inc(S["const_pool"], 1)
            pool.wait_ge(S["txt_ids"], 16)
            for b in range(BATCH):
                pool.indirect_dma_start(
                    out=tx[:, b, :], out_offset=None, in_=A["L0_txt_item_emb"],
                    in_offset=bass.IndirectOffsetOnAxis(ap=tok_idx[:, b:b + 1].bitcast(U32), axis=0),
                ).then_inc(S["txt_embed"], 16)
            pool.affine_select(out=ident[:, :], in_=ident[:, :], compare_op=ALU.not_equal, fill=1.0,
                               base=0, pattern=[[-1, P]], channel_multiplier=1)
            pool.affine_select(out=causal_t[:, :], in_=causal_t[:, :], compare_op=ALU.is_ge, fill=NEG,
                               base=0, pattern=[[-1, TXT]], channel_multiplier=1)
            pool.affine_select(out=identb[:, :], in_=identb[:, :], compare_op=ALU.not_equal, fill=1.0,
                               base=0, pattern=[[-1, P]], channel_multiplier=1)
            pool.affine_select(out=causalb[:, :], in_=causalb[:, :], compare_op=ALU.is_ge, fill=NEG,
                               base=0, pattern=[[-1, P]], channel_multiplier=1)
            pool.affine_select(out=causal01[:, :], in_=causal01[:, :], compare_op=ALU.is_ge, fill=0.0,
                               base=0, pattern=[[1, P]], channel_multiplier=-1)
            pool.affine_select(out=hmask[:, :], in_=hmask[:, :], compare_op=ALU.is_ge, fill=0.0,
                               base=0, pattern=[[-HD, HEADS]], channel_multiplier=1)
            pool.drain()
            pool.affine_select(out=hmask[:, :], in_=hmask[:, :], compare_op=ALU.is_gt, fill=0.0,
                               base=HD, pattern=[[HD, HEADS]], channel_multiplier=-1)
            pool.drain().then_inc(S["const_pool"], 1)

            def rstd_txt(turn, k):
                pool.wait_ge(S["tx_stat"], nth(turn, 2, k))
                pool.tensor_tensor(tx_ve[:, :], tx_mv[:, :, 1], eps[0:TXT, 0:BATCH], ALU.add)
                pool.drain()
                pool.tensor_tensor(tx_rs[:, :], tx_ve[:, :], neghalf[0:TXT, 0:BATCH], ALU.pow).then_inc(S["tx_rstd"], 1)

            pool.wait_ge(S["setup_done"], 1)
            rstd_txt(0, 1)
            with pool.Fori(0, LAYERS) as l:
                add_bias(pool, bo_r, l)
                pool.wait_ge(S["e_high"], nth(l, 1, 1))
                experts = bass.ds(2 * l, 2)
                pool.tensor_tensor(w1_l[:, experts, :], w1_raw[:, :, :], w1_h[:, experts, :].bitcast(F32), ALU.subtract).then_inc(S["e_split"], 1)
                rstd_txt(l, 2)
                add_bias(pool, b2_r, l)
                rstd_txt(l, 3)
                pool.wait_ge(S["stat_tok"], nth(l, 1, 1))
                tiles = bass.ds(l * TILES, TT)
                pool.tensor_tensor(va_l[:, tiles], mv_l[:, tiles, 1], eps[:, 0:TT], ALU.add)
                pool.drain()
                pool.tensor_tensor(rs_l[:, tiles], va_l[:, tiles], neghalf[:, 0:TT], ALU.pow).then_inc(S["rstd_lin"], 1)
            pool.wait_ge(S["stat_tok"], BATCH + 1)
            pool.tensor_tensor(va_l[:, TT::TILES], mv_l[:, TT::TILES, 1], eps[:, 0:BATCH], ALU.add)
            pool.drain()
            pool.tensor_tensor(rs_l[:, TT::TILES], va_l[:, TT::TILES], neghalf[:, 0:BATCH], ALU.pow).then_inc(S["rstd_lin"], 1)


            with pool.Fori(0, PAIRS) as p:
                for i in range(TILES):
                    for s in range(2):
                        if i == 0:
                            pool.wait_ge(S["la_q"], nth(p, 2, s + 1))
                        else:
                            pool.wait_ge(S["la_at"], nth(p, 2 * TILES, 2 * i + s - 1))
                        r = ROWS[i]
                        pool.tensor_tensor(lqbd[:, s, :, 0:r], lq[:, s, i * P:i * P + r].unsqueeze(1).broadcast_to([P, LH, r]),
                                           hmask[:, :].unsqueeze(2).broadcast_to([P, LH, r]), ALU.mult).then_inc(S["la_qbd"], 1)
                pool.wait_ge(S["stat_h"], nth(p, 1, 1))
                tiles = bass.ds(p * 2 * TILES, 2 * TILES)
                pool.tensor_tensor(va_f[:, tiles], mv_f[:, tiles, 1], eps[:, 0:2 * TILES], ALU.add)
                pool.drain()
                pool.tensor_tensor(rs_f[:, tiles], va_f[:, tiles], neghalf[:, 0:2 * TILES], ALU.pow)
                pool.drain()
                pool.tensor_tensor(vb_f[:, tiles], rs_f[:, tiles], rs_f[:, tiles], ALU.mult)
                pool.drain()
                pool.tensor_tensor(vb_f[:, tiles], vb_f[:, tiles], mv_f[:, tiles, 1], ALU.mult)
                pool.drain()
                pool.tensor_tensor(vb_f[:, tiles], vb_f[:, tiles], eps[:, 0:2 * TILES], ALU.add)
                pool.drain()
                pool.tensor_tensor(va_f[:, tiles], vb_f[:, tiles], neghalf[:, 0:2 * TILES], ALU.pow)
                pool.drain()
                pool.tensor_tensor(rs_f[:, tiles], rs_f[:, tiles], va_f[:, tiles], ALU.mult).then_inc(S["rstd_h"], 1)

            with pool.Fori(0, PAIRS) as p:
                for s in range(2):
                    pool.wait_ge(S["fa_ss"], nth(p, 2, s + 1))
                    pool.tensor_tensor(ss[:, s, :, :], ss[:, s, :, :], tiny[:, :].rearrange("p (t h) -> p t h", t=TILES), ALU.add)
                    pool.drain()
                    pool.tensor_tensor(ssr[:, s, :, :], ss[:, s, :, :], neghalf[:, :].rearrange("p (t h) -> p t h", t=TILES), ALU.pow).then_inc(S["fa_rs"], 1)
                for s in range(2):
                    pool.wait_ge(S["y_high"], nth(p, 2, s + 1))
                    for cols in (bass.ds((2 * p + s) * TOK, TOK), bass.ds(BATCH * TOK + (2 * p + s) * TXT, TXT)):
                        op = pool.tensor_tensor(y_l[:, cols], y_all[:, cols], y_h[:, cols].bitcast(F32), ALU.subtract)
                    op.then_inc(S["y_split"], 1)

        @block.tensor
        def _(pe):
            def transpose(dst, src, rows_in):
                return pe.transpose(dst, src, ident[0:rows_in, 0:rows_in])

            pe.wait_ge(S["const_pool"], 2)
            pe.wait_ge(S["params"], 16 * N_PARAMS)
            transpose(ps[:, 7, 0:NVEC], vrow[:, :], NVEC).then_inc(S["setup_psum"], 1)
            pe.wait_ge(S["qk_weights"], 16 * 12)

            def tok_turn_x(b):
                pe.wait_ge(S["x_loaded"], nth(b, 16, 16))
                for t in range(TT):
                    mm = transpose(ps[:, BANK_XT, t * P:(t + 1) * P], x_in[:, t, :], P)
                mm.then_inc(S["proj_full"], 1)

            def tok_project_qk(b):
                pe.wait_ge(S["xT_ready"], nth(b, 1, 1))
                for bank, w0 in ((BANK_Q, 0), (BANK_K, P)):
                    pe.matmul(ps[:, bank, :], w_qk[:, w0:w0 + P], xT[:, :], start=True, stop=True).then_inc(S["proj_full"], 1)

            def tok_project_v(b):
                pe.wait_ge(S["out_done"], nth(b, UNITS, 1))
                for half in range(2):
                    for t in range(2):
                        tile_ = 2 * half + t
                        mm = pe.matmul(ps[:, BANK_V + half, t * 256:(t + 1) * 256], xT[:, tile_ * P:(tile_ + 1) * P],
                                       w_tv[:, :], start=True, stop=True)
                    mm.then_inc(S["proj_full"], 1)

            def tok_scores(b, n):
                i, a = divmod(n, 4)
                if n == 0:
                    pe.wait_ge(S["q_ready"], nth(b, 1, 1))
                    pe.wait_ge(S["k_ready"], nth(b, 1, 1))
                if n >= 2:
                    pe.wait_ge(S["prob_ready"], nth(b, UNITS, n - 1))
                pe.matmul(ps[:, BANK_S + n % 2, :], qT[32 * a:32 * a + DQ, i * P:(i + 1) * P],
                          kT[32 * a:32 * a + DQ, :], start=True, stop=True).then_inc(S["score_full"], 1)

            def tok_turn(b, n):
                pe.wait_ge(S["prob_ready"], nth(b, UNITS, n + 1))
                if n == 0:
                    pe.wait_ge(S["va_ready"], nth(b, 1, 1))
                    pe.wait_ge(S["vb_ready"], nth(b, 1, 1))
                else:
                    pe.wait_ge(S["probT_ready"], nth(b, UNITS, n))
                for j in range(TT):
                    mm = transpose(ps[:, BANK_T, j * P:(j + 1) * P], prob[:, n % 2, j * P:(j + 1) * P], P)
                mm.then_inc(S["probT_full"], 1)

            def tok_values(b, n):
                a = n % 4
                pe.wait_ge(S["probT_ready"], nth(b, UNITS, n + 1))
                pe.wait_ge(S["out_done"], nth(b, UNITS, n + 1))
                for j in range(TT):
                    mm = pe.matmul(ps[:, BANK_O, 0:2 * CH], probT[:, n % 2, j * P:(j + 1) * P],
                                   v_tok[:, j, a // 2 * 2 * CH:(a // 2 + 1) * 2 * CH], start=(j == 0), stop=(j == TT - 1))
                mm.then_inc(S["out_full"], 1)

            def txt_turn_norm(l, k):
                pe.wait_ge(S["tx_norm"], nth(l, 2, k))
                for b in range(BATCH):
                    mm = transpose(ps[:, BANK_TX, b * TXT:(b + 1) * TXT], tx_n[:, b, :], TXT)
                mm.then_inc(S["tx_normT"], 1)

            def txt_project(l):
                pe.wait_ge(S["tx_hT"], nth(l, 2, 1))
                pe.wait_ge(S["wk_loaded"], nth(l, 16, 16))
                pe.matmul(ps[:, BANK_TK, 0:SEQ4], w_k[:, :], hT[:, :], start=True, stop=True).then_inc(S["tx_k"], 1)
                pe.wait_ge(S["wq_loaded"], nth(l, 16, 16))
                pe.matmul(ps[:, BANK_TQ, 0:SEQ4], w_q[:, :], hT[:, :], start=True, stop=True).then_inc(S["tx_q"], 1)
                pe.wait_ge(S["wv_loaded"], nth(l, 16, 16))
                for b in range(BATCH):
                    mm = pe.matmul(ps[0:TXT, BANK_TV, b * D:(b + 1) * D], hT[:, b * TXT:(b + 1) * TXT], w_v[:, :], start=True, stop=True)
                mm.then_inc(S["tx_v"], 1)

            def txt_scores(l, b):
                if b == 0:
                    pe.wait_ge(S["tx_qs"], nth(l, 1, 1))
                    pe.wait_ge(S["tx_vs"], nth(l, 1, 1))
                else:
                    pe.wait_ge(S["tx_masked"], nth(l, BATCH, b))
                pe.wait_ge(S["tx_kbd"], nth(l, BATCH, b + 1))
                for g in range(2):
                    mm = pe.matmul(ps[0:TXT, BANK_TX + g, 0:HALF], tqT[:, b * TXT:(b + 1) * TXT],
                                   kbd[:, b, g * HALF:(g + 1) * HALF], start=True, stop=True)
                mm.then_inc(S["tx_score"], 1)

            def txt_turn_probs(l, b, g):
                pe.wait_ge(S["tx_exp"], nth(l, BATCH, b + 1))
                if 2 * b + g >= 1:
                    pe.wait_ge(S["tx_pT"], nth(l, 2 * BATCH, 2 * b + g))
                for k in range(HEADS // 2):
                    h = g * HEADS // 2 + k
                    mm = transpose(ps[0:TXT, BANK_TPT, k * TXT:(k + 1) * TXT], ts[:, b, h * TXT:(h + 1) * TXT], TXT)
                mm.then_inc(S["tx_pt"], 1)

            def txt_values(l, b):
                pe.wait_ge(S["tx_pT"], nth(l, 2 * BATCH, 2 * b + 2))
                if b == 0:
                    pe.wait_ge(S["tx_kbd"], nth(l, BATCH, BATCH))
                else:
                    pe.wait_ge(S["tx_ctx"], nth(l, BATCH, b))
                for h in range(HEADS):
                    mm = pe.matmul(ps[0:TXT, BANK_TC, h * (HD + 1):(h + 1) * (HD + 1)],
                                   tpT[:, b, h * TXT:(h + 1) * TXT], tv[:, b, h, :], start=True, stop=True)
                mm.then_inc(S["tx_pv"], 1)

            def txt_turn_ctx(l):
                pe.wait_ge(S["tx_ctx"], nth(l, BATCH, BATCH))
                pe.wait_ge(S["tx_masked"], nth(l, BATCH, BATCH))
                for b in range(BATCH):
                    mm = transpose(ps[:, BANK_TX, b * TXT:(b + 1) * TXT], tctx[:, b, :], TXT)
                mm.then_inc(S["tx_ct"], 1)

            def txt_out(l):
                pe.wait_ge(S["tx_cT"], nth(l, 1, 1))
                pe.wait_ge(S["wo_loaded"], nth(l, 16, 16))
                for b in range(BATCH):
                    mm = pe.matmul(ps[0:TXT, BANK_TY, b * D:(b + 1) * D], cT[:, b * TXT:(b + 1) * TXT], w_o[:, :], start=True, stop=True)
                mm.then_inc(S["tx_o"], 1)

            def txt_up(l):
                pe.wait_ge(S["tx_hT"], nth(l, 2, 2))
                pe.wait_ge(S["w1_loaded"], nth(l, 16, 16))
                for j in range(KT):
                    pe.matmul(ps[:, BANKS_UP[j], 0:SEQ4], w_1[:, j * P:(j + 1) * P], hT[:, :], start=True, stop=True).then_inc(S["tx_f1"], 1)

            def txt_down(l):
                pe.wait_ge(S["tx_g"], nth(l, KT, KT))
                pe.wait_ge(S["w2_loaded"], nth(l, 16, 16))
                for b in range(BATCH):
                    for j in range(KT):
                        mm = pe.matmul(ps[0:TXT, BANK_TY, b * D:(b + 1) * D], gact[:, j, b * TXT:(b + 1) * TXT],
                                       w_2[:, j, :], start=(j == 0), stop=(j == KT - 1))
                mm.then_inc(S["tx_f2"], 1)

            with pe.Fori(0, BATCH) as t:
                tok_turn_x(t)
                tok_project_qk(t)
                txt_turn_norm(t, 1)
                txt_project(t)
                tok_project_v(t)
                for n in range(UNITS + 2):
                    if n < UNITS:
                        tok_scores(t, n)
                    if n in AT_SCORES:
                        txt_scores(t, AT_SCORES.index(n))
                    for b in range(BATCH):
                        for g in range(2):
                            if n == AT_TURN[b][g]:
                                txt_turn_probs(t, b, g)
                    if n in AT_VALUES:
                        txt_values(t, AT_VALUES.index(n))
                    if n == AT_CTX_TURN:
                        txt_turn_ctx(t)
                    if n == AT_OUT:
                        txt_out(t)
                    if n == AT_TURN2:
                        txt_turn_norm(t, 2)
                    if n == AT_UP:
                        txt_up(t)
                    if n == AT_DOWN:
                        txt_down(t)
                    if 1 <= n <= UNITS:
                        tok_turn(t, n - 1)
                    if n >= 2:
                        tok_values(t, n - 2)

            pe.wait_ge(S["seq_tok"], BATCH)
            pe.wait_ge(S["tx_norm"], 2 * LAYERS + 1)
            pe.wait_ge(S["l_weights"], 16 * 4)
            for k in range(6):
                mm = transpose(ps[:, k // 4, k % 4 * P:(k % 4 + 1) * P], w_lraw[:, k, :], P)
            for k in range(4):
                mm = transpose(ps[:, 2, k * P:(k + 1) * P], w_loraw[:, k * P:(k + 1) * P], P)
            mm.then_inc(S["l_wT"], 1)
            pe.wait_ge(S["l_wT_done"], 1)

            def wide(bank, lhsT, rhs, width=T):
                pe.matmul(banks(bank, 512), lhsT, rhs[:, 0:512], start=True, stop=True)
                return pe.matmul(ps[:, bank + 1, 0:width - 512], lhsT, rhs[:, 512:width], start=True, stop=True)

            def turn_tiles(s):
                for i in range(TILES):
                    r = ROWS[i]
                    c0 = 4 * s * 512 + i * P
                    mm = transpose(psf[:, c0:c0 + r], xn[0:r, s, i, :], r)
                return mm

            BO, BS, BA = 0, 1, 2

            def la_scores(p, s, i):
                r = ROWS[i]
                pe.wait_ge(S["la_qbd"], nth(p, 2 * TILES, 2 * i + s + 1))
                for g in range(2):
                    mm = pe.matmul(ps[0:r, 4 * s + BA + g, 0:4 * r], lk[:, s, i * P:i * P + r],
                                   lqbd[:, s, 4 * g:4 * g + 4, 0:r], start=True, stop=True)
                mm.then_inc(S["la_at"], 1)

            def la_outputs(p, s, i):
                r = ROWS[i]
                pe.wait_ge(S["la_masked"], nth(p, 2 * TILES, 2 * i + s + 1))
                if i >= 1:
                    pe.wait_ge(S["la_sbd"], nth(p, 2 * TT, 2 * (i - 1) + s + 1))
                    pe.wait_ge(S["seq_tile"], nth(p, 2 * TILES, 2 * (i - 1) + s + 1))
                bank = 4 * s + BO
                for g in range(4):
                    if i >= 1:
                        pe.matmul(ps[:, bank, g * r:(g + 1) * r], lsbd[:, s, g * P:(g + 1) * P], lq[:, s, i * P:i * P + r],
                                  start=True, stop=False, skip_group_check=True)
                    for h in (2 * g, 2 * g + 1):
                        p0 = LV * (h % 2)
                        mm = pe.matmul(ps[p0:p0 + LV, bank, g * r:(g + 1) * r], lv[0:r, s, i, h * LV:(h + 1) * LV],
                                       la[0:r, s, h, 0:r], start=(i == 0), stop=True, skip_group_check=True)
                mm.then_inc(S["la_ot"], 1)

            def la_state(p, s, i):
                pe.matmul(ps[:, 4 * s + BS, :], lktok[:, s, i, :], lv[:, s, i, :], start=(i == 0), stop=(i == TT - 1),
                          skip_group_check=True).then_inc(S["la_state"], 1)

            def la_project(p, s, i):
                r = ROWS[i]
                pe.wait_ge(S["la_lo"], nth(p, 2 * TILES, 2 * i + s + 1))
                for g in range(4):
                    mm = pe.matmul(ps[0:r, 4 * s + BO, 0:D], lo[:, s, g, 0:r], w_loT[:, g, :],
                                   start=(g == 0), stop=(g == 3))
                mm.then_inc(S["la_y"], 1)

            with pe.Fori(0, PAIRS) as p:
                for s in range(2):
                    pe.wait_ge(S["lin_free"], nth(p, 2, s + 1))
                    pe.wait_ge(S["la_norm"], nth(p, 2, s + 1))
                    turn_tiles(s).then_inc(S["la_normT"], 1)
                for s in range(2):
                    pe.wait_ge(S["la_hT"], nth(p, 2, s + 1))
                    wide(4 * s + 2, w_lT[:, P:2 * P], sT[:, s, :]).then_inc(S["la_qk"], 1)
                    wide(4 * s, w_lT[:, 0:P], sT[:, s, :]).then_inc(S["la_qk"], 1)
                for s in range(2):
                    pe.wait_ge(S["la_feat"], nth(p, 4, 2 * s + 2))
                    for i in range(TILES):
                        if i >= 2:
                            pe.wait_ge(S["la_vdone"], nth(p, 2 * TILES, TILES * s + i - 1))
                        pe.matmul(ps[:, 4 * s + i % 2, :], sT[:, s, i * P:(i + 1) * P], w_lT[:, 2 * P:6 * P], start=True, stop=True).then_inc(S["la_vfull"], 1)
                    for i in range(TT):
                        mm = transpose(ps[:, 4 * s + 2, i * P:(i + 1) * P], lk[:, s, i * P:(i + 1) * P], P)
                    mm.then_inc(S["la_ktps"], 1)
                    pe.wait_ge(S["la_qz"], nth(p, 2, s + 1))
                    for i in range(TILES):
                        mm = pe.matmul(ps[:, 4 * s + 3, i * LH:(i + 1) * LH], lz[:, s, i * P:(i + 1) * P], hmask[:, :], start=True, stop=True)
                    mm.then_inc(S["la_den"], 1)
                for s in range(2):
                    pe.wait_ge(S["la_rden"], nth(p, 2, s + 1))
                    pe.wait_ge(S["la_ktok"], nth(p, 2, s + 1))
                    for i in range(TILES):
                        r = ROWS[i]
                        c0 = (4 * s + 2) * 512 + i * P
                        mm = transpose(psf[:, c0:c0 + r], lrexp[0:r, s, i, :, :].rearrange("p h d -> p (h d)"), r)
                    mm.then_inc(S["la_rT"], 1)
                pe.wait_ge(S["la_q"], nth(p, 2, 2))
                pe.wait_ge(S["la_vdone"], nth(p, 2 * TILES, 2 * TILES))
                for i in range(TILES):
                    for s in range(2):
                        la_scores(p, s, i)
                    if i >= 1:
                        for s in range(2):
                            la_project(p, s, i - 1)
                    for s in range(2):
                        la_outputs(p, s, i)
                    if i < TT:
                        for s in range(2):
                            la_state(p, s, i)
                for s in range(2):
                    la_project(p, s, TT)

            pe.wait_ge(S["lin_free"], BATCH + 2)
            pe.wait_ge(S["block_params"], 16 * (7 + E))
            units = [(i, h, s) for i in range(TILES) for h in range(FH) for s in range(2)]

            def fa_scores(p, n):
                i, h, s = units[n]
                r, width = ROWS[i], min((i + 1) * P, T)
                if n >= 2:
                    pe.wait_ge(S["fa_exp"], nth(p, FU, n - 1))
                lhsT = fq[h * FD:(h + 1) * FD, s, i * P:i * P + r]
                for c, w in ((0, min(width, 512)), (512, width - 512)):
                    if w > 0:
                        pe.matmul(ps[0:r, 4 * s + c // 512, 0:w], lhsT, fk[h * FD:(h + 1) * FD, s, c:c + w],
                                  start=True, stop=False, skip_group_check=True)
                c0 = 4 * s * 512 + i * P
                pe.matmul(psf[0:r, c0:c0 + r], identb[0:r, 0:r], causalb[0:r, 0:r],
                          start=False, stop=True, skip_group_check=True).then_inc(S["fa_s"], 1)

            def wait_pT(p, n):
                pe.wait_ge(S["fa_pT_act" if n % 2 == 0 else "fa_pT_dve"], nth(p, FU // 2, n // 2 + 1))

            def fa_turn(p, n):
                i, h, s = units[n]
                r = ROWS[i]
                pe.wait_ge(S["fa_pn"], nth(p, FU, n + 1))
                if n >= 2:
                    wait_pT(p, n - 2)
                for j in range(i + 1):
                    c = ROWS[j]
                    mm = transpose(ps[0:c, 4 * s + 2, j * r:(j + 1) * r], fpn[0:r, s, j * P:j * P + c], r)
                mm.then_inc(S["fa_pt"], 1)

            def fa_values(p, n):
                i, h, s = units[n]
                r = ROWS[i]
                wait_pT(p, n)
                if h == 0 and i >= 1:
                    pe.wait_ge(S["fa_oT"], nth(p, 2 * TILES, 2 * (i - 1) + s + 1))
                for j in range(i + 1):
                    c = ROWS[j]
                    mm = pe.matmul(ps[h * FD:(h + 1) * FD, 4 * s + 3, 0:r],
                                   qkv[0:c, s, j, 2 * D + h * FD:2 * D + (h + 1) * FD], fpT[0:c, s, j * r:(j + 1) * r],
                                   start=(j == 0), stop=(j == i))
                mm.then_inc(S["fa_o"], 1)

            with pe.Fori(0, PAIRS) as p:
                for s in range(2):
                    pe.wait_ge(S["y_done"], nth(p, 2, s + 1))
                    pe.wait_ge(S["fa_xn"], nth(p, 2, s + 1))
                    turn_tiles(s).then_inc(S["fa_xT"], 1)
                for i in range(TILES):
                    for s in range(2):
                        if i == 0:
                            pe.wait_ge(S["fa_hT"], nth(p, 2, s + 1))
                        if i >= 2:
                            pe.wait_ge(S["fa_qkv_sb"], nth(p, 2 * TILES, 2 * (i - 2) + s + 1))
                        pe.matmul(ps[:, 4 * s + 2 + i % 2, 0:3 * D], sT[:, s, i * P:(i + 1) * P], w_fqkv[:, :],
                                  start=True, stop=True).then_inc(S["fa_qkv"], 1)
                for s in range(2):
                    pe.wait_ge(S["fa_norm"], nth(p, 2, s + 1))
                    for part in range(2):
                        for i in range(TILES):
                            r = ROWS[i]
                            c0 = (4 * s + 2 * part) * 512 + i * P
                            mm = transpose(psf[:, c0:c0 + r], qkv[0:r, s, i, part * D:(part + 1) * D], r)
                        mm.then_inc(S["fa_T"], 1)
                pe.wait_ge(S["fa_qT"], nth(p, 2, 2))
                pe.wait_ge(S["fa_kT"], nth(p, 2, 2))
                for n in range(FU + 3):
                    if n < FU:
                        fa_scores(p, n)
                    if 2 <= n <= FU + 1:
                        fa_turn(p, n - 2)
                    if n >= 3:
                        fa_values(p, n - 3)
                for s in range(2):
                    pe.wait_ge(S["fa_oT"], nth(p, 2 * TILES, 2 * TT + s + 1))
                    wide(4 * s, w_fo[:, :], foT[:, s, :]).then_inc(S["y_ps"], 1)

            pe.wait_ge(S["y_done"], BATCH + 2)
            pe.wait_ge(S["e_split"], BATCH)
            for j in range(TILES_ALL):
                c0, r = (j * P, P) if j < BATCH * TT else (BATCH * TOK + (j - BATCH * TT) * TXT, TXT)
                mm = pe.matmul(ps[0:r, 7, j * E:(j + 1) * E], y_all[:, c0:c0 + r], w_gate[:, :], start=True, stop=True)
            mm.then_inc(S["g_ps"], 1)
            pe.wait_ge(S["y_split"], BATCH)

            def experts(c, r, cols):
                width = 4 * r

                def up(e):
                    for f in range(EK):
                        n = e * EK + f
                        if n >= 4:
                            pe.wait_ge(S["up_done"], nth(c, E * EK, n - 3))
                        for k, (w, y) in enumerate(((w1_h, y_h), (w1_h, y_l), (w1_l, y_h))):
                            mm = pe.matmul(ps[:, n % 4, 0:width], w[:, e, f * P:(f + 1) * P], y[:, cols], start=(k == 0), stop=(k == 2))
                        mm.then_inc(S["up"], 1)

                def down(e):
                    pe.wait_ge(S["up_done"], nth(c, E * EK, (e + 1) * EK))
                    if e >= 4:
                        pe.wait_ge(S["acc_done"], nth(c, E, E + e - 3))
                    for i in range(4):
                        for f in range(EK):
                            mm = pe.matmul(ps[0:r, 4 + e % 4, i * P:(i + 1) * P], hid[:, e % 2, f, i * r:(i + 1) * r],
                                           w2_e[:, e * EK + f, :], start=(f == 0), stop=(f == EK - 1))
                    mm.then_inc(S["down"], 1)

                up(0)
                pe.wait_ge(S["g_chunk"], nth(c, 1, 1))
                pe.wait_ge(S["acc_done"], nth(c, E, E))
                for i in range(4):
                    mm = transpose(ps[0:E, 4, i * r:(i + 1) * r], gate_c[0:r, i, :], r)
                mm.then_inc(S["g_tps"], 1)
                up(1)
                pe.wait_ge(S["g_T"], nth(c, 1, 1))
                for i in range(4):
                    mm = pe.matmul(ps[0:r, 5, i * P:(i + 1) * P], gateT[:, i * r:(i + 1) * r], b2_e[:, :], start=True, stop=True)
                mm.then_inc(S["b2_ps"], 1)
                for e in range(E):
                    if 1 <= e < E - 1:
                        up(e + 1)
                    if e == 1:
                        pe.wait_ge(S["acc_init"], nth(c, 1, 1))
                    down(e)

            with pe.Fori(0, BATCH) as c:
                experts(c, P, bass.ds(c * TOK, TOK))
            experts(BATCH, TXT, slice(BATCH * TOK, POS))

        @block.vector
        def _(dve):
            def one(buffer, k):
                return buffer[:, bass.ds(k, 1), :].rearrange("p a d -> p (a d)")

            def seq_at(k):
                return one(seq, k)

            dve.sem_inc(S["out_done"], 1)
            dve.sem_inc(S["lin_free"], 2)
            dve.sem_inc(S["acc_done"], E)
            dve.memset(tv[:, :, :, HD:HD + 1], 1.0)
            dve.memset(seq[:, :, :], 0.0)
            dve.wait_ge(S["setup_psum"], 1)
            dve.tensor_copy(vcol[:, :], ps[:, 7, 0:NVEC])
            dve.tensor_scalar(tmask[:, :, :], padrow[:, :, :], 0.0, NEG, ALU.is_equal, ALU.mult)
            dve.drain()
            dve.tensor_tensor(tmask[:, :, :], tmask[:, :, :], causal_t[:, :].unsqueeze(1).broadcast_to([TXT, BATCH, TXT]), ALU.add)
            dve.tensor_scalar(bq4[:, :], vcol[:, VEC["bq"]:VEC["bq"] + LAYERS], HD ** -0.5, None, ALU.mult)
            dve.scalar_tensor_tensor(qkg[:, :], vcol[:, VEC["qn"]:VEC["qn"] + 1], FD ** 0.5,
                                     vcol[:, VEC["kn"]:VEC["kn"] + 1], ALU.mult, ALU.mult)
            dve.wait_ge(S["txt_embed"], 16 * BATCH)
            dve.tensor_tensor(tx[:, :, :], tx[:, :, :], pos[:, :].unsqueeze(1).broadcast_to([TXT, BATCH, D]), ALU.add)
            dve.drain().then_inc(S["setup_done"], 1)

            def tok_keys(b):
                dve.wait_ge(S["proj_full"], nth(b, 5, 3))
                dve.tensor_copy(kT[:, :], ps[:, BANK_K, :]).then_inc(S["k_ready"], 1)

            def tok_vb(b):
                dve.wait_ge(S["proj_full"], nth(b, 5, 5))
                dve.tensor_copy(v_tok[:, 2:4, :], ps[:, BANK_V + 1, :]).then_inc(S["vb_ready"], 1)

            def tok_max(b, n):
                dve.wait_ge(S["score_full"], nth(b, UNITS, n + 1))
                dve.tensor_reduce(nmax[:, n:n + 1], ps[:, n % 2, :], AX.X, ALU.max, negate=True).then_inc(S["max_ready"], 1)

            def tok_rsum(b, n):
                dve.wait_ge(S["prob_ready"], nth(b, UNITS, n + 1))
                dve.reciprocal(rsum[:, n:n + 1], psum_e[:, n:n + 1])

            def tok_out(b, n):
                i, a = divmod(n, 4)
                s = a // 2
                dve.wait_ge(S["out_full"], nth(b, UNITS, n + 1))
                o = ps[:, BANK_O, a % 2 * CH:(a % 2 + 1) * CH]
                if a % 2 == 0:
                    dve.tensor_scalar(intra[:, s, :], o, rsum[:, n:n + 1], mix[:, s:s + 1], ALU.mult, ALU.mult).then_inc(S["out_done"], 1)
                else:
                    dst = seq[:, bass.ds(b * TILES + i, 1), s * CH:(s + 1) * CH]
                    dve.scalar_tensor_tensor(dst, o.unsqueeze(1), rsum[:, n:n + 1], intra[:, s, :].unsqueeze(1), ALU.mult, ALU.add).then_inc(S["out_done"], 1)

            def norm_stats(l, k):
                for b in range(BATCH):
                    dve.bn_stats(tx_st[:, b, :], tx[:, b, :])
                dve.drain()
                for b in range(BATCH):
                    mm = dve.bn_aggr(tx_mv[:, b, :], tx_st[:, b, :])
                mm.then_inc(S["tx_stat"], 1)

            def normalise(l, k):
                dve.wait_ge(S["tx_rstd"], nth(l, 2, k))
                for b in range(BATCH):
                    mm = dve.tensor_scalar(tx_n[:, b, :], tx[:, b, :], tx_mv[:, b, 0:1], tx_rs[:, b:b + 1], ALU.subtract, ALU.mult)
                mm.then_inc(S["tx_norm"], 1)

            def scale_turned(l, k, g, c):
                dve.wait_ge(S["tx_normT"], nth(l, 2, k))
                dve.tensor_scalar(hT[:, :], ps[:, BANK_TX, 0:SEQ4], vcol[:, bass.ds(VEC[g] + l, 1)], vcol[:, bass.ds(VEC[c] + l, 1)],
                                  ALU.mult, ALU.add).then_inc(S["tx_hT"], 1)

            def txt_kbd(l, b):
                dve.scalar_tensor_tensor(
                    kbd[:, b, :].rearrange("p (h t) -> p h t", h=HEADS),
                    ps[:, BANK_TK, b * TXT:(b + 1) * TXT].unsqueeze(1).broadcast_to([P, HEADS, TXT]),
                    vcol[:, bass.ds(VEC["bk"] + l, 1)],
                    hmask[:, :].unsqueeze(2).broadcast_to([P, HEADS, TXT]), ALU.add, ALU.mult).then_inc(S["tx_kbd"], 1)

            def txt_vs(l):
                dve.wait_ge(S["tx_v"], nth(l, 1, 1))
                for b in range(BATCH):
                    mm = dve.tensor_tensor(tv[:, b, :, 0:HD], ps[0:TXT, BANK_TV, b * D:(b + 1) * D].rearrange("p (h d) -> p h d", h=HEADS),
                                           bv_r[:, bass.ds(l, 1), :].rearrange("p a (h d) -> p (a h) d", h=HEADS), ALU.add)
                mm.then_inc(S["tx_vs"], 1)

            def txt_mask(l, b):
                dve.wait_ge(S["tx_score"], nth(l, BATCH, b + 1))
                dve.tensor_tensor(ts[:, b, :].rearrange("p (g h t) -> p g h t", g=2, h=HEADS // 2),
                                  ps[0:TXT, BANK_TX:BANK_TX + 2, 0:HALF].rearrange("p g (h t) -> p g h t", t=TXT),
                                  tmask[:, b, :].unsqueeze(1).unsqueeze(1).broadcast_to([TXT, 2, HEADS // 2, TXT]),
                                  ALU.add).then_inc(S["tx_masked"], 1)

            def txt_shift(l, b):
                s3 = ts[:, b, :].rearrange("p (h t) -> p h t", h=HEADS)
                dve.tensor_reduce(tnm[:, b, :], s3, AX.X, ALU.max, negate=True)
                dve.drain()
                dve.tensor_tensor(s3, s3, tnm[:, b, :].unsqueeze(2).broadcast_to([TXT, HEADS, TXT]), ALU.add).then_inc(S["tx_shift"], 1)

            def txt_context(l, b):
                dve.wait_ge(S["tx_pv"], nth(l, BATCH, b + 1))
                o = ps[0:TXT, BANK_TC, 0:HEADS * (HD + 1)].rearrange("p (h d) -> p h d", h=HEADS)
                dve.reciprocal(trs[:, b, :], o[:, :, HD])
                dve.drain()
                dve.tensor_tensor(tctx[:, b, :].rearrange("p (h d) -> p h d", h=HEADS), o[:, :, 0:HD],
                                  trs[:, b, :].unsqueeze(2).broadcast_to([TXT, HEADS, HD]), ALU.mult).then_inc(S["tx_ctx"], 1)

            def txt_residual(l, product, k):
                dve.wait_ge(S[product], nth(l, 1, 1))
                dve.wait_ge(S["tx_resid"], nth(l, 2, k))
                dve.tensor_tensor(tx[:, :, :], ps[0:TXT, BANK_TY, :].rearrange("p (b d) -> p b d", b=BATCH), tx_res[:, :, :], ALU.add)
                dve.drain()

            norm_stats(0, 1)
            with dve.Fori(0, BATCH) as t:
                dve.wait_ge(S["proj_full"], nth(t, 5, 1))
                dve.tensor_copy(xT[:, :], ps[:, BANK_XT, :]).then_inc(S["xT_ready"], 1)
                normalise(t, 1)
                tok_keys(t)
                scale_turned(t, 1, "g1", "c1")
                dve.wait_ge(S["tx_k"], nth(t, 1, 1))
                txt_kbd(t, 0)
                txt_vs(t)
                tok_vb(t)
                dve.wait_ge(S["e_loaded"], nth(t, 32, 32))
                dve.tensor_copy(w1_h[:, bass.ds(2 * t, 2), :], w1_raw[:, :, :]).then_inc(S["e_high"], 1)
                for n in range(UNITS + 2):
                    if n < UNITS:
                        tok_max(t, n)
                    dve.drain()
                    if 1 <= n <= UNITS:
                        tok_rsum(t, n - 1)
                    if n in AT_SCORES:
                        txt_mask(t, AT_SCORES.index(n))
                    if n < BATCH - 1:
                        txt_kbd(t, n + 1)
                    if n in AT_SHIFT:
                        txt_shift(t, AT_SHIFT.index(n))
                    if n in AT_VALUES:
                        txt_context(t, AT_VALUES.index(n))
                    if n == AT_OUT:
                        txt_residual(t, "tx_o", 1)
                        norm_stats(t, 2)
                    if n == AT_NORM2:
                        normalise(t, 2)
                    if n == AT_TURN2:
                        scale_turned(t, 2, "g2", "c2")
                    if n == AT_DOWN:
                        txt_residual(t, "tx_f2", 2)
                        norm_stats(t, 3)
                    if n >= 2:
                        tok_out(t, n - 2)
                dve.drain().then_inc(S["seq_tok"], 1)
                for i in range(TT):
                    dve.bn_stats(st5[:, 0, i, :], seq_at(t * TILES + i))
                dve.drain()
                for i in range(TT):
                    dve.bn_aggr(mv5[:, i, :], st5[:, 0, i, :])
                dve.drain()
                dve.tensor_copy(mv_l[:, bass.ds(t * TILES, TT), :], mv5[:, 0:TT, :]).then_inc(S["stat_tok"], 1)
            normalise(LAYERS, 1)
            dve.drain()
            dve.tensor_tensor(tx_n[:, :, :], tx_n[:, :, :], lnf_g[:, :].unsqueeze(1).broadcast_to([TXT, BATCH, D]), ALU.mult)
            dve.drain()
            dve.tensor_tensor(seq[0:TXT, TT::TILES, :], tx_n[:, :, :], lnf_b[:, :].unsqueeze(1).broadcast_to([TXT, BATCH, D]), ALU.add).then_inc(S["seq_txt"], 1)

            dve.drain()
            dve.wait_ge(S["l_wT"], 1)
            dve.tensor_copy(w_lT[:, :], banks(0, 6 * P))
            dve.tensor_copy(w_loT[:, :, :], ps[:, 2, :].rearrange("p (g n) -> p g n", g=4)).then_inc(S["l_wT_done"], 1)
            for b in range(BATCH):
                dve.bn_stats(st5[:, 0, b, :], seq[:, b * TILES + TT, :])
            dve.drain()
            for b in range(BATCH):
                op = dve.bn_aggr(mv_l[:, b * TILES + TT, :], st5[:, 0, b, :])
            op.then_inc(S["stat_tok"], 1)
            dve.memset(lz[:, :, :], 0.0)
            dve.wait_ge(S["rstd_lin"], BATCH + 1)

            def normalise5(p, s, mv, rs, done):
                for i in range(TILES):
                    k = (2 * p + s) * TILES + i
                    op = dve.tensor_scalar(xn[:, s, i, :], seq_at(k), mv[:, bass.ds(k, 1), 0], rs[:, bass.ds(k, 1)], ALU.subtract, ALU.mult)
                op.then_inc(S[done], 1)

            def la_features(p, s):
                dve.wait_ge(S["la_qk"], nth(p, 4, 2 * s + 1))
                dve.tensor_scalar(lt1[:, s, :], banks(4 * s + 2, T), 0.0, None, ALU.min).then_inc(S["la_min"], 1)
                dve.wait_ge(S["la_qk"], nth(p, 4, 2 * s + 2))
                dve.tensor_scalar(lt2[:, s, :], banks(4 * s, T), 0.0, None, ALU.min).then_inc(S["la_min"], 1)
                dve.wait_ge(S["la_exp"], nth(p, 4, 2 * s + 1))
                dve.scalar_tensor_tensor(lk[:, s, :], banks(4 * s + 2, T), 0.0, lt1[:, s, :], ALU.max, ALU.add).then_inc(S["la_feat"], 1)
                dve.wait_ge(S["la_exp"], nth(p, 4, 2 * s + 2))
                dve.scalar_tensor_tensor(lq[:, s, :], banks(4 * s, T), 0.0, lt2[:, s, :], ALU.max, ALU.add).then_inc(S["la_feat"], 1)
                dve.drain()
                dve.tensor_tensor_scan(lz[:, s, 0:T], ones[:, :], lk[:, s, :], 0.0, ALU.mult, ALU.add)
                dve.drain()
                dve.tensor_tensor(lz[:, s, 0:T], lz[:, s, 0:T], lq[:, s, :], ALU.mult).then_inc(S["la_qz"], 1)

            def la_reciprocal(p, s):
                dve.wait_ge(S["la_den"], nth(p, 2, s + 1))
                den = lden[:, s, :, :]
                dve.tensor_scalar(den, ps[:, 4 * s + 3, 0:TILES * LH].rearrange("p (t h) -> p t h", h=LH), 1e-6, None, ALU.max)
                dve.drain()
                dve.reciprocal(den, den)
                dve.drain()
                dve.tensor_copy(lrexp[:, s, :, :, :], den.unsqueeze(3).broadcast_to([P, TILES, LH, LD])).then_inc(S["la_rden"], 1)

            def la_mask(p, s, i):
                r = ROWS[i]
                dve.wait_ge(S["la_at"], nth(p, 2 * TILES, 2 * i + s + 1))
                bank = 4 * s + 2
                dve.tensor_tensor(la[0:r, s, :, 0:r].rearrange("p (g h) t -> p g h t", g=2),
                                  ps[0:r, bank:bank + 2, 0:4 * r].rearrange("p g (h t) -> p g h t", h=4),
                                  causal01[0:r, 0:r].unsqueeze(1).unsqueeze(1).broadcast_to([r, 2, 4, r]),
                                  ALU.mult).then_inc(S["la_masked"], 1)

            def la_keep_state(p, s, i):
                dve.wait_ge(S["la_state"], nth(p, 2 * TT, 2 * i + s + 1))
                dve.tensor_tensor(lsbd[:, s, :].rearrange("p (h v) -> p h v", h=LH), ps[:, 4 * s + 1, :].rearrange("p (h v) -> p h v", h=LH),
                                  hmask[:, :].unsqueeze(2).broadcast_to([P, LH, LV]), ALU.mult).then_inc(S["la_sbd"], 1)

            def la_residual(p, s, i):
                r = ROWS[i]
                dve.wait_ge(S["la_y"], nth(p, 2 * TILES, 2 * i + s + 1))
                at_ = seq[0:r, bass.ds((2 * p + s) * TILES + i, 1), :]
                dve.tensor_tensor(at_, ps[0:r, 4 * s, 0:D].unsqueeze(1), at_, ALU.add).then_inc(S["seq_tile"], 1)

            with dve.Fori(0, PAIRS) as p:
                for s in range(2):
                    normalise5(p, s, mv_l, rs_l, "la_norm")
                for s in range(2):
                    dve.wait_ge(S["la_normT"], nth(p, 2, s + 1))
                    dve.tensor_copy(sT[:, s, 0:T], banks(4 * s, T)).then_inc(S["la_hT"], 1)
                for s in range(2):
                    la_features(p, s)
                for s in range(2):
                    la_reciprocal(p, s)
                for s in range(2):
                    dve.wait_ge(S["la_rT"], nth(p, 2, s + 1))
                    dve.tensor_tensor(lq[:, s, :], banks(4 * s + 2, T), lq[:, s, :], ALU.mult).then_inc(S["la_q"], 1)
                for i in range(TILES):
                    for s in range(2):
                        la_mask(p, s, i)
                    if i >= 1:
                        for s in range(2):
                            la_residual(p, s, i - 1)
                    if i < TT:
                        for s in range(2):
                            la_keep_state(p, s, i)
                    if i >= 1:
                        dve.drain()
                        for s in range(2):
                            dve.bn_stats(st5[:, s, i - 1, :], seq_at((2 * p + s) * TILES + i - 1))
                for s in range(2):
                    la_residual(p, s, TT)
                dve.drain().then_inc(S["lin_free"], 2)
                for s in range(2):
                    dve.bn_stats(st5[:, s, TT, :], seq_at((2 * p + s) * TILES + TT))
                dve.drain()
                for s in range(2):
                    for i in range(TILES):
                        dve.bn_aggr(mv5[:, s * TILES + i, :], st5[:, s, i, :])
                dve.drain()
                dve.tensor_copy(mv_f[:, bass.ds(p * 2 * TILES, 2 * TILES), :], mv5[:, :, :]).then_inc(S["stat_h"], 1)

            dve.wait_ge(S["block_params"], 16 * (7 + E))
            units = [(i, h, s) for i in range(TILES) for h in range(FH) for s in range(2)]

            def rowmax(p, n):
                i, h, s = units[n]
                r, width = ROWS[i], min((i + 1) * P, T)
                dve.wait_ge(S["fa_s"], nth(p, FU, n + 1))
                dve.tensor_reduce(fnm[0:r, n:n + 1], banks(4 * s, width, r), AX.X, ALU.max, negate=True).then_inc(S["fa_max"], 1)

            def scale(p, n):
                i, h, s = units[n]
                r, width = ROWS[i], min((i + 1) * P, T)
                dve.wait_ge(S["fa_exp"], nth(p, FU, n + 1))
                dve.reciprocal(frs[0:r, n:n + 1], fsum[0:r, n:n + 1])
                dve.drain()
                if n >= 2:
                    dve.wait_ge(S["fa_pt"], nth(p, FU, n - 1))
                dve.tensor_scalar(fpn[0:r, s, 0:width], fp[0:r, s, 0:width], frs[0:r, n:n + 1], None, ALU.mult).then_inc(S["fa_pn"], 1)

            def copy_pT(p, n):
                i, h, s = units[n]
                r = ROWS[i]
                dve.wait_ge(S["fa_pt"], nth(p, FU, n + 1))
                if n >= 2:
                    dve.wait_ge(S["fa_o"], nth(p, FU, n - 1))
                if i < TT:
                    dve.tensor_copy(fpT[:, s, 0:(i + 1) * r], ps[:, 4 * s + 2, 0:(i + 1) * r]).then_inc(S["fa_pT_dve"], 1)
                else:
                    dve.tensor_copy(fpT[:, s, 0:TT * r], ps[:, 4 * s + 2, 0:TT * r])
                    dve.tensor_copy(fpT[0:r, s, TT * r:(TT + 1) * r], ps[0:r, 4 * s + 2, TT * r:(TT + 1) * r]).then_inc(S["fa_pT_dve"], 1)

            with dve.Fori(0, PAIRS) as p:
                dve.wait_ge(S["rstd_h"], nth(p, 1, 1))
                for s in range(2):
                    normalise5(p, s, mv_f, rs_f, "fa_xn")
                for s in range(2):
                    dve.wait_ge(S["fa_xT"], nth(p, 2, s + 1))
                    dve.tensor_scalar(sT[:, s, 0:T], banks(4 * s, T), vcol[:, VEC["fg"]:VEC["fg"] + 1],
                                      vcol[:, VEC["fc"]:VEC["fc"] + 1], ALU.mult, ALU.add).then_inc(S["fa_hT"], 1)
                for s in range(2):
                    dve.wait_ge(S["fa_qkv_sb"], nth(p, 2 * TILES, 2 * TT + s + 1))
                    dve.tensor_tensor(sq[:, s, :, :], qkv[:, s, :, 0:2 * D], qkv[:, s, :, 0:2 * D], ALU.mult)
                    dve.drain()
                    dve.tensor_reduce(ss[:, s, :, :], sq[:, s, :, :].rearrange("p t (h d) -> p t h d", d=FD), AX.X, ALU.add).then_inc(S["fa_ss"], 1)
                for s in range(2):
                    dve.wait_ge(S["fa_rs"], nth(p, 2, s + 1))
                    qk4 = qkv[:, s, :, 0:2 * D].rearrange("p t (h d) -> p t h d", d=FD)
                    dve.tensor_tensor(qk4, qk4, ssr[:, s, :, :].unsqueeze(3).broadcast_to([P, TILES, 2 * FH, FD]), ALU.mult).then_inc(S["fa_norm"], 1)
                for s in range(2):
                    dve.wait_ge(S["fa_T"], nth(p, 4, 2 * s + 1))
                    dve.tensor_scalar(fq[:, s, :], banks(4 * s, T), qkg[:, 0:1], None, ALU.mult).then_inc(S["fa_qT"], 1)
                for n in range(FU + 2):
                    if n < FU:
                        rowmax(p, n)
                    if 1 <= n <= FU:
                        scale(p, n - 1)
                    if n >= 2 and (n - 2) % 2 == 1:
                        copy_pT(p, n - 2)
                for s in range(2):
                    dve.wait_ge(S["y_done"], nth(p, 2, s + 3))
                    for cols in (bass.ds((2 * p + s) * TOK, TOK), bass.ds(BATCH * TOK + (2 * p + s) * TXT, TXT)):
                        op = dve.tensor_copy(y_h[:, cols], y_all[:, cols])
                    op.then_inc(S["y_high"], 1)

            dve.memset(lg[:, :, :], 0.0)
            dve.wait_ge(S["g_ps"], 1)
            dve.drain()
            for rows_, t0, t1 in ((P, 0, BATCH * TT), (TXT, BATCH * TT, TILES_ALL)):
                dve.tensor_tensor(lg[0:rows_, t0:t1, :], ps[0:rows_, 7, t0 * E:t1 * E].rearrange("p (t e) -> p t e", e=E),
                                  gb_r[0:rows_, :].unsqueeze(1).broadcast_to([rows_, t1 - t0, E]), ALU.add)
            dve.drain()
            dve.tensor_reduce(lgm[:, :], lg[:, :, :], AX.X, ALU.max, negate=True)
            dve.drain()
            dve.tensor_tensor(lg[:, :, :], lg[:, :, :], lgm[:, :].unsqueeze(2).broadcast_to([P, TILES_ALL, E]), ALU.add).then_inc(S["g_shift"], 1)
            dve.wait_ge(S["g_exp"], 1)
            dve.tensor_reduce(lgm[:, :], lg[:, :, :], AX.X, ALU.add)
            dve.drain()
            dve.reciprocal(lgm[:, :], lgm[:, :])
            dve.drain()
            dve.tensor_tensor(gate[:, :, :], lg[:, :, :], lgm[:, :].unsqueeze(2).broadcast_to([P, TILES_ALL, E]), ALU.mult)
            dve.drain()

            def experts(c, r, tile_at):
                def accumulate(e):
                    dve.drain()
                    dve.wait_ge(S["down"], nth(c, E, e + 1))
                    for i in range(4):
                        at_ = tile_at(i)
                        op = dve.scalar_tensor_tensor(at_, ps[0:r, 4 + e % 4, i * P:(i + 1) * P].unsqueeze(1),
                                                      gate[0:r, bass.ds(c * TT + i, 1), e], at_, ALU.mult, ALU.add)
                    op.then_inc(S["acc_done"], 1)

                dve.tensor_copy(gate_c[0:r, :, :], gate[0:r, bass.ds(c * TT, 4), :]).then_inc(S["g_chunk"], 1)
                dve.wait_ge(S["g_tps"], nth(c, 1, 1))
                dve.tensor_copy(gateT[:, 0:4 * r], ps[0:E, 4, 0:4 * r]).then_inc(S["g_T"], 1)
                dve.wait_ge(S["b2_ps"], nth(c, 1, 1))
                for i in range(4):
                    at_ = tile_at(i)
                    op = dve.tensor_tensor(at_, ps[0:r, 5, i * P:(i + 1) * P].unsqueeze(1), at_, ALU.add)
                op.then_inc(S["acc_init"], 1)
                for e in range(E):
                    accumulate(e)

            with dve.Fori(0, BATCH) as c:
                experts(c, P, lambda i: seq[:, bass.ds(c * TILES + i, 1), :])
            experts(BATCH, TXT, lambda i: seq[0:TXT, i * TILES + TT:i * TILES + TT + 1, :])

        @block.scalar
        def _(act):
            act.wait_ge(S["setup_done"], 1)

            def tok_exp(b, n):
                act.wait_ge(S["max_ready"], nth(b, UNITS, n + 1))
                if n >= 2:
                    act.wait_ge(S["probT_full"], nth(b, UNITS, n - 1))
                act.activation(prob[:, n % 2, :], ps[:, n % 2, :], ACT.Exp, bias=nmax[:, n:n + 1],
                               accum_out=psum_e[:, n:n + 1]).then_inc(S["prob_ready"], 1)

            def tok_probT(b, n):
                act.wait_ge(S["probT_full"], nth(b, UNITS, n + 1))
                act.activation(probT[:, n % 2, :], ps[:, BANK_T, :], ACT.Copy).then_inc(S["probT_ready"], 1)

            def txt_exp(l, b):
                act.wait_ge(S["tx_shift"], nth(l, BATCH, b + 1))
                act.activation(ts[:, b, :], ts[:, b, :], ACT.Exp).then_inc(S["tx_exp"], 1)

            def txt_pT(l, b, g):
                act.wait_ge(S["tx_pt"], nth(l, 2 * BATCH, 2 * b + g + 1))
                act.activation(tpT[:, b, g * HALF:(g + 1) * HALF], ps[0:TXT, BANK_TPT, 0:HALF], ACT.Copy).then_inc(S["tx_pT"], 1)

            def txt_gelu(l):
                for j in range(KT):
                    act.wait_ge(S["tx_f1"], nth(l, KT, j + 1))
                    act.activation(gact[:, j, :], ps[:, BANKS_UP[j], 0:SEQ4], ACT.Gelu,
                                   bias=vcol[:, bass.ds(VEC["b1"] + l * KT + j, 1)]).then_inc(S["tx_g"], 1)

            with act.Fori(0, BATCH) as t:
                act.wait_ge(S["proj_full"], nth(t, 5, 2))
                act.activation(qT[:, :], ps[:, BANK_Q, :], ACT.Copy, scale=DQ ** -0.5).then_inc(S["q_ready"], 1)
                act.wait_ge(S["tx_q"], nth(t, 1, 1))
                act.activation(tqT[:, :], ps[:, BANK_TQ, 0:SEQ4], ACT.Identity, bias=bq4[:, bass.ds(t, 1)], scale=HD ** -0.5).then_inc(S["tx_qs"], 1)
                act.wait_ge(S["proj_full"], nth(t, 5, 4))
                act.activation(v_tok[:, 0:2, :], ps[:, BANK_V, :], ACT.Copy).then_inc(S["va_ready"], 1)
                for n in range(UNITS + 2):
                    if n < UNITS:
                        tok_exp(t, n)
                    if n in AT_SHIFT:
                        txt_exp(t, AT_SHIFT.index(n))
                    for b in range(BATCH):
                        for g in range(2):
                            if n == AT_TURN[b][g]:
                                txt_pT(t, b, g)
                    if n == AT_CTX_TURN:
                        act.wait_ge(S["tx_ct"], nth(t, 1, 1))
                        act.activation(cT[:, :], ps[:, BANK_TX, 0:SEQ4], ACT.Copy).then_inc(S["tx_cT"], 1)
                    if 1 <= n <= UNITS:
                        tok_probT(t, n - 1)
                    if n == AT_UP:
                        txt_gelu(t)

            with act.Fori(0, PAIRS) as p:
                def exps(s):
                    for k, part in enumerate((lt1, lt2)):
                        act.wait_ge(S["la_min"], nth(p, 4, 2 * s + k + 1))
                        act.activation(part[:, s, :], part[:, s, :], ACT.Exp).then_inc(S["la_exp"], 1)

                def values(s, i):
                    act.wait_ge(S["la_vfull"], nth(p, 2 * TILES, TILES * s + i + 1))
                    act.activation(lv[:, s, i, :], ps[:, 4 * s + i % 2, :], ACT.Copy).then_inc(S["la_vdone"], 1)

                exps(0)
                for i in range(2):
                    values(0, i)
                exps(1)
                for s in range(2):
                    for i in range(2 if s == 0 else 0, TILES):
                        values(s, i)
                    act.wait_ge(S["la_ktps"], nth(p, 2, s + 1))
                    act.activation(lktok[:, s, :, :], ps[:, 4 * s + 2, :].rearrange("p (t d) -> p t d", t=TT), ACT.Copy).then_inc(S["la_ktok"], 1)
                for i in range(TILES):
                    for s in range(2):
                        r = ROWS[i]
                        act.wait_ge(S["la_ot"], nth(p, 2 * TILES, 2 * i + s + 1))
                        act.activation(lo[:, s, :, 0:r], ps[:, 4 * s, 0:4 * r].rearrange("p (g t) -> p g t", g=4), ACT.Copy).then_inc(S["la_lo"], 1)

            act.sem_inc(S["y_done"], 2)
            units = [(i, h, s) for i in range(TILES) for h in range(FH) for s in range(2)]

            def exp(p, n):
                i, h, s = units[n]
                r, width = ROWS[i], min((i + 1) * P, T)
                act.wait_ge(S["fa_max"], nth(p, FU, n + 1))
                if n >= 2:
                    act.wait_ge(S["fa_pn"], nth(p, FU, n - 1))
                act.activation(fp[0:r, s, 0:width], banks(4 * s, width, r), ACT.Exp, bias=fnm[0:r, n:n + 1],
                               accum_out=fsum[0:r, n:n + 1]).then_inc(S["fa_exp"], 1)

            def copy_pT(p, n):
                i, h, s = units[n]
                r = ROWS[i]
                act.wait_ge(S["fa_pt"], nth(p, FU, n + 1))
                if n >= 2:
                    act.wait_ge(S["fa_o"], nth(p, FU, n - 1))
                if i < TT:
                    act.activation(fpT[:, s, 0:(i + 1) * r], ps[:, 4 * s + 2, 0:(i + 1) * r], ACT.Copy).then_inc(S["fa_pT_act"], 1)
                else:
                    act.activation(fpT[:, s, 0:TT * r], ps[:, 4 * s + 2, 0:TT * r], ACT.Copy)
                    act.activation(fpT[0:r, s, TT * r:(TT + 1) * r], ps[0:r, 4 * s + 2, TT * r:(TT + 1) * r], ACT.Copy).then_inc(S["fa_pT_act"], 1)

            def copy_oT(p, n):
                i, h, s = units[n]
                if h == FH - 1:
                    r = ROWS[i]
                    act.wait_ge(S["fa_o"], nth(p, FU, n + 1))
                    act.activation(foT[:, s, i * P:i * P + r], ps[:, 4 * s + 3, 0:r], ACT.Copy).then_inc(S["fa_oT"], 1)

            with act.Fori(0, PAIRS) as p:
                for i in range(TILES):
                    for s in range(2):
                        act.wait_ge(S["fa_qkv"], nth(p, 2 * TILES, 2 * i + s + 1))
                        act.activation(qkv[:, s, i, :], ps[:, 4 * s + 2 + i % 2, 0:3 * D], ACT.Copy).then_inc(S["fa_qkv_sb"], 1)
                for s in range(2):
                    act.wait_ge(S["fa_T"], nth(p, 4, 2 * s + 2))
                    act.activation(fk[:, s, :], banks(4 * s + 2, T), ACT.Copy).then_inc(S["fa_kT"], 1)
                for n in range(FU + 4):
                    if n < FU:
                        exp(p, n)
                    if 2 <= n < FU + 2 and (n - 2) % 2 == 0:
                        copy_pT(p, n - 2)
                    if n >= 4:
                        copy_oT(p, n - 4)
                for s in range(2):
                    act.wait_ge(S["y_ps"], nth(p, 2, s + 1))
                    act.activation(y_all[:, bass.ds((2 * p + s) * TOK, TOK)], ps[:, 4 * s, :], ACT.Copy)
                    act.activation(y_all[:, bass.ds(BATCH * TOK + (2 * p + s) * TXT, TXT)], ps[:, 4 * s + 1, 0:TXT], ACT.Copy).then_inc(S["y_done"], 1)

            act.wait_ge(S["g_shift"], 1)
            act.activation(lg[:, :, :], lg[:, :, :], ACT.Exp).then_inc(S["g_exp"], 1)

            def experts(c, r):
                for n in range(E * EK):
                    e, f = divmod(n, EK)
                    act.wait_ge(S["up"], nth(c, E * EK, n + 1))
                    if f == 0 and e >= 2:
                        act.wait_ge(S["down"], nth(c, E, e - 1))
                    act.activation(hid[:, e % 2, f, 0:4 * r], ps[:, n % 4, 0:4 * r], ACT.Gelu_apprx_tanh,
                                   bias=vcol[:, VEC["eb"] + n:VEC["eb"] + n + 1]).then_inc(S["up_done"], 1)

            with act.Fori(0, BATCH) as c:
                experts(c, P)
            experts(BATCH, TXT)


N_PARAMS = 2 + 6 + 2 + 2 + 4 + 1 + BATCH + 5

def kernel(**inputs):
    import numpy as np
    import concourse.bacc as bacc
    from concourse.bass_utils import run_bass_kernel_spmd

    nc = bacc.Bacc("TRN2", target_bir_lowering=False, num_devices=1)
    arrays, aps = {}, {}
    for name, value in inputs.items():
        a = np.ascontiguousarray(value)
        arrays["in_" + name] = a
        aps[name] = nc.dram_tensor("in_" + name, a.shape, mybir.dt.from_np(a.dtype), kind="ExternalInput").ap()
    out = nc.dram_tensor("out", (BATCH, T, D), F32, kind="ExternalOutput").ap()
    fusion_kernel(nc, aps, out)
    r = run_bass_kernel_spmd(nc, [arrays], core_ids=[0])
    return r.results[0]["out"]
```

```python
from contextlib import ExitStack

import concourse.bass as bass
from concourse import mybir

F32 = mybir.dt.float32
F32R = mybir.dt.float32r
BF16 = mybir.dt.bfloat16
I32 = mybir.dt.int32
U32 = mybir.dt.uint32
ALU = mybir.AluOpType
ACT = mybir.ActivationFunctionType
AX = mybir.AxisListType

P = 128
BATCH, TOK, CH = 4, 512, 64
TXT = 77
D = 2 * CH
TT = TOK // P
TILES = TT + 1
T = TOK + TXT
ROWS = [P] * TT + [TXT]
NEG = -1.0e30

DQ = CH // 8
UNITS = 4 * TT

LAYERS, HEADS, HD, FF = 4, 8, 16, 512
SEQ4 = BATCH * TXT
KT = FF // P

LH, LD, LV = 8, 16, 64
LVA = LV + 1
FH, FD = 2, 64
E, EF = 8, 512
EK = EF // P

PAIRS = BATCH // 2
POS = BATCH * T
TILES_ALL = BATCH * TILES
TXT_ROWS = [min(P, BATCH * TXT - r) for r in range(0, BATCH * TXT, P)]
GT = BATCH * TT + len(TXT_ROWS)
TXT_PIECES = []
for _b in range(BATCH):
    _r = 0
    while _r < TXT:
        _tile, _p = divmod(_b * TXT + _r, P)
        _n = min(TXT - _r, P - _p)
        TXT_PIECES.append((_b, _r, _tile, _p, _n))
        _r += _n


def fusion_kernel(nc, A, out):
    ctx = ExitStack()
    with ctx:
        def sb(name, shape, dt=F32):
            return ctx.enter_context(nc.sbuf_tensor(name, shape, dt))

        def sem(name):
            return ctx.enter_context(nc.semaphore(name))

        TP = TILES * P
        vec_txt = [("bq", LAYERS), ("bk", LAYERS), ("g1", LAYERS), ("c1", LAYERS), ("g2", LAYERS),
                   ("c2", LAYERS), ("b1", LAYERS * KT)]
        vec_last = [("eb", E * EK), ("fg", 1), ("fc", 1), ("qn", 1), ("kn", 1)]
        VEC, NVEC = {}, []
        for names in (vec_txt, vec_last):
            at = 0
            for n, c in names:
                VEC[n] = at
                at += c
            NVEC.append(at)
        seq = sb("seq", [P, BATCH * TILES, D])
        ident = sb("ident", [P, P])
        neghalf = sb("neghalf", [P, 4 * TILES])
        eps = sb("eps", [P, TILES_ALL])
        tiny = sb("tiny", [P, 4 * TILES])
        mix = sb("mix", [P, 2])
        hmask = sb("hmask", [P, HEADS])
        vrow = sb("vrow", [NVEC[0], D])
        vcol = sb("vcol", [P, NVEC[0]])
        vrow_f = sb("vrow_f", [NVEC[1], D])
        vcol_f = sb("vcol_f", [P, NVEC[1]])
        bq4 = sb("bq4", [P, LAYERS])
        qkg = sb("qkg", [P, 1])
        mv_l = sb("mv_l", [P, TILES_ALL, 2])
        va_l = sb("va_l", [P, TILES_ALL])
        rs_l = sb("rs_l", [P, TILES_ALL])
        nb_l = sb("nb_l", [P, TILES_ALL])
        mv_f = sb("mv_f", [P, TILES_ALL, 2])
        va_f = sb("va_f", [P, TILES_ALL])
        vb_f = sb("vb_f", [P, TILES_ALL])
        rs_f = sb("rs_f", [P, TILES_ALL])
        nb_f = sb("nb_f", [P, TILES_ALL])
        minus = sb("minus", [P, 2 * TILES])
        st5 = sb("st5", [P, 2, TILES, 6])
        mv5 = sb("mv5", [P, 2 * TILES, 2])
        xn = sb("xn", [P, 2, TILES, D])
        sT = sb("sT", [P, 2, TP])
        w_lraw = sb("w_lraw", [P, 6, D])
        w_loraw = sb("w_loraw", [P, LH * LV])
        w_lT = sb("w_lT", [P, 6 * P])
        w_loT = sb("w_loT", [P, 4, D])
        ones = sb("ones", [P, T])
        causal01 = sb("causal01", [P, P])
        w_fqkv = sb("w_fqkv", [P, 3 * D])
        w_fo = sb("w_fo", [P, D])
        w_gate = sb("w_gate", [P, E])
        gb_r = sb("gb_r", [P, E])
        b2_e = sb("b2_e", [2 * E, D])
        identb = sb("identb", [P, P], BF16)
        causalb = sb("causalb", [P, P], BF16)
        w1_h = sb("w1_h", [P, E, EF], F32R)
        w1_l = sb("w1_l", [P, E, EF], F32R)
        w2_e = sb("w2_e", [P, E * EK, D])
        lg = sb("lg", [P, GT, E])
        lgm = sb("lgm", [P, GT])
        gate = sb("gate", [P, GT, E])
        txt_acc = sb("txt_acc", [P, len(TXT_ROWS), D])

        first_half = ExitStack()

        def sb1(name, shape, dt=F32):
            return first_half.enter_context(nc.sbuf_tensor(name, shape, dt))

        x_in = sb1("x_in", [P, TT, D])
        w_qk_in = sb1("w_qk_in", [P, 2, 4, DQ])
        w_qk = sb1("w_qk", [P, 2, 4, 32])
        low_sel = sb1("low_sel", [P, 2, 4])
        low_rows = sb1("low_rows", [P, 2])
        q_high = sb1("q_high", [P, TOK], F32R)
        k_high = sb1("k_high", [P, TOK], F32R)
        w_tv = sb1("w_tv", [P, 4 * CH])
        xT = sb1("xT", [P, TOK])
        qT = sb1("qT", [P, TOK], F32R)
        kT = sb1("kT", [P, TOK], F32R)
        v_tok = sb1("v_tok", [P, TT, 4 * CH])
        prob = sb1("prob", [P, 2, TOK])
        probT = sb1("probT", [P, 2, TOK])
        nmax = sb1("nmax", [P, UNITS])
        psum_e = sb1("psum_e", [P, UNITS])
        rsum = sb1("rsum", [P, UNITS])
        intra = sb1("intra", [P, 2, CH])
        tx = sb1("tx", [TXT, BATCH, D])
        tx_res = sb1("tx_res", [TXT, BATCH, D])
        tx_n = sb1("tx_n", [TXT, BATCH, D])
        tx_st = sb1("tx_st", [TXT, BATCH, 6])
        tx_mv = sb1("tx_mv", [TXT, BATCH, 2])
        tx_ve = sb1("tx_ve", [TXT, BATCH])
        tx_rs = sb1("tx_rs", [TXT, BATCH])
        tok_idx = sb1("tok_idx", [TXT, BATCH], I32)
        pos = sb1("pos", [TXT, D])
        padrow = sb1("padrow", [TXT, BATCH, TXT])
        causal_t = sb1("causal_t", [TXT, TXT])
        tmask = sb1("tmask", [TXT, BATCH, TXT], BF16)
        w_q = sb1("w_q", [D, D])
        w_k = sb1("w_k", [D, D])
        w_v = sb1("w_v", [D, D])
        w_o = sb1("w_o", [D, D])
        w_1 = sb1("w_1", [D, FF])
        w_2 = sb1("w_2", [P, KT, D])
        bv_r = sb1("bv_r", [TXT, LAYERS, D])
        bo_r = sb1("bo_r", [TXT, LAYERS, D])
        b2_r = sb1("b2_r", [TXT, LAYERS, D])
        lnf_g = sb1("lnf_g", [TXT, D])
        lnf_b = sb1("lnf_b", [TXT, D])
        hT = sb1("hT", [P, SEQ4])
        tqT = sb1("tqT", [P, SEQ4])
        kbd = sb1("kbd", [P, BATCH, HEADS * TXT])
        tv = sb1("tv", [TXT, BATCH, HEADS, HD + 1])
        ts = sb1("ts", [TXT, BATCH, HEADS * TXT])
        tpT = sb1("tpT", [TXT, BATCH, HEADS * TXT])
        tnm = sb1("tnm", [TXT, BATCH, HEADS])
        trs = sb1("trs", [TXT, BATCH, HEADS])
        tctx = sb1("tctx", [TXT, BATCH, D])
        cT = sb1("cT", [P, SEQ4])
        gact = sb1("gact", [P, KT, SEQ4])
        w1_raw = sb1("w1_raw", [P, 2, EF])
        first_half.close()

        y_all = sb("y_all", [P, POS])
        y_h = sb("y_h", [P, POS], F32R)
        y_l = sb("y_l", [P, POS], F32R)

        linear_part = ExitStack()

        def sb2(name, shape, dt=F32):
            return linear_part.enter_context(nc.sbuf_tensor(name, shape, dt))

        lt1 = sb2("lt1", [P, 2, T])
        lt2 = sb2("lt2", [P, 2, T])
        lz = sb2("lz", [P, 2, TP])
        lq = sb2("lq", [P, 2, T])
        lk = sb2("lk", [P, 2, T])
        lv = sb2("lv", [P, 2, TILES, LH * LV])
        lktok = sb2("lktok", [P, 2, TT, P])
        lden = sb2("lden", [P, 2, TILES, LH])
        lrexp = sb2("lrexp", [P, 2, TILES, LH, LD])
        lqbd = sb2("lqbd", [P, 2, LH, P])
        la = sb2("la", [P, 2, LH, P])
        lo = sb2("lo", [P, 2, 4, P])
        lsbd = sb2("lsbd", [P, 2, LH * LV])
        linear_part.close()

        gate_parts = sb("gate_parts", [P, GT, 2, E], F32R)
        w2_h = sb("w2_h", [P, E * EK, D], F32R)
        w2_l = sb("w2_l", [P, E * EK, D], F32R)
        gate_sel = sb("gate_sel", [2 * E, E, P], F32R)

        attention_part = ExitStack()

        def sb3(name, shape, dt=F32):
            return attention_part.enter_context(nc.sbuf_tensor(name, shape, dt))

        CHUNKS = [(0, 3), (3, TILES)]
        BANK_LQ, BANK_LTXT, BANK_LK, BANK_LV = 0, 1, 2, 3
        COL_LK, COL_LQ = P, 2 * P
        TILE_ORDER = [3, 4, 2, 1, 0]
        FU = 2 * FH * TILES
        qkv = sb3("qkv", [P, 2, TILES, 3 * D])
        sq = sb3("sq", [P, 2, TILES, 2 * D])
        ss = sb3("ss", [P, 2, TILES, 2 * FH])
        ssr = sb3("ssr", [P, 2, TILES, 2 * FH])
        fq = sb3("fq", [P, 2, T])
        fk = sb3("fk", [P, 2, T])
        fp = sb3("fp", [P, 2, T])
        fpn = sb3("fpn", [P, 2, T])
        fpT = sb3("fpT", [P, 2, 512])
        fnm = sb3("fnm", [P, FU])
        fsum = sb3("fsum", [P, FU])
        frs = sb3("frs", [P, FU])
        foT = sb3("foT", [P, 2, T])
        attention_part.close()

        hid = sb("hid", [P, 4, TOK])
        hid_h = sb("hid_h", [P, 2, EK, TOK], F32R)
        hid_l = sb("hid_l", [P, 2, EK, TOK], F32R)
        gated = sb("gated", [P, 2, TOK])
        acc = sb("acc", [P, TOK])
        gateT = sb("gateT", [2 * E, TOK], F32R)
        gate_c = sb("gate_c", [P, 4, 2 * E])

        ps = ctx.enter_context(nc.psum_tensor("ps", [P, 8, 512], F32))
        psf = ps[:, :, :].rearrange("p b n -> p (b n)")

        def banks(first, width, rows_=P):
            return psf[0:rows_, first * 512:first * 512 + width]

        S = {}
        for n in ("""const_pool x_loaded qk_weights qk_repeated qk_high params txt_ids txt_embed params_later setup_psum setup_done
                  proj_full xT_ready q_ready k_ready va_ready vb_ready
                  score_full max_ready prob_ready probT_full probT_ready out_full out_done
                  wq_loaded wk_loaded wv_loaded wo_loaded w1_loaded w2_loaded
                  tx_stat tx_rstd tx_resid tx_norm tx_normT tx_hT tx_k tx_q tx_v tx_kbd tx_qs tx_vs
                  tx_score tx_shift tx_exp tx_pt tx_pT tx_pv tx_ctx tx_ct tx_cT tx_o
                  tx_f1 tx_g tx_f2 seq_tok
                  block_params l_weights e_loaded e_high e_split l_wT l_wT_done
                  stat_tok rstd_lin stat_h rstd_h
                  la_norm la_normT la_hT la_qk la_min la_exp la_feat la_vfull la_vdone la_qz la_den la_rden la_rT la_q
                  la_ktps la_ktok la_qbd la_at la_masked la_ot la_lo la_state la_sbd la_y seq_tile lin_free
                  fa_xn fa_xT fa_hT fa_qkv fa_qkv_sb fa_ss fa_rs fa_norm fa_T fa_qT fa_kT fa_s fa_max fa_exp fa_pn
                  fa_pt fa_pT_act fa_pT_dve fa_o fa_oT y_ps y_done y_high y_split
                  g_ps g_shift g_exp g_chunk g_tps g_T b2_ps acc_init txt_moved w2_split
                  up up_done hid_split gate_ps down acc_used acc_done y_turned chunk_done stored""").split():
            S[n] = sem(n)

        AT_NORM1, AT_TURN1, AT_PROJECT = 1, 2, 3
        AT_SCORES = [4, 5, 6, 7]
        AT_TURN = [5, 6, 7, 8]
        AT_VALUES = [6, 7, 8, 9]
        AT_CTX_TURN, AT_OUT, AT_NORM2, AT_TURN2, AT_UP, AT_DOWN = 10, 11, 12, 15, 16, 17
        AT_SPLIT = 13
        HALF = HEADS * TXT // 2
        BANK_XT, BANK_Q, BANK_K, BANK_V = 0, 1, 0, 2
        BANK_S, BANK_T, BANK_O = 0, 2, 3
        BANK_TX = 4
        BANK_TV, BANK_TQ, BANK_TK = 5, 6, 7
        BANK_TY, BANK_TPT, BANK_TC = 5, 6, 7
        BANKS_UP = [5, 6, 7, 4]

        block = ctx.enter_context(nc.Block())

        def nth(turn, per_turn, k):
            return turn * per_turn + k

        def add_bias(pool, rows_, l):
            pool.tensor_tensor(tx_res[:, :, :], tx[:, :, :],
                               rows_[:, bass.ds(l, 1), :].broadcast_to([TXT, BATCH, D]), ALU.add).then_inc(S["tx_resid"], 1)

        @block.sync
        def _(sp):
            tokw = [("w1", 0, 0), ("w4", 0, 1), ("w7", 1, 2), ("w10", 1, 3)]
            tokk = [("w2", 0, 0), ("w5", 1, 1), ("w8", 1, 2), ("w11", 0, 3)]
            tokv = [("w3", 0, 0), ("w6", 1, 1), ("w9", 1, 2), ("w12", 0, 3)]
            sp.dma_start(x_in[:, :, :], A["x"][0].rearrange("(t p) c s -> p t (c s)", p=P)).then_inc(S["x_loaded"], 16)
            sp.dma_start(tok_idx[:, :], A["x_txt"].rearrange("b s -> s b"), allow_slow_non_contiguous=True).then_inc(S["txt_ids"], 16)
            sp.wait_ge(S["const_pool"], 1)
            for name, chan, a in tokw:
                sp.dma_start(w_qk_in[chan:D:2, 0, a, :], A[f"L0_tok_{name}"]).then_inc(S["qk_weights"], 16)
            for name, chan, a in tokk:
                sp.dma_start(w_qk_in[chan:D:2, 1, a, :], A[f"L0_tok_{name}"]).then_inc(S["qk_weights"], 16)
            for name, chan, a in tokv:
                sp.dma_start(w_tv[chan:D:2, CH * a:CH * (a + 1)], A[f"L0_tok_{name}"]).then_inc(S["qk_weights"], 16)
            def param(dst, src):
                sp.dma_start(dst, src).then_inc(S["params"], 16)
            param(mix[:, 0:1], A["L0_tok_alpha"].partition_broadcast(P))
            param(mix[:, 1:2], A["L0_tok_gamma"].partition_broadcast(P))
            for n, src in (("bq", "txt_bq"), ("bk", "txt_bk"), ("g1", "txt_ln1_g"), ("c1", "txt_ln1_b"),
                           ("g2", "txt_ln2_g"), ("c2", "txt_ln2_b")):
                param(vrow[VEC[n]:VEC[n] + LAYERS, :], A[f"L0_{src}"])
            param(vrow[VEC["b1"]:VEC["b1"] + LAYERS * KT, :], A["L0_txt_b1"].rearrange("l (j p) -> (l j) p", p=P))
            param(pos[:, :], A["L0_txt_pos_emb"][0:TXT, :])
            param(padrow[:, :, :], A["mask_BS_f1_0"].partition_broadcast(TXT))
            def later(dst, src):
                sp.dma_start(dst, src).then_inc(S["params_later"], 16)
            later(bv_r[:, :, :], A["L0_txt_bv"].partition_broadcast(TXT))
            later(bo_r[:, :, :], A["L0_txt_bo"].partition_broadcast(TXT))
            later(b2_r[:, :, :], A["L0_txt_b2"].partition_broadcast(TXT))
            later(lnf_g[:, :], A["L0_txt_lnf_g"].partition_broadcast(TXT))
            later(lnf_b[:, :], A["L0_txt_lnf_b"].partition_broadcast(TXT))

            def layer_weights(l, first=False):
                for dst, src, loaded, used, per in (
                        (w_k[:, :], "Wk", "wk_loaded", "tx_k", 1),
                        (w_q[:, :], "Wq", "wq_loaded", "tx_q", 1),
                        (w_v[:, :], "Wv", "wv_loaded", "tx_v", 1),
                        (w_o[:, :], "Wo", "wo_loaded", "tx_o", 1),
                        (w_1[:, :], "W1", "w1_loaded", "tx_f1", KT),
                        (w_2[:, :, :], "W2", "w2_loaded", "tx_f2", 1)):
                    if not first:
                        sp.wait_ge(S[used], l * per)
                    t = A[f"L0_txt_{src}"]
                    s = t[l, :, :]
                    if src == "W2":
                        s = s.rearrange("(j p) n -> p j n", p=P)
                    sp.dma_start(dst, s).then_inc(S[loaded], 16)

            layer_weights(0, first=True)
            def expert_weights(t):
                for k in range(2):
                    sp.dma_start(w1_raw[:, k, :], A["L0_ffn_W1"][2 * t + k, :, :]).then_inc(S["e_loaded"], 16)

            expert_weights(0)
            with sp.Fori(1, BATCH) as b:
                sp.wait_ge(S["proj_full"], nth(b, 5, -4))
                sp.dma_start(x_in[:, :, :], A["x"][b, :, :, :].rearrange("(t p) c s -> p t (c s)", p=P)).then_inc(S["x_loaded"], 16)
                layer_weights(b)
                sp.wait_ge(S["e_split"], b)
                expert_weights(b)

            def load(signal, dst, src):
                sp.dma_start(dst, src).then_inc(S[signal], 16)
            load("l_weights", vrow_f[VEC["eb"]:VEC["eb"] + E * EK, :], A["L0_ffn_b1"].rearrange("e (j p) -> (e j) p", p=P))
            load("l_weights", vrow_f[VEC["fg"]:VEC["fg"] + 1, :], A["L0_ffn_ln_g"].unsqueeze(0))
            load("l_weights", vrow_f[VEC["fc"]:VEC["fc"] + 1, :], A["L0_ffn_ln_b"].unsqueeze(0))
            for h in range(FH):
                load("l_weights", vrow_f[VEC["qn"]:VEC["qn"] + 1, h * FD:(h + 1) * FD], A["L0_ffn_qn_g"].unsqueeze(0))
                load("l_weights", vrow_f[VEC["kn"]:VEC["kn"] + 1, h * FD:(h + 1) * FD], A["L0_ffn_kn_g"].unsqueeze(0))
            for k, n in enumerate(("q", "k")):
                load("l_weights", w_lraw[:, k, :], A[f"L0_attn_W_{n}"])
            load("l_weights", w_lraw[:, 2:6, :], A["L0_attn_W_v"].rearrange("(j p) n -> p j n", p=P))
            load("l_weights", w_loraw[:, :], A["L0_attn_W_out"])
            for k, n in enumerate(("q", "k", "v")):
                load("block_params", w_fqkv[:, k * D:(k + 1) * D], A[f"L0_ffn_W{n}"])
            for e in range(E):
                load("block_params", w2_e[:, e * EK:(e + 1) * EK, :], A["L0_ffn_W2"][e].rearrange("(j p) n -> p j n", p=P))
            load("block_params", w_fo[:, :], A["L0_ffn_Wo"])
            load("block_params", w_gate[:, :], A["L0_ffn_gate_W"])
            load("block_params", gb_r[:, :], A["L0_ffn_gate_b"].partition_broadcast(P))
            for k in range(2):
                load("block_params", b2_e[k * E:(k + 1) * E, :], A["L0_ffn_b2"])
            sp.wait_ge(S["lin_free"], BATCH + 2)
            for b, r0, tile_, p0, n in TXT_PIECES:
                sp.dma_start(txt_acc[p0:p0 + n, tile_, :], seq[r0:r0 + n, b * TILES + TT, :]).then_inc(S["txt_moved"], 16)

            for b in range(BATCH):
                sp.wait_ge(S["chunk_done"], b + 1)
                sp.dma_start(out[b, 0:TOK, :].rearrange("(t p) c -> p t c", p=P), seq[:, TILES * b:TILES * b + TT, :]).then_inc(S["stored"], 16)
            sp.wait_ge(S["chunk_done"], BATCH + 1)
            for b, r0, tile_, p0, n in TXT_PIECES:
                sp.dma_start(out[b, TOK + r0:TOK + r0 + n, :], txt_acc[p0:p0 + n, tile_, :]).then_inc(S["stored"], 16)
            sp.wait_ge(S["stored"], 16 * (BATCH + len(TXT_PIECES)))

        @block.gpsimd
        def _(pool):
            pool.memset(w_qk_in[:, :, :, :], 0.0)
            pool.memset(w_tv[:, :], 0.0)
            pool.memset(ident[:, :], 0.0)
            pool.drain().then_inc(S["const_pool"], 1)
            pool.affine_select(out=ident[:, :], in_=ident[:, :], compare_op=ALU.not_equal, fill=1.0,
                               base=0, pattern=[[-1, P]], channel_multiplier=1)
            pool.memset(w_qk[:, :, :, :], 0.0)
            pool.memset(low_sel[:, :, :], -1.0)
            pool.drain()
            for k, low in enumerate((2 * DQ, DQ)):
                pool.affine_select(out=low_sel[:, k, :], in_=low_sel[:, k, :], compare_op=ALU.is_ge, fill=0.0,
                                   base=-low, pattern=[[-32, 4]], channel_multiplier=1)
            pool.drain()
            for k, low in enumerate((2 * DQ, DQ)):
                pool.affine_select(out=low_sel[:, k, :], in_=low_sel[:, k, :], compare_op=ALU.is_gt, fill=0.0,
                                   base=low + DQ, pattern=[[32, 4]], channel_multiplier=-1)
            pool.drain().then_inc(S["const_pool"], 1)
            pool.memset(neghalf[:, :], -0.5)
            pool.memset(eps[:, :], 1e-5)
            pool.memset(tiny[:, :], 1e-12)
            pool.memset(minus[:, :], -1.0)
            pool.memset(hmask[:, :], 1.0)
            pool.memset(causal_t[:, :], 0.0)
            pool.memset(identb[:, :], 0.0)
            pool.memset(causalb[:, :], 0.0)
            pool.wait_ge(S["txt_ids"], 16)
            for b in range(BATCH):
                pool.indirect_dma_start(
                    out=tx[:, b, :], out_offset=None, in_=A["L0_txt_item_emb"],
                    in_offset=bass.IndirectOffsetOnAxis(ap=tok_idx[:, b:b + 1].bitcast(U32), axis=0),
                ).then_inc(S["txt_embed"], 16)
            pool.memset(ones[:, :], 1.0)
            pool.memset(causal01[:, :], 1.0)
            pool.memset(sT[:, :, :], 0.0)
            pool.drain()
            pool.affine_select(out=causal_t[:, :], in_=causal_t[:, :], compare_op=ALU.is_ge, fill=NEG,
                               base=0, pattern=[[-1, TXT]], channel_multiplier=1)
            pool.affine_select(out=identb[:, :], in_=identb[:, :], compare_op=ALU.not_equal, fill=1.0,
                               base=0, pattern=[[-1, P]], channel_multiplier=1)
            pool.affine_select(out=causalb[:, :], in_=causalb[:, :], compare_op=ALU.is_ge, fill=NEG,
                               base=0, pattern=[[-1, P]], channel_multiplier=1)
            pool.affine_select(out=causal01[:, :], in_=causal01[:, :], compare_op=ALU.is_ge, fill=0.0,
                               base=0, pattern=[[1, P]], channel_multiplier=-1)
            pool.affine_select(out=hmask[:, :], in_=hmask[:, :], compare_op=ALU.is_ge, fill=0.0,
                               base=0, pattern=[[-HD, HEADS]], channel_multiplier=1)
            pool.drain()
            pool.affine_select(out=hmask[:, :], in_=hmask[:, :], compare_op=ALU.is_gt, fill=0.0,
                               base=HD, pattern=[[HD, HEADS]], channel_multiplier=-1)
            pool.drain().then_inc(S["const_pool"], 1)

            def rstd_txt(turn, k):
                pool.wait_ge(S["tx_stat"], nth(turn, 2, k))
                pool.tensor_tensor(tx_ve[:, :], tx_mv[:, :, 1], eps[0:TXT, 0:BATCH], ALU.add)
                pool.drain()
                pool.tensor_tensor(tx_rs[:, :], tx_ve[:, :], neghalf[0:TXT, 0:BATCH], ALU.pow).then_inc(S["tx_rstd"], 1)

            def deviations(tiles, n):
                pool.tensor_tensor(va_l[:, tiles], mv_l[:, tiles, 1], eps[:, 0:n], ALU.add)
                pool.tensor_tensor(nb_l[:, tiles], mv_l[:, tiles, 0], minus[:, 0:n], ALU.mult)
                pool.drain()
                pool.tensor_tensor(rs_l[:, tiles], va_l[:, tiles], neghalf[:, 0:n], ALU.pow)
                pool.drain()
                pool.tensor_tensor(nb_l[:, tiles], nb_l[:, tiles], rs_l[:, tiles], ALU.mult).then_inc(S["rstd_lin"], 1)

            pool.wait_ge(S["setup_done"], 1)
            pool.wait_ge(S["params_later"], 16 * 5)
            rstd_txt(0, 1)
            with pool.Fori(0, LAYERS) as l:
                add_bias(pool, bo_r, l)
                rstd_txt(l, 2)
                add_bias(pool, b2_r, l)
                pool.wait_ge(S["e_high"], nth(l, 1, 1))
                experts = bass.ds(2 * l, 2)
                pool.tensor_tensor(w1_l[:, experts, :], w1_raw[:, :, :], w1_h[:, experts, :].bitcast(F32), ALU.subtract).then_inc(S["e_split"], 1)
                pool.wait_ge(S["stat_tok"], nth(l, 1, 1))
                tiles = bass.ds(l * TILES, TT)
                deviations(tiles, TT)
                rstd_txt(l, 3)
            pool.wait_ge(S["stat_tok"], BATCH + 1)
            deviations(slice(TT, TILES_ALL, TILES), BATCH)


            with pool.Fori(0, PAIRS) as p:
                for i in range(TILES):
                    for s in range(2):
                        if i == 0:
                            pool.wait_ge(S["la_q"], nth(p, 2, s + 1))
                        else:
                            pool.wait_ge(S["la_at"], nth(p, 2 * TILES, 2 * i + s - 1))
                        r = ROWS[i]
                        pool.tensor_tensor(lqbd[:, s, :, 0:r], lq[:, s, i * P:i * P + r].unsqueeze(1).broadcast_to([P, LH, r]),
                                           hmask[:, :].unsqueeze(2).broadcast_to([P, LH, r]), ALU.mult).then_inc(S["la_qbd"], 1)
                pool.wait_ge(S["stat_h"], nth(p, 1, 1))
                tiles = bass.ds(p * 2 * TILES, 2 * TILES)
                pool.tensor_tensor(va_f[:, tiles], mv_f[:, tiles, 1], eps[:, 0:2 * TILES], ALU.add)
                pool.drain()
                pool.tensor_tensor(rs_f[:, tiles], va_f[:, tiles], neghalf[:, 0:2 * TILES], ALU.pow)
                pool.drain()
                pool.tensor_tensor(vb_f[:, tiles], rs_f[:, tiles], rs_f[:, tiles], ALU.mult)
                pool.drain()
                pool.tensor_tensor(vb_f[:, tiles], vb_f[:, tiles], mv_f[:, tiles, 1], ALU.mult)
                pool.drain()
                pool.tensor_tensor(vb_f[:, tiles], vb_f[:, tiles], eps[:, 0:2 * TILES], ALU.add)
                pool.drain()
                pool.tensor_tensor(va_f[:, tiles], vb_f[:, tiles], neghalf[:, 0:2 * TILES], ALU.pow)
                pool.drain()
                pool.tensor_tensor(rs_f[:, tiles], rs_f[:, tiles], va_f[:, tiles], ALU.mult)
                pool.tensor_tensor(nb_f[:, tiles], mv_f[:, tiles, 0], minus[:, 0:2 * TILES], ALU.mult)
                pool.drain()
                pool.tensor_tensor(nb_f[:, tiles], nb_f[:, tiles], rs_f[:, tiles], ALU.mult).then_inc(S["rstd_h"], 1)

            pool.wait_ge(S["block_params"], 16 * (8 + E))
            with pool.Fori(0, PAIRS) as p:
                for g, (t0, t1) in enumerate(CHUNKS):
                    for s in range(2):
                        pool.wait_ge(S["fa_ss"], nth(p, 2 * TILES, 2 * (t1 - 1) + s + 1))
                        pool.tensor_tensor(ss[:, s, t0:t1, :], ss[:, s, t0:t1, :], tiny[:, 0:4 * (t1 - t0)].rearrange("p (t h) -> p t h", h=4), ALU.add)
                        pool.drain()
                        pool.tensor_tensor(ssr[:, s, t0:t1, :], ss[:, s, t0:t1, :], neghalf[:, 0:4 * (t1 - t0)].rearrange("p (t h) -> p t h", h=4), ALU.pow).then_inc(S["fa_rs"], 1)
                half = bass.ds(p * (E * EK // 2), E * EK // 2)
                pool.tensor_copy(w2_h[:, half, :], w2_e[:, half, :])
                pool.drain()
                pool.tensor_tensor(w2_l[:, half, :], w2_e[:, half, :], w2_h[:, half, :].bitcast(F32), ALU.subtract).then_inc(S["w2_split"], 1)
                for s in range(2):
                    pool.wait_ge(S["y_high"], nth(p, 2, s + 1))
                    for cols in (bass.ds((2 * p + s) * TOK, TOK), bass.ds(BATCH * TOK + (2 * p + s) * TXT, TXT)):
                        op = pool.tensor_tensor(y_l[:, cols], y_all[:, cols], y_h[:, cols].bitcast(F32), ALU.subtract)
                    op.then_inc(S["y_split"], 1)

        @block.tensor
        def _(pe):
            def transpose(dst, src, rows_in):
                return pe.transpose(dst, src, ident[0:rows_in, 0:rows_in])

            def tok_turn_x(b):
                pe.wait_ge(S["x_loaded"], nth(b, 16, 16))
                for t in range(TT):
                    mm = transpose(ps[:, BANK_XT, t * P:(t + 1) * P], x_in[:, t, :], P)
                mm.then_inc(S["proj_full"], 1)

            def tok_project_qk(b):
                pe.wait_ge(S["xT_ready"], nth(b, 1, 1))
                for k, bank in enumerate((BANK_Q, BANK_K)):
                    pe.matmul(ps[:, bank, :], w_qk[:, k, :, :].rearrange("p a r -> p (a r)"), xT[:, :], start=True, stop=True).then_inc(S["proj_full"], 1)

            def tok_project_v(b):
                pe.wait_ge(S["out_done"], nth(b, UNITS, 1))
                for half in range(2):
                    for t in range(2):
                        tile_ = 2 * half + t
                        mm = pe.matmul(ps[:, BANK_V + half, t * 256:(t + 1) * 256], xT[:, tile_ * P:(tile_ + 1) * P],
                                       w_tv[:, :], start=True, stop=True)
                    mm.then_inc(S["proj_full"], 1)

            def tok_scores(b, n):
                i, a = divmod(n, 4)
                if n == 0:
                    pe.wait_ge(S["q_ready"], nth(b, 1, 1))
                    pe.wait_ge(S["k_ready"], nth(b, 1, 1))
                if n >= 2:
                    pe.wait_ge(S["prob_ready"], nth(b, UNITS, n - 1))
                rows_ = slice(32 * a, 32 * a + 3 * DQ)
                pe.matmul(ps[:, BANK_S + n % 2, :], qT[rows_, i * P:(i + 1) * P], kT[rows_, :], start=True, stop=True).then_inc(S["score_full"], 1)

            def tok_turn(b, n):
                pe.wait_ge(S["prob_ready"], nth(b, UNITS, n + 1))
                if n == 0:
                    pe.wait_ge(S["va_ready"], nth(b, 1, 1))
                    pe.wait_ge(S["vb_ready"], nth(b, 1, 1))
                else:
                    pe.wait_ge(S["probT_ready"], nth(b, UNITS, n))
                for j in range(TT):
                    mm = transpose(ps[:, BANK_T, j * P:(j + 1) * P], prob[:, n % 2, j * P:(j + 1) * P], P)
                mm.then_inc(S["probT_full"], 1)

            def tok_values(b, n):
                a = n % 4
                pe.wait_ge(S["probT_ready"], nth(b, UNITS, n + 1))
                pe.wait_ge(S["out_done"], nth(b, UNITS, n + 1))
                for j in range(TT):
                    mm = pe.matmul(ps[:, BANK_O, 0:2 * CH], probT[:, n % 2, j * P:(j + 1) * P],
                                   v_tok[:, j, a // 2 * 2 * CH:(a // 2 + 1) * 2 * CH], start=(j == 0), stop=(j == TT - 1))
                mm.then_inc(S["out_full"], 1)

            def txt_turn_norm(l, k):
                pe.wait_ge(S["tx_norm"], nth(l, 2, k))
                for b in range(BATCH):
                    mm = transpose(ps[:, BANK_TX, b * TXT:(b + 1) * TXT], tx_n[:, b, :], TXT)
                mm.then_inc(S["tx_normT"], 1)

            def txt_project(l):
                pe.wait_ge(S["tx_hT"], nth(l, 2, 1))
                pe.wait_ge(S["wk_loaded"], nth(l, 16, 16))
                pe.matmul(ps[:, BANK_TK, 0:SEQ4], w_k[:, :], hT[:, :], start=True, stop=True).then_inc(S["tx_k"], 1)
                pe.wait_ge(S["wq_loaded"], nth(l, 16, 16))
                pe.matmul(ps[:, BANK_TQ, 0:SEQ4], w_q[:, :], hT[:, :], start=True, stop=True).then_inc(S["tx_q"], 1)
                pe.wait_ge(S["wv_loaded"], nth(l, 16, 16))
                for b in range(BATCH):
                    mm = pe.matmul(ps[0:TXT, BANK_TV, b * D:(b + 1) * D], hT[:, b * TXT:(b + 1) * TXT], w_v[:, :], start=True, stop=True)
                mm.then_inc(S["tx_v"], 1)

            def txt_scores(l, b):
                if b == 0:
                    pe.wait_ge(S["tx_qs"], nth(l, 1, 1))
                    pe.wait_ge(S["tx_vs"], nth(l, 1, 1))
                else:
                    pe.wait_ge(S["tx_shift"], nth(l, BATCH, b))
                pe.wait_ge(S["tx_kbd"], nth(l, BATCH, b + 1))
                for g in range(2):
                    pe.matmul(ps[0:TXT, BANK_TX + g, 0:HALF], tqT[:, b * TXT:(b + 1) * TXT],
                              kbd[:, b, g * HALF:(g + 1) * HALF], start=True, stop=False)
                    mm = pe.matmul(ps[0:TXT, BANK_TX + g, 0:HALF], identb[0:TXT, 0:TXT],
                                   tmask[:, b, :].unsqueeze(1).broadcast_to([TXT, HEADS // 2, TXT]), start=False, stop=True)
                mm.then_inc(S["tx_score"], 1)

            def txt_turn_probs(l, b, g):
                pe.wait_ge(S["tx_exp"], nth(l, BATCH, b + 1))
                if 2 * b + g >= 1:
                    pe.wait_ge(S["tx_pT"], nth(l, 2 * BATCH, 2 * b + g))
                for k in range(HEADS // 2):
                    h = g * HEADS // 2 + k
                    mm = transpose(ps[0:TXT, BANK_TPT, k * TXT:(k + 1) * TXT], ts[:, b, h * TXT:(h + 1) * TXT], TXT)
                mm.then_inc(S["tx_pt"], 1)

            def txt_values(l, b):
                pe.wait_ge(S["tx_pT"], nth(l, 2 * BATCH, 2 * b + 2))
                if b == 0:
                    pe.wait_ge(S["tx_kbd"], nth(l, BATCH, BATCH))
                else:
                    pe.wait_ge(S["tx_ctx"], nth(l, BATCH, b))
                for h in range(HEADS):
                    mm = pe.matmul(ps[0:TXT, BANK_TC, h * (HD + 1):(h + 1) * (HD + 1)],
                                   tpT[:, b, h * TXT:(h + 1) * TXT], tv[:, b, h, :], start=True, stop=True)
                mm.then_inc(S["tx_pv"], 1)

            def txt_turn_ctx(l):
                pe.wait_ge(S["tx_ctx"], nth(l, BATCH, BATCH))
                pe.wait_ge(S["tx_shift"], nth(l, BATCH, BATCH))
                for b in range(BATCH):
                    mm = transpose(ps[:, BANK_TX, b * TXT:(b + 1) * TXT], tctx[:, b, :], TXT)
                mm.then_inc(S["tx_ct"], 1)

            def txt_out(l):
                pe.wait_ge(S["tx_cT"], nth(l, 1, 1))
                pe.wait_ge(S["wo_loaded"], nth(l, 16, 16))
                for b in range(BATCH):
                    mm = pe.matmul(ps[0:TXT, BANK_TY, b * D:(b + 1) * D], cT[:, b * TXT:(b + 1) * TXT], w_o[:, :], start=True, stop=True)
                mm.then_inc(S["tx_o"], 1)

            def txt_up(l):
                pe.wait_ge(S["tx_hT"], nth(l, 2, 2))
                pe.wait_ge(S["w1_loaded"], nth(l, 16, 16))
                for j in range(KT):
                    pe.matmul(ps[:, BANKS_UP[j], 0:SEQ4], w_1[:, j * P:(j + 1) * P], hT[:, :], start=True, stop=True).then_inc(S["tx_f1"], 1)

            def txt_down(l):
                pe.wait_ge(S["tx_g"], nth(l, KT, KT))
                pe.wait_ge(S["w2_loaded"], nth(l, 16, 16))
                for b in range(BATCH):
                    for j in range(KT):
                        mm = pe.matmul(ps[0:TXT, BANK_TY, b * D:(b + 1) * D], gact[:, j, b * TXT:(b + 1) * TXT],
                                       w_2[:, j, :], start=(j == 0), stop=(j == KT - 1))
                mm.then_inc(S["tx_f2"], 1)

            def first_loop_turn(t, last=False):
                tok_project_v(t)
                for n in range(UNITS + 2):
                    if n < UNITS:
                        tok_scores(t, n)
                    if n == AT_TURN1:
                        txt_turn_norm(t, 1)
                    if n == AT_PROJECT:
                        txt_project(t)
                    if n in AT_VALUES:
                        txt_values(t, AT_VALUES.index(n))
                    if n in AT_SCORES:
                        txt_scores(t, AT_SCORES.index(n))
                    if n in AT_TURN:
                        txt_turn_probs(t, AT_TURN.index(n), 0)
                    if n == AT_CTX_TURN:
                        txt_turn_ctx(t)
                    if n == AT_OUT:
                        txt_out(t)
                    if n == UNITS and not last:
                        tok_turn_x(t + 1)
                    if n == AT_TURN2:
                        txt_turn_norm(t, 2)
                    if 1 <= n <= UNITS:
                        tok_turn(t, n - 1)
                    if n == UNITS + 1 and not last:
                        tok_project_qk(t + 1)
                    if n >= 2:
                        tok_values(t, n - 2)
                    if n in AT_TURN:
                        txt_turn_probs(t, AT_TURN.index(n), 1)
                    if n == AT_UP:
                        txt_up(t)
                    if n == AT_DOWN:
                        txt_down(t)

            pe.wait_ge(S["const_pool"], 2)
            tok_turn_x(0)
            pe.wait_ge(S["qk_repeated"], 1)
            tok_project_qk(0)
            pe.wait_ge(S["const_pool"], 3)
            pe.wait_ge(S["params"], 16 * N_PARAMS)
            transpose(ps[:, 7, 0:NVEC[0]], vrow[:, :], NVEC[0]).then_inc(S["setup_psum"], 1)
            pe.wait_ge(S["setup_done"], 1)
            with pe.Fori(0, BATCH - 1) as t:
                first_loop_turn(t)
            first_loop_turn(BATCH - 1, last=True)

            pe.wait_ge(S["seq_tok"], BATCH)
            pe.wait_ge(S["l_weights"], 16 * (4 + 3 + 2 * FH))
            for k in range(6):
                mm = transpose(ps[:, k // 4, k % 4 * P:(k % 4 + 1) * P], w_lraw[:, k, :], P)
            for k in range(4):
                transpose(ps[:, 2, k * P:(k + 1) * P], w_loraw[:, k * P:(k + 1) * P], P)
            transpose(ps[:, 3, 0:NVEC[1]], vrow_f[:, :], NVEC[1]).then_inc(S["l_wT"], 1)
            pe.wait_ge(S["l_wT_done"], 1)
            pe.wait_ge(S["tx_norm"], 2 * LAYERS + 1)

            def wide(bank, lhsT, rhs, width=T):
                pe.matmul(banks(bank, 512), lhsT, rhs[:, 0:512], start=True, stop=True)
                return pe.matmul(ps[:, bank + 1, 0:width - 512], lhsT, rhs[:, 512:width], start=True, stop=True)

            def turn_tiles(s, tiles):
                for i in tiles:
                    r = ROWS[i]
                    c0 = 4 * s * 512 + i * P
                    mm = transpose(psf[:, c0:c0 + r], xn[0:r, s, i, :], r)
                return mm

            BO, BS, BA = 0, 1, 2

            def la_scores(p, s, i):
                r = ROWS[i]
                pe.wait_ge(S["la_qbd"], nth(p, 2 * TILES, 2 * i + s + 1))
                for g in range(2):
                    mm = pe.matmul(ps[0:r, 4 * s + BA + g, 0:4 * r], lk[:, s, i * P:i * P + r],
                                   lqbd[:, s, 4 * g:4 * g + 4, 0:r], start=True, stop=True)
                mm.then_inc(S["la_at"], 1)

            def la_outputs(p, s, i):
                r = ROWS[i]
                pe.wait_ge(S["la_masked"], nth(p, 2 * TILES, 2 * i + s + 1))
                if i >= 1:
                    pe.wait_ge(S["la_sbd"], nth(p, 2 * TT, 2 * (i - 1) + s + 1))
                    pe.wait_ge(S["seq_tile"], nth(p, 2 * TILES, 2 * (i - 1) + s + 1))
                bank = 4 * s + BO
                for g in range(4):
                    if i >= 1:
                        pe.matmul(ps[:, bank, g * r:(g + 1) * r], lsbd[:, s, g * P:(g + 1) * P], lq[:, s, i * P:i * P + r],
                                  start=True, stop=False, skip_group_check=True)
                    for h in (2 * g, 2 * g + 1):
                        p0 = LV * (h % 2)
                        mm = pe.matmul(ps[p0:p0 + LV, bank, g * r:(g + 1) * r], lv[0:r, s, i, h * LV:(h + 1) * LV],
                                       la[0:r, s, h, 0:r], start=(i == 0), stop=True, skip_group_check=True)
                mm.then_inc(S["la_ot"], 1)

            def la_state(p, s, i):
                pe.matmul(ps[:, 4 * s + BS, :], lktok[:, s, i, :], lv[:, s, i, :], start=(i == 0), stop=(i == TT - 1),
                          skip_group_check=True).then_inc(S["la_state"], 1)

            def la_project(p, s, i):
                r = ROWS[i]
                pe.wait_ge(S["la_lo"], nth(p, 2 * TILES, 2 * i + s + 1))
                for g in range(4):
                    mm = pe.matmul(ps[0:r, 4 * s + BO, 0:D], lo[:, s, g, 0:r], w_loT[:, g, :],
                                   start=(g == 0), stop=(g == 3))
                mm.then_inc(S["la_y"], 1)

            with pe.Fori(0, PAIRS) as p:
                for s in range(2):
                    pe.wait_ge(S["lin_free"], nth(p, 2, s + 1))
                    pe.wait_ge(S["la_norm"], nth(p, 4, s + 1))
                    turn_tiles(s, range(TT)).then_inc(S["la_normT"], 1)
                w_query, w_key = w_lT[:, 0:P], w_lT[:, P:2 * P]
                for s in range(2):
                    pe.wait_ge(S["la_hT"], nth(p, 4, s + 1))
                    for w, bank in ((w_key, BANK_LK), (w_query, BANK_LQ)):
                        pe.matmul(ps[:, 4 * s + bank, :], w, sT[:, s, 0:TOK], start=True, stop=True).then_inc(S["la_qk"], 1)
                for i in range(TILES):
                    for s in range(2):
                        if i >= 1:
                            pe.wait_ge(S["la_vdone"], nth(p, 2 * TILES, 2 * (i - 1) + s + 1))
                        pe.matmul(ps[:, 4 * s + BANK_LV, :], sT[:, s, i * P:(i + 1) * P], w_lT[:, 2 * P:6 * P], start=True, stop=True).then_inc(S["la_vfull"], 1)
                    if i == 1:
                        for s in range(2):
                            pe.wait_ge(S["la_norm"], nth(p, 4, s + 3))
                            turn_tiles(s, [TT]).then_inc(S["la_normT"], 1)
                    if i == 3:
                        for s in range(2):
                            pe.wait_ge(S["la_hT"], nth(p, 4, s + 3))
                            for w, col in ((w_key, COL_LK), (w_query, COL_LQ)):
                                pe.matmul(ps[:, 4 * s + BANK_LTXT, col:col + TXT], w, sT[:, s, TOK:T], start=True, stop=True).then_inc(S["la_qk"], 1)
                for s in range(2):
                    pe.wait_ge(S["la_feat"], nth(p, 8, 2 * s + 2))
                    for i in range(TT):
                        mm = transpose(ps[:, 4 * s + BANK_LK, i * P:(i + 1) * P], lk[:, s, i * P:(i + 1) * P], P)
                    mm.then_inc(S["la_ktps"], 1)
                for s in range(2):
                    pe.wait_ge(S["la_qz"], nth(p, 2, s + 1))
                    for i in range(TILES):
                        mm = pe.matmul(ps[:, 4 * s + BANK_LQ, i * LH:(i + 1) * LH], lz[:, s, i * P:(i + 1) * P], hmask[:, :], start=True, stop=True)
                    mm.then_inc(S["la_den"], 1)
                pe.wait_ge(S["la_vdone"], nth(p, 2 * TILES, 2 * TILES))
                for s in range(2):
                    pe.wait_ge(S["la_rden"], nth(p, 2, s + 1))
                    pe.wait_ge(S["la_ktok"], nth(p, 2, s + 1))
                    for i in range(TILES):
                        r = ROWS[i]
                        c0 = (4 * s + 2) * 512 + i * P
                        mm = transpose(psf[:, c0:c0 + r], lrexp[0:r, s, i, :, :].rearrange("p h d -> p (h d)"), r)
                    mm.then_inc(S["la_rT"], 1)
                pe.wait_ge(S["la_q"], nth(p, 2, 2))
                for i in range(TILES):
                    for s in range(2):
                        la_scores(p, s, i)
                    if i >= 1:
                        for s in range(2):
                            la_project(p, s, i - 1)
                    for s in range(2):
                        la_outputs(p, s, i)
                    if i < TT:
                        for s in range(2):
                            la_state(p, s, i)
                for s in range(2):
                    la_project(p, s, TT)

            pe.wait_ge(S["lin_free"], BATCH + 2)
            pe.wait_ge(S["block_params"], 16 * (8 + E))
            units = [(i, h, s) for i in TILE_ORDER for h in range(FH) for s in range(2)]

            def fa_scores(p, n):
                i, h, s = units[n]
                r, width = ROWS[i], min((i + 1) * P, T)
                if n >= 2:
                    pe.wait_ge(S["fa_exp"], nth(p, FU, n - 1))
                lhsT = fq[h * FD:(h + 1) * FD, s, i * P:i * P + r]
                for c, w in ((0, min(width, 512)), (512, width - 512)):
                    if w > 0:
                        pe.matmul(ps[0:r, 4 * s + c // 512, 0:w], lhsT, fk[h * FD:(h + 1) * FD, s, c:c + w],
                                  start=True, stop=False, skip_group_check=True)
                c0 = 4 * s * 512 + i * P
                pe.matmul(psf[0:r, c0:c0 + r], identb[0:r, 0:r], causalb[0:r, 0:r],
                          start=False, stop=True, skip_group_check=True).then_inc(S["fa_s"], 1)

            def wait_pT(p, n):
                pe.wait_ge(S["fa_pT_act" if n % 2 == 0 else "fa_pT_dve"], nth(p, FU // 2, n // 2 + 1))

            def fa_turn(p, n):
                i, h, s = units[n]
                r = ROWS[i]
                pe.wait_ge(S["fa_pn"], nth(p, FU, n + 1))
                if n >= 2:
                    wait_pT(p, n - 2)
                for j in range(i + 1):
                    c = ROWS[j]
                    mm = transpose(ps[0:c, 4 * s + 2, j * r:(j + 1) * r], fpn[0:r, s, j * P:j * P + c], r)
                mm.then_inc(S["fa_pt"], 1)

            def fa_values(p, n):
                i, h, s = units[n]
                r = ROWS[i]
                wait_pT(p, n)
                k = TILE_ORDER.index(i)
                if h == 0 and k >= 1:
                    pe.wait_ge(S["fa_oT"], nth(p, 2 * TILES, 2 * (k - 1) + s + 1))
                for j in range(i + 1):
                    c = ROWS[j]
                    mm = pe.matmul(ps[h * FD:(h + 1) * FD, 4 * s + 3, 0:r],
                                   qkv[0:c, s, j, 2 * D + h * FD:2 * D + (h + 1) * FD], fpT[0:c, s, j * r:(j + 1) * r],
                                   start=(j == 0), stop=(j == i))
                mm.then_inc(S["fa_o"], 1)

            with pe.Fori(0, PAIRS) as p:
                for s in range(2):
                    pe.wait_ge(S["y_done"], nth(p, 2, s + 1))
                    pe.wait_ge(S["fa_xn"], nth(p, 2, s + 1))
                    turn_tiles(s, range(TILES)).then_inc(S["fa_xT"], 1)
                for i in range(TILES):
                    for s in range(2):
                        if i == 0:
                            pe.wait_ge(S["fa_hT"], nth(p, 2, s + 1))
                        if i >= 2:
                            pe.wait_ge(S["fa_qkv_sb"], nth(p, 2 * TILES, 2 * (i - 2) + s + 1))
                        pe.matmul(ps[:, 4 * s + 2 + i % 2, 0:3 * D], sT[:, s, i * P:(i + 1) * P], w_fqkv[:, :],
                                  start=True, stop=True).then_inc(S["fa_qkv"], 1)
                for g, (t0, t1) in enumerate(CHUNKS):
                    for s in range(2):
                        pe.wait_ge(S["fa_norm"], nth(p, 4, 2 * g + s + 1))
                        for part in range(2):
                            for i in range(t0, t1):
                                r = ROWS[i]
                                c0 = (4 * s + 2 * part) * 512 + i * P
                                mm = transpose(psf[:, c0:c0 + r], qkv[0:r, s, i, part * D:(part + 1) * D], r)
                            if g == 1:
                                mm.then_inc(S["fa_T"], 1)
                pe.wait_ge(S["fa_qT"], nth(p, 2, 2))
                pe.wait_ge(S["fa_kT"], nth(p, 2, 2))
                for n in range(FU + 3):
                    if n < FU:
                        fa_scores(p, n)
                    if 2 <= n <= FU + 1:
                        fa_turn(p, n - 2)
                    if n >= 3:
                        fa_values(p, n - 3)
                for s in range(2):
                    pe.wait_ge(S["fa_oT"], nth(p, 2 * TILES, 2 * TT + s + 1))
                    wide(4 * s, w_fo[:, :], foT[:, s, :]).then_inc(S["y_ps"], 1)

            pe.wait_ge(S["y_done"], BATCH + 2)
            pe.wait_ge(S["e_split"], BATCH)
            for j, r in enumerate([P] * (BATCH * TT) + TXT_ROWS):
                mm = pe.matmul(ps[0:r, 7, j * E:(j + 1) * E], y_all[:, j * P:j * P + r], w_gate[:, :], start=True, stop=True)
            mm.then_inc(S["g_ps"], 1)
            pe.wait_ge(S["y_split"], BATCH)
            pe.wait_ge(S["w2_split"], PAIRS)

            def experts(c, rows, cols, first=False):
                width = sum(rows)

                def up(e):
                    for f in range(EK):
                        n = e * EK + f
                        if n >= 4:
                            pe.wait_ge(S["up_done"], nth(c, E * EK, n - 3))
                        for k, (w, y) in enumerate(((w1_h, y_h), (w1_h, y_l), (w1_l, y_h))):
                            mm = pe.matmul(ps[:, n % 4, 0:width], w[:, e, f * P:(f + 1) * P], y[:, cols], start=(k == 0), stop=(k == 2))
                        mm.then_inc(S["up"], 1)

                def gates(e):
                    if e >= 2:
                        pe.wait_ge(S["acc_used"], nth(c, E, e - 1))
                    pe.matmul(ps[:, 6 + e % 2, 0:width], gate_sel[:, e, :], gateT[:, 0:width], start=True, stop=True).then_inc(S["gate_ps"], 1)

                def down(e):
                    if e >= 2:
                        pe.wait_ge(S["acc_used"], nth(c, E, e - 1))
                    for f in range(EK):
                        pe.wait_ge(S["hid_split"], nth(c, E * EK, e * EK + f + 1))
                        for k, (w, h) in enumerate(((w2_h, hid_h), (w2_l, hid_h), (w2_h, hid_l))):
                            mm = pe.matmul(ps[:, 4 + (e + 1) % 2, 0:width], w[:, e * EK + f, :], h[:, e % 2, f, 0:width],
                                           start=(f == 0 and k == 0), stop=(f == EK - 1 and k == 2))
                    mm.then_inc(S["down"], 1)

                up(0)
                pe.wait_ge(S["g_chunk"], nth(c, 1, 1))
                if not first:
                    pe.wait_ge(S["acc_used"], nth(c, E, 0))
                for i, r in enumerate(rows):
                    mm = transpose(ps[0:2 * E, 6, i * P:i * P + r], gate_c[0:r, i, :], r)
                mm.then_inc(S["g_tps"], 1)
                if not first:
                    turn_back(c - 1, [P] * TT)
                up(1)
                pe.wait_ge(S["g_T"], nth(c, 1, 1))
                pe.matmul(ps[:, 4, 0:width], b2_e[:, :], gateT[:, 0:width].bitcast(F32), start=True, stop=True).then_inc(S["b2_ps"], 1)
                if not first:
                    pe.wait_ge(S["chunk_done"], c)
                gates(0)
                down(0)
                for e in range(1, E):
                    if e < E - 1:
                        up(e + 1)
                    if e == 1:
                        pe.wait_ge(S["acc_init"], nth(c, 1, 1))
                    gates(e)
                    down(e)

            def turn_back(c, rows):
                pe.wait_ge(S["acc_done"], nth(c, 1, 1))
                for i, r in enumerate(rows):
                    mm = transpose(ps[0:r, 5, i * P:(i + 1) * P], acc[:, i * P:i * P + r], P)
                mm.then_inc(S["y_turned"], 1)

            experts(0, [P] * TT, slice(0, TOK), first=True)
            with pe.Fori(1, BATCH) as c:
                experts(c, [P] * TT, bass.ds(c * TOK, TOK))
            experts(BATCH, TXT_ROWS, slice(BATCH * TOK, POS))
            turn_back(BATCH, TXT_ROWS)

        @block.vector
        def _(dve):
            def one(buffer, k):
                return buffer[:, bass.ds(k, 1), :].rearrange("p a d -> p (a d)")

            def seq_at(k):
                return one(seq, k)

            dve.sem_inc(S["out_done"], 1)
            dve.sem_inc(S["lin_free"], 2)
            dve.memset(tv[:, :, :, HD:HD + 1], 1.0)
            dve.memset(seq[:, :, :], 0.0)
            def tok_queries_keys(b):
                for k, (dst, high, bank, ready) in enumerate(((qT, q_high, BANK_Q, "q_ready"), (kT, k_high, BANK_K, "k_ready"))):
                    dve.wait_ge(S["qk_high"], nth(b, 2, k + 1))
                    dve.scalar_tensor_tensor(dst[:, :], high[:, :].bitcast(F32), low_rows[:, k:k + 1], ps[:, bank, :],
                                             ALU.mult, ALU.add).then_inc(S[ready], 1)

            def tok_max(b, n):
                dve.wait_ge(S["score_full"], nth(b, UNITS, n + 1))
                dve.tensor_reduce(nmax[:, n:n + 1], ps[:, n % 2, :], AX.X, ALU.max, negate=True).then_inc(S["max_ready"], 1)

            def tok_rsum(b, n):
                dve.wait_ge(S["prob_ready"], nth(b, UNITS, n + 1))
                dve.reciprocal(rsum[:, n:n + 1], psum_e[:, n:n + 1])

            def tok_out(b, n):
                i, a = divmod(n, 4)
                s = a // 2
                dve.wait_ge(S["out_full"], nth(b, UNITS, n + 1))
                o = ps[:, BANK_O, a % 2 * CH:(a % 2 + 1) * CH]
                if a % 2 == 0:
                    dve.tensor_scalar(intra[:, s, :], o, rsum[:, n:n + 1], mix[:, s:s + 1], ALU.mult, ALU.mult).then_inc(S["out_done"], 1)
                else:
                    dst = seq[:, bass.ds(b * TILES + i, 1), s * CH:(s + 1) * CH]
                    dve.scalar_tensor_tensor(dst, o.unsqueeze(1), rsum[:, n:n + 1], intra[:, s, :].unsqueeze(1), ALU.mult, ALU.add).then_inc(S["out_done"], 1)

            def norm_stats(l, k):
                for b in range(BATCH):
                    dve.bn_stats(tx_st[:, b, :], tx[:, b, :])
                dve.drain()
                for b in range(BATCH):
                    mm = dve.bn_aggr(tx_mv[:, b, :], tx_st[:, b, :])
                mm.then_inc(S["tx_stat"], 1)

            def normalise(l, k):
                dve.wait_ge(S["tx_rstd"], nth(l, 2, k))
                for b in range(BATCH):
                    mm = dve.tensor_scalar(tx_n[:, b, :], tx[:, b, :], tx_mv[:, b, 0:1], tx_rs[:, b:b + 1], ALU.subtract, ALU.mult)
                mm.then_inc(S["tx_norm"], 1)

            def scale_turned(l, k, g, c):
                dve.wait_ge(S["tx_normT"], nth(l, 2, k))
                dve.tensor_scalar(hT[:, :], ps[:, BANK_TX, 0:SEQ4], vcol[:, bass.ds(VEC[g] + l, 1)], vcol[:, bass.ds(VEC[c] + l, 1)],
                                  ALU.mult, ALU.add).then_inc(S["tx_hT"], 1)

            def txt_kbd(l, b):
                dve.scalar_tensor_tensor(
                    kbd[:, b, :].rearrange("p (h t) -> p h t", h=HEADS),
                    ps[:, BANK_TK, b * TXT:(b + 1) * TXT].unsqueeze(1).broadcast_to([P, HEADS, TXT]),
                    vcol[:, bass.ds(VEC["bk"] + l, 1)],
                    hmask[:, :].unsqueeze(2).broadcast_to([P, HEADS, TXT]), ALU.add, ALU.mult).then_inc(S["tx_kbd"], 1)

            def txt_vs(l):
                dve.wait_ge(S["tx_v"], nth(l, 1, 1))
                dve.wait_ge(S["params_later"], 16 * 5)
                for b in range(BATCH):
                    mm = dve.tensor_tensor(tv[:, b, :, 0:HD], ps[0:TXT, BANK_TV, b * D:(b + 1) * D].rearrange("p (h d) -> p h d", h=HEADS),
                                           bv_r[:, bass.ds(l, 1), :].rearrange("p a (h d) -> p (a h) d", h=HEADS), ALU.add)
                mm.then_inc(S["tx_vs"], 1)

            def txt_shift(l, b):
                dve.wait_ge(S["tx_score"], nth(l, BATCH, b + 1))
                scores = ps[0:TXT, BANK_TX:BANK_TX + 2, 0:HALF].rearrange("p g (h t) -> p g h t", t=TXT)
                dve.tensor_reduce(tnm[:, b, :].rearrange("p (g h) -> p g h", g=2), scores, AX.X, ALU.max, negate=True)
                dve.drain()
                dve.tensor_tensor(ts[:, b, :].rearrange("p (g h t) -> p g h t", g=2, h=HEADS // 2), scores,
                                  tnm[:, b, :].rearrange("p (g h) -> p g h", g=2).unsqueeze(3).broadcast_to([TXT, 2, HEADS // 2, TXT]),
                                  ALU.add).then_inc(S["tx_shift"], 1)

            def txt_context(l, b):
                dve.wait_ge(S["tx_pv"], nth(l, BATCH, b + 1))
                o = ps[0:TXT, BANK_TC, 0:HEADS * (HD + 1)].rearrange("p (h d) -> p h d", h=HEADS)
                dve.reciprocal(trs[:, b, :], o[:, :, HD])
                dve.drain()
                dve.tensor_tensor(tctx[:, b, :].rearrange("p (h d) -> p h d", h=HEADS), o[:, :, 0:HD],
                                  trs[:, b, :].unsqueeze(2).broadcast_to([TXT, HEADS, HD]), ALU.mult).then_inc(S["tx_ctx"], 1)

            def txt_residual(l, product, k):
                dve.wait_ge(S[product], nth(l, 1, 1))
                dve.wait_ge(S["tx_resid"], nth(l, 2, k))
                dve.tensor_tensor(tx[:, :, :], ps[0:TXT, BANK_TY, :].rearrange("p (b d) -> p b d", b=BATCH), tx_res[:, :, :], ALU.add)
                dve.drain()

            def seq_stats(t, i):
                dve.bn_stats(st5[:, 0, i, :], seq_at(t * TILES + i))

            def first_loop_turn(t, last=False):
                for n in range(UNITS + 2):
                    if n < UNITS:
                        tok_max(t, n)
                    if n == AT_NORM1:
                        normalise(t, 1)
                    dve.drain()
                    if 1 <= n <= UNITS:
                        tok_rsum(t, n - 1)
                    if n == AT_TURN1:
                        scale_turned(t, 1, "g1", "c1")
                    if n == AT_PROJECT:
                        dve.wait_ge(S["tx_k"], nth(t, 1, 1))
                        txt_kbd(t, 0)
                        txt_vs(t)
                        txt_kbd(t, 1)
                    if AT_PROJECT < n < AT_PROJECT + BATCH - 1:
                        txt_kbd(t, n - AT_PROJECT + 1)
                    if n in AT_VALUES:
                        txt_context(t, AT_VALUES.index(n))
                    if n in AT_SCORES:
                        txt_shift(t, AT_SCORES.index(n))
                    if n == AT_OUT:
                        txt_residual(t, "tx_o", 1)
                        norm_stats(t, 2)
                    if n == AT_NORM2:
                        normalise(t, 2)
                    if n == AT_SPLIT:
                        dve.wait_ge(S["e_loaded"], nth(t, 32, 32))
                        dve.tensor_copy(w1_h[:, bass.ds(2 * t, 2), :], w1_raw[:, :, :]).then_inc(S["e_high"], 1)
                    if n == AT_TURN2:
                        scale_turned(t, 2, "g2", "c2")
                    if n == UNITS + 1 and not last:
                        tok_queries_keys(t + 1)
                    if n >= 2:
                        tok_out(t, n - 2)
                    if n >= 8 and n % TT == 0:
                        seq_stats(t, n // TT - 2)
                dve.drain().then_inc(S["seq_tok"], 1)
                seq_stats(t, TT - 1)
                dve.drain()
                for i in range(TT):
                    dve.bn_aggr(mv5[:, i, :], st5[:, 0, i, :])
                dve.drain()
                dve.tensor_copy(mv_l[:, bass.ds(t * TILES, TT), :], mv5[:, 0:TT, :]).then_inc(S["stat_tok"], 1)
                txt_residual(t, "tx_f2", 2)
                norm_stats(t, 3)

            dve.wait_ge(S["const_pool"], 2)
            dve.tensor_reduce(low_rows[:, :], low_sel[:, :, :], AX.X, ALU.add)
            dve.wait_ge(S["qk_weights"], 16 * 12)
            for part in range(3):
                cols = slice(part * DQ, (part + 1) * DQ)
                dve.tensor_scalar(w_qk[:, 0, :, cols], w_qk_in[:, 0, :, :], DQ ** -0.5, None, ALU.mult)
                dve.tensor_copy(w_qk[:, 1, :, cols], w_qk_in[:, 1, :, :])
            dve.drain().then_inc(S["qk_repeated"], 1)
            tok_queries_keys(0)
            dve.wait_ge(S["params"], 16 * N_PARAMS)
            dve.wait_ge(S["const_pool"], 3)
            dve.wait_ge(S["setup_psum"], 1)
            dve.tensor_copy(vcol[:, :], ps[:, 7, 0:NVEC[0]])
            dve.tensor_scalar(padrow[:, :, :], padrow[:, :, :], 0.0, NEG, ALU.is_equal, ALU.mult)
            dve.drain()
            dve.tensor_tensor(tmask[:, :, :], padrow[:, :, :], causal_t[:, :].unsqueeze(1).broadcast_to([TXT, BATCH, TXT]), ALU.add)
            dve.tensor_scalar(bq4[:, :], vcol[:, VEC["bq"]:VEC["bq"] + LAYERS], HD ** -0.5, None, ALU.mult)
            dve.wait_ge(S["txt_embed"], 16 * BATCH)
            dve.tensor_tensor(tx[:, :, :], tx[:, :, :], pos[:, :].unsqueeze(1).broadcast_to([TXT, BATCH, D]), ALU.add)
            dve.drain().then_inc(S["setup_done"], 1)
            norm_stats(0, 1)
            with dve.Fori(0, BATCH - 1) as t:
                first_loop_turn(t)
            first_loop_turn(BATCH - 1, last=True)
            normalise(LAYERS, 1)
            dve.drain()
            dve.tensor_tensor(tx_n[:, :, :], tx_n[:, :, :], lnf_g[:, :].unsqueeze(1).broadcast_to([TXT, BATCH, D]), ALU.mult)
            dve.drain()
            dve.tensor_tensor(seq[0:TXT, TT::TILES, :], tx_n[:, :, :], lnf_b[:, :].unsqueeze(1).broadcast_to([TXT, BATCH, D]), ALU.add)

            dve.drain()
            for b in range(BATCH):
                dve.bn_stats(st5[:, 0, b, :], seq[:, b * TILES + TT, :])
            dve.drain()
            for b in range(BATCH):
                op = dve.bn_aggr(mv_l[:, b * TILES + TT, :], st5[:, 0, b, :])
            op.then_inc(S["stat_tok"], 1)
            dve.memset(lz[:, :, T:TP], 0.0)
            def la_features(p, s, text):
                k0 = 4 * text + 2 * s
                cols = slice(TOK, T) if text else slice(0, TOK)
                if text:
                    src = [ps[:, 4 * s + BANK_LTXT, c:c + TXT] for c in (COL_LK, COL_LQ)]
                else:
                    src = [ps[:, 4 * s + bank, :] for bank in (BANK_LK, BANK_LQ)]
                for k, part in enumerate((lt1, lt2)):
                    dve.wait_ge(S["la_qk"], nth(p, 8, k0 + (2 if text else k + 1)))
                    dve.tensor_scalar(part[:, s, cols], src[k], 0.0, None, ALU.min).then_inc(S["la_min"], 1)
                for k, (part, feat) in enumerate(((lt1, lk), (lt2, lq))):
                    dve.wait_ge(S["la_exp"], nth(p, 8, k0 + k + 1))
                    dve.scalar_tensor_tensor(feat[:, s, cols], src[k], 0.0, part[:, s, cols], ALU.max, ALU.add).then_inc(S["la_feat"], 1)

            def la_running(p):
                dve.drain()
                for s in range(2):
                    dve.tensor_tensor_scan(lz[:, s, 0:T], ones[:, :], lk[:, s, :], 0.0, ALU.mult, ALU.add)
                dve.drain()
                for s in range(2):
                    dve.tensor_tensor(lz[:, s, 0:T], lz[:, s, 0:T], lq[:, s, :], ALU.mult).then_inc(S["la_qz"], 1)

            def la_reciprocal(p, s):
                dve.wait_ge(S["la_den"], nth(p, 2, s + 1))
                den = lden[:, s, :, :]
                dve.tensor_scalar(den, ps[:, 4 * s + BANK_LQ, 0:TILES * LH].rearrange("p (t h) -> p t h", h=LH), 1e-6, None, ALU.max)
                dve.drain()
                dve.reciprocal(den, den)
                dve.drain()
                dve.tensor_copy(lrexp[:, s, :, :, :], den.unsqueeze(3).broadcast_to([P, TILES, LH, LD])).then_inc(S["la_rden"], 1)

            def la_mask(p, s, i):
                r = ROWS[i]
                dve.wait_ge(S["la_at"], nth(p, 2 * TILES, 2 * i + s + 1))
                bank = 4 * s + 2
                dve.tensor_tensor(la[0:r, s, :, 0:r].rearrange("p (g h) t -> p g h t", g=2),
                                  ps[0:r, bank:bank + 2, 0:4 * r].rearrange("p g (h t) -> p g h t", h=4),
                                  causal01[0:r, 0:r].unsqueeze(1).unsqueeze(1).broadcast_to([r, 2, 4, r]),
                                  ALU.mult).then_inc(S["la_masked"], 1)

            def la_keep_state(p, s, i):
                dve.wait_ge(S["la_state"], nth(p, 2 * TT, 2 * i + s + 1))
                dve.tensor_tensor(lsbd[:, s, :].rearrange("p (h v) -> p h v", h=LH), ps[:, 4 * s + 1, :].rearrange("p (h v) -> p h v", h=LH),
                                  hmask[:, :].unsqueeze(2).broadcast_to([P, LH, LV]), ALU.mult).then_inc(S["la_sbd"], 1)

            def la_residual(p, s, i):
                r = ROWS[i]
                dve.wait_ge(S["la_y"], nth(p, 2 * TILES, 2 * i + s + 1))
                at_ = seq[0:r, bass.ds((2 * p + s) * TILES + i, 1), :]
                dve.tensor_tensor(at_, ps[0:r, 4 * s, 0:D].unsqueeze(1), at_, ALU.add).then_inc(S["seq_tile"], 1)

            with dve.Fori(0, PAIRS) as p:
                for text in (0, 1):
                    for s in range(2):
                        la_features(p, s, text)
                la_running(p)
                for s in range(2):
                    la_reciprocal(p, s)
                for s in range(2):
                    dve.wait_ge(S["la_rT"], nth(p, 2, s + 1))
                    dve.tensor_tensor(lq[:, s, :], banks(4 * s + 2, T), lq[:, s, :], ALU.mult).then_inc(S["la_q"], 1)
                for i in range(TILES):
                    for s in range(2):
                        la_mask(p, s, i)
                    if i >= 1:
                        for s in range(2):
                            la_residual(p, s, i - 1)
                    if i < TT:
                        for s in range(2):
                            la_keep_state(p, s, i)
                    if i >= 1:
                        dve.drain()
                        for s in range(2):
                            dve.bn_stats(st5[:, s, i - 1, :], seq_at((2 * p + s) * TILES + i - 1))
                for s in range(2):
                    la_residual(p, s, TT)
                dve.drain().then_inc(S["lin_free"], 2)
                for s in range(2):
                    dve.bn_stats(st5[:, s, TT, :], seq_at((2 * p + s) * TILES + TT))
                dve.drain()
                for s in range(2):
                    for i in range(TILES):
                        dve.bn_aggr(mv5[:, s * TILES + i, :], st5[:, s, i, :])
                dve.drain()
                dve.tensor_copy(mv_f[:, bass.ds(p * 2 * TILES, 2 * TILES), :], mv5[:, :, :]).then_inc(S["stat_h"], 1)

            dve.wait_ge(S["block_params"], 16 * (8 + E))
            dve.wait_ge(S["l_wT_done"], 1)
            dve.scalar_tensor_tensor(qkg[:, :], vcol_f[:, VEC["qn"]:VEC["qn"] + 1], FD ** 0.5,
                                     vcol_f[:, VEC["kn"]:VEC["kn"] + 1], ALU.mult, ALU.mult)
            dve.drain()
            units = [(i, h, s) for i in TILE_ORDER for h in range(FH) for s in range(2)]

            def rowmax(p, n):
                i, h, s = units[n]
                r, width = ROWS[i], min((i + 1) * P, T)
                dve.wait_ge(S["fa_s"], nth(p, FU, n + 1))
                dve.tensor_reduce(fnm[0:r, n:n + 1], banks(4 * s, width, r), AX.X, ALU.max, negate=True).then_inc(S["fa_max"], 1)

            def scale(p, n):
                i, h, s = units[n]
                r, width = ROWS[i], min((i + 1) * P, T)
                dve.wait_ge(S["fa_exp"], nth(p, FU, n + 1))
                dve.reciprocal(frs[0:r, n:n + 1], fsum[0:r, n:n + 1])
                dve.drain()
                if n >= 2:
                    dve.wait_ge(S["fa_pt"], nth(p, FU, n - 1))
                dve.tensor_scalar(fpn[0:r, s, 0:width], fp[0:r, s, 0:width], frs[0:r, n:n + 1], None, ALU.mult).then_inc(S["fa_pn"], 1)

            def copy_pT(p, n):
                i, h, s = units[n]
                r = ROWS[i]
                dve.wait_ge(S["fa_pt"], nth(p, FU, n + 1))
                if n >= 2:
                    dve.wait_ge(S["fa_o"], nth(p, FU, n - 1))
                if i < TT:
                    dve.tensor_copy(fpT[:, s, 0:(i + 1) * r], ps[:, 4 * s + 2, 0:(i + 1) * r]).then_inc(S["fa_pT_dve"], 1)
                else:
                    dve.tensor_copy(fpT[:, s, 0:TT * r], ps[:, 4 * s + 2, 0:TT * r])
                    dve.tensor_copy(fpT[0:r, s, TT * r:(TT + 1) * r], ps[0:r, 4 * s + 2, TT * r:(TT + 1) * r]).then_inc(S["fa_pT_dve"], 1)

            with dve.Fori(0, PAIRS) as p:
                for s in range(2):
                    dve.wait_ge(S["fa_xT"], nth(p, 2, s + 1))
                    dve.tensor_scalar(sT[:, s, 0:T], banks(4 * s, T), vcol_f[:, VEC["fg"]:VEC["fg"] + 1],
                                      vcol_f[:, VEC["fc"]:VEC["fc"] + 1], ALU.mult, ALU.add).then_inc(S["fa_hT"], 1)
                def lengths(i):
                    for s in range(2):
                        dve.wait_ge(S["fa_qkv_sb"], nth(p, 2 * TILES, 2 * i + s + 1))
                        dve.tensor_tensor(sq[:, s, i, :], qkv[:, s, i, 0:2 * D], qkv[:, s, i, 0:2 * D], ALU.mult)
                    dve.drain()
                    for s in range(2):
                        dve.tensor_reduce(ss[:, s, i, :], sq[:, s, i, :].rearrange("p (h d) -> p h d", d=FD), AX.X, ALU.add).then_inc(S["fa_ss"], 1)

                for i in range(TILES):
                    lengths(i)
                for g, (t0, t1) in enumerate(CHUNKS):
                    for s in range(2):
                        dve.wait_ge(S["fa_rs"], nth(p, 4, 2 * g + s + 1))
                        qk4 = qkv[:, s, t0:t1, 0:2 * D].rearrange("p t (h d) -> p t h d", d=FD)
                        dve.tensor_tensor(qk4, qk4, ssr[:, s, t0:t1, :].unsqueeze(3).broadcast_to([P, t1 - t0, 2 * FH, FD]), ALU.mult).then_inc(S["fa_norm"], 1)
                for s in range(2):
                    dve.wait_ge(S["fa_T"], nth(p, 4, 2 * s + 1))
                    dve.tensor_scalar(fq[:, s, :], banks(4 * s, T), qkg[:, 0:1], None, ALU.mult).then_inc(S["fa_qT"], 1)
                for n in range(FU + 2):
                    if n < FU:
                        rowmax(p, n)
                    if 1 <= n <= FU:
                        scale(p, n - 1)
                    if n >= 2 and (n - 2) % 2 == 1:
                        copy_pT(p, n - 2)
                for s in range(2):
                    dve.wait_ge(S["y_done"], nth(p, 2, s + 3))
                    for cols in (bass.ds((2 * p + s) * TOK, TOK), bass.ds(BATCH * TOK + (2 * p + s) * TXT, TXT)):
                        op = dve.tensor_copy(y_h[:, cols], y_all[:, cols])
                    op.then_inc(S["y_high"], 1)

            dve.memset(lg[:, :, :], 0.0)
            dve.wait_ge(S["g_ps"], 1)
            dve.drain()
            for rows_, t0, t1 in ((P, 0, GT - 1), (TXT_ROWS[-1], GT - 1, GT)):
                dve.tensor_tensor(lg[0:rows_, t0:t1, :], ps[0:rows_, 7, t0 * E:t1 * E].rearrange("p (t e) -> p t e", e=E),
                                  gb_r[0:rows_, :].unsqueeze(1).broadcast_to([rows_, t1 - t0, E]), ALU.add)
            dve.drain()
            dve.tensor_reduce(lgm[:, :], lg[:, :, :], AX.X, ALU.max, negate=True)
            dve.drain()
            dve.tensor_tensor(lg[:, :, :], lg[:, :, :], lgm[:, :].unsqueeze(2).broadcast_to([P, GT, E]), ALU.add).then_inc(S["g_shift"], 1)
            dve.wait_ge(S["g_exp"], 1)
            dve.tensor_reduce(lgm[:, :], lg[:, :, :], AX.X, ALU.add)
            dve.drain()
            dve.reciprocal(lgm[:, :], lgm[:, :])
            dve.drain()
            dve.tensor_tensor(gate[:, :, :], lg[:, :, :], lgm[:, :].unsqueeze(2).broadcast_to([P, GT, E]), ALU.mult)
            dve.drain()
            dve.tensor_copy(gate_parts[:, :, 0, :], gate[:, :, :])
            dve.tensor_tensor(gate_sel[:, :, :], ident[0:2 * E, 0:E].unsqueeze(2).broadcast_to([2 * E, E, P]),
                              ident[0:2 * E, E:2 * E].unsqueeze(2).broadcast_to([2 * E, E, P]), ALU.add)
            dve.drain()
            dve.tensor_tensor(gate_parts[:, :, 1, :], gate[:, :, :], gate_parts[:, :, 0, :].bitcast(F32), ALU.subtract)
            dve.drain()

            def finish(c, rows, tile_at):
                dve.wait_ge(S["y_turned"], nth(c, 1, 1))
                for i, r in enumerate(rows):
                    at_ = tile_at(i, r)
                    op = dve.tensor_tensor(at_, ps[0:r, 5, i * P:(i + 1) * P].unsqueeze(1), at_, ALU.add)
                op.then_inc(S["chunk_done"], 1)

            def signal_tile(c):
                return lambda i, r: seq[0:r, bass.ds(c * TILES + i, 1), :]

            def experts(c, rows, first=False):
                width = sum(rows)

                def low(e, f):
                    n = e * EK + f
                    dve.wait_ge(S["up_done"], nth(c, E * EK, n + 1))
                    dve.tensor_tensor(hid_l[:, e % 2, f, 0:width], hid[:, n % 4, 0:width],
                                      hid_h[:, e % 2, f, 0:width].bitcast(F32), ALU.subtract).then_inc(S["hid_split"], 1)

                def gated_product(e):
                    dve.wait_ge(S["gate_ps"], nth(c, E, e + 1))
                    dve.tensor_copy(gated[:, e % 2, 0:width], ps[:, 6 + e % 2, 0:width])
                    dve.drain()
                    dve.wait_ge(S["down"], nth(c, E, e + 1))
                    dve.tensor_tensor(gated[:, e % 2, 0:width], ps[:, 4 + (e + 1) % 2, 0:width], gated[:, e % 2, 0:width], ALU.mult).then_inc(S["acc_used"], 1)

                def accumulate(e):
                    op = dve.tensor_tensor(acc[:, 0:width], gated[:, e % 2, 0:width], acc[:, 0:width], ALU.add)
                    if e == E - 1:
                        op.then_inc(S["acc_done"], 1)

                dve.tensor_copy(gate_c[:, 0:len(rows), :], gate_parts[:, bass.ds(c * TT, len(rows)), :, :].bitcast(F32)
                                .rearrange("p t k e -> p t (k e)")).then_inc(S["g_chunk"], 1)
                low(0, 0)
                low(0, 1)
                dve.wait_ge(S["g_tps"], nth(c, 1, 1))
                dve.tensor_copy(gateT[:, 0:width], ps[0:2 * E, 6, 0:width]).then_inc(S["g_T"], 1)
                low(0, 2)
                low(0, 3)
                if not first:
                    finish(c - 1, [P] * TT, signal_tile(c - 1))
                for f in range(EK):
                    low(1, f)
                dve.wait_ge(S["b2_ps"], nth(c, 1, 1))
                dve.tensor_copy(acc[:, 0:width], ps[:, 4, 0:width]).then_inc(S["acc_init"], 1)
                for e in range(E):
                    gated_product(e)
                    if e + 2 < E:
                        low(e + 2, 0)
                    dve.drain()
                    accumulate(e)
                    if e + 2 < E:
                        for f in range(1, EK):
                            low(e + 2, f)

            experts(0, [P] * TT, first=True)
            with dve.Fori(1, BATCH) as c:
                experts(c, [P] * TT)
            dve.wait_ge(S["txt_moved"], 16 * len(TXT_PIECES))
            experts(BATCH, TXT_ROWS)
            finish(BATCH, TXT_ROWS, lambda i, r: txt_acc[0:r, i:i + 1, :])

        @block.scalar
        def _(act):

            def tok_exp(b, n):
                act.wait_ge(S["max_ready"], nth(b, UNITS, n + 1))
                if n >= 2:
                    act.wait_ge(S["probT_full"], nth(b, UNITS, n - 1))
                act.activation(prob[:, n % 2, :], ps[:, n % 2, :], ACT.Exp, bias=nmax[:, n:n + 1],
                               accum_out=psum_e[:, n:n + 1]).then_inc(S["prob_ready"], 1)

            def tok_probT(b, n):
                act.wait_ge(S["probT_full"], nth(b, UNITS, n + 1))
                act.activation(probT[:, n % 2, :], ps[:, BANK_T, :], ACT.Copy).then_inc(S["probT_ready"], 1)

            def txt_exp(l, b):
                act.wait_ge(S["tx_shift"], nth(l, BATCH, b + 1))
                act.activation(ts[:, b, :], ts[:, b, :], ACT.Exp).then_inc(S["tx_exp"], 1)

            def txt_pT(l, b, g):
                act.wait_ge(S["tx_pt"], nth(l, 2 * BATCH, 2 * b + g + 1))
                act.activation(tpT[:, b, g * HALF:(g + 1) * HALF], ps[0:TXT, BANK_TPT, 0:HALF], ACT.Copy).then_inc(S["tx_pT"], 1)

            def txt_gelu(l):
                for j in range(KT):
                    act.wait_ge(S["tx_f1"], nth(l, KT, j + 1))
                    act.activation(gact[:, j, :], ps[:, BANKS_UP[j], 0:SEQ4], ACT.Gelu,
                                   bias=vcol[:, bass.ds(VEC["b1"] + l * KT + j, 1)]).then_inc(S["tx_g"], 1)

            def tok_xT(b):
                act.wait_ge(S["proj_full"], nth(b, 5, 1))
                act.activation(xT[:, :], ps[:, BANK_XT, :], ACT.Copy).then_inc(S["xT_ready"], 1)

            def tok_high(b):
                for k, (high, bank) in enumerate(((q_high, BANK_Q), (k_high, BANK_K))):
                    act.wait_ge(S["proj_full"], nth(b, 5, k + 2))
                    act.activation(high[:, :], ps[:, bank, :], ACT.Copy).then_inc(S["qk_high"], 1)

            def first_loop_turn(t, last=False):
                act.wait_ge(S["proj_full"], nth(t, 5, 4))
                act.activation(v_tok[:, 0:2, :], ps[:, BANK_V, :], ACT.Copy).then_inc(S["va_ready"], 1)
                act.wait_ge(S["proj_full"], nth(t, 5, 5))
                act.activation(v_tok[:, 2:4, :], ps[:, BANK_V + 1, :], ACT.Copy).then_inc(S["vb_ready"], 1)
                for n in range(UNITS + 2):
                    if n < UNITS:
                        tok_exp(t, n)
                    if n == AT_PROJECT:
                        act.wait_ge(S["tx_q"], nth(t, 1, 1))
                        act.activation(tqT[:, :], ps[:, BANK_TQ, 0:SEQ4], ACT.Identity, bias=bq4[:, bass.ds(t, 1)], scale=HD ** -0.5).then_inc(S["tx_qs"], 1)
                    if n in AT_TURN:
                        txt_pT(t, AT_TURN.index(n), 0)
                    if n == AT_CTX_TURN:
                        act.wait_ge(S["tx_ct"], nth(t, 1, 1))
                        act.activation(cT[:, :], ps[:, BANK_TX, 0:SEQ4], ACT.Copy).then_inc(S["tx_cT"], 1)
                    if n == UNITS and not last:
                        tok_xT(t + 1)
                    if 1 <= n <= UNITS:
                        tok_probT(t, n - 1)
                    if n in AT_TURN:
                        txt_pT(t, AT_TURN.index(n), 1)
                    if n in AT_SCORES:
                        txt_exp(t, AT_SCORES.index(n))
                    if n == AT_UP:
                        txt_gelu(t)
                    if n == UNITS + 1 and not last:
                        tok_high(t + 1)

            tok_xT(0)
            tok_high(0)
            act.wait_ge(S["setup_done"], 1)
            with act.Fori(0, BATCH - 1) as t:
                first_loop_turn(t)
            first_loop_turn(BATCH - 1, last=True)

            act.wait_ge(S["l_wT"], 1)
            act.activation(w_lT[:, :], banks(0, 6 * P), ACT.Copy)
            act.activation(vcol_f[:, :], ps[:, 3, 0:NVEC[1]], ACT.Copy)
            act.activation(w_loT[:, :, :], ps[:, 2, :].rearrange("p (g n) -> p g n", g=4), ACT.Copy)
            act.drain().then_inc(S["l_wT_done"], 1)

            def normalise5(p, s, tiles, rs, nb, done):
                for i in tiles:
                    k = (2 * p + s) * TILES + i
                    op = act.activation(xn[:, s, i, :], seq[:, bass.ds(k, 1), :].rearrange("p a d -> p (a d)"), ACT.Identity,
                                        bias=nb[:, bass.ds(k, 1)], scale=rs[:, bass.ds(k, 1)])
                op.then_inc(S[done], 1)

            with act.Fori(0, PAIRS) as p:
                act.wait_ge(S["rstd_lin"], BATCH)
                for s in range(2):
                    normalise5(p, s, range(TT), rs_l, nb_l, "la_norm")
                for s in range(2):
                    act.wait_ge(S["la_normT"], nth(p, 4, s + 1))
                    act.activation(sT[:, s, 0:TOK], ps[:, 4 * s, :], ACT.Copy).then_inc(S["la_hT"], 1)

                def exps(s, text):
                    cols = slice(TOK, T) if text else slice(0, TOK)
                    for k, part in enumerate((lt1, lt2)):
                        act.wait_ge(S["la_min"], nth(p, 8, 4 * text + 2 * s + k + 1))
                        act.activation(part[:, s, cols], part[:, s, cols], ACT.Exp).then_inc(S["la_exp"], 1)

                def values(i):
                    for s in range(2):
                        act.wait_ge(S["la_vfull"], nth(p, 2 * TILES, 2 * i + s + 1))
                        act.activation(lv[:, s, i, :], ps[:, 4 * s + BANK_LV, :], ACT.Copy).then_inc(S["la_vdone"], 1)

                exps(0, 0)
                values(0)
                exps(1, 0)
                values(1)
                act.wait_ge(S["rstd_lin"], BATCH + 1)
                for s in range(2):
                    normalise5(p, s, [TT], rs_l, nb_l, "la_norm")
                for s in range(2):
                    act.wait_ge(S["la_normT"], nth(p, 4, s + 3))
                    act.activation(sT[:, s, TOK:T], ps[:, 4 * s + BANK_LTXT, 0:TXT], ACT.Copy).then_inc(S["la_hT"], 1)
                values(2)
                values(3)
                exps(0, 1)
                exps(1, 1)
                values(4)
                for s in range(2):
                    act.wait_ge(S["la_ktps"], nth(p, 2, s + 1))
                    act.activation(lktok[:, s, :, :], ps[:, 4 * s + BANK_LK, :].rearrange("p (t d) -> p t d", t=TT), ACT.Copy).then_inc(S["la_ktok"], 1)
                for i in range(TILES):
                    for s in range(2):
                        r = ROWS[i]
                        act.wait_ge(S["la_ot"], nth(p, 2 * TILES, 2 * i + s + 1))
                        act.activation(lo[:, s, :, 0:r], ps[:, 4 * s, 0:4 * r].rearrange("p (g t) -> p g t", g=4), ACT.Copy).then_inc(S["la_lo"], 1)

            act.sem_inc(S["y_done"], 2)
            units = [(i, h, s) for i in TILE_ORDER for h in range(FH) for s in range(2)]

            def exp(p, n):
                i, h, s = units[n]
                r, width = ROWS[i], min((i + 1) * P, T)
                act.wait_ge(S["fa_max"], nth(p, FU, n + 1))
                if n >= 2:
                    act.wait_ge(S["fa_pn"], nth(p, FU, n - 1))
                act.activation(fp[0:r, s, 0:width], banks(4 * s, width, r), ACT.Exp, bias=fnm[0:r, n:n + 1],
                               accum_out=fsum[0:r, n:n + 1]).then_inc(S["fa_exp"], 1)

            def copy_pT(p, n):
                i, h, s = units[n]
                r = ROWS[i]
                act.wait_ge(S["fa_pt"], nth(p, FU, n + 1))
                if n >= 2:
                    act.wait_ge(S["fa_o"], nth(p, FU, n - 1))
                if i < TT:
                    act.activation(fpT[:, s, 0:(i + 1) * r], ps[:, 4 * s + 2, 0:(i + 1) * r], ACT.Copy).then_inc(S["fa_pT_act"], 1)
                else:
                    act.activation(fpT[:, s, 0:TT * r], ps[:, 4 * s + 2, 0:TT * r], ACT.Copy)
                    act.activation(fpT[0:r, s, TT * r:(TT + 1) * r], ps[0:r, 4 * s + 2, TT * r:(TT + 1) * r], ACT.Copy).then_inc(S["fa_pT_act"], 1)

            def copy_oT(p, n):
                i, h, s = units[n]
                if h == FH - 1:
                    r = ROWS[i]
                    act.wait_ge(S["fa_o"], nth(p, FU, n + 1))
                    act.activation(foT[:, s, i * P:i * P + r], ps[:, 4 * s + 3, 0:r], ACT.Copy).then_inc(S["fa_oT"], 1)

            with act.Fori(0, PAIRS) as p:
                act.wait_ge(S["rstd_h"], nth(p, 1, 1))
                for s in range(2):
                    normalise5(p, s, range(TILES), rs_f, nb_f, "fa_xn")
                for i in range(TILES):
                    for s in range(2):
                        act.wait_ge(S["fa_qkv"], nth(p, 2 * TILES, 2 * i + s + 1))
                        act.activation(qkv[:, s, i, :], ps[:, 4 * s + 2 + i % 2, 0:3 * D], ACT.Copy).then_inc(S["fa_qkv_sb"], 1)
                for s in range(2):
                    act.wait_ge(S["fa_T"], nth(p, 4, 2 * s + 2))
                    act.activation(fk[:, s, :], banks(4 * s + 2, T), ACT.Copy).then_inc(S["fa_kT"], 1)
                for n in range(FU + 4):
                    if n < FU:
                        exp(p, n)
                    if 2 <= n < FU + 2 and (n - 2) % 2 == 0:
                        copy_pT(p, n - 2)
                    if n >= 4:
                        copy_oT(p, n - 4)
                for s in range(2):
                    act.wait_ge(S["y_ps"], nth(p, 2, s + 1))
                    act.activation(y_all[:, bass.ds((2 * p + s) * TOK, TOK)], ps[:, 4 * s, :], ACT.Copy)
                    act.activation(y_all[:, bass.ds(BATCH * TOK + (2 * p + s) * TXT, TXT)], ps[:, 4 * s + 1, 0:TXT], ACT.Copy).then_inc(S["y_done"], 1)

            act.wait_ge(S["g_shift"], 1)
            act.activation(lg[:, :, :], lg[:, :, :], ACT.Exp).then_inc(S["g_exp"], 1)

            def experts(c, width):
                for n in range(E * EK):
                    e, f = divmod(n, EK)
                    act.wait_ge(S["up"], nth(c, E * EK, n + 1))
                    if n >= 4:
                        act.wait_ge(S["hid_split"], nth(c, E * EK, n - 3))
                    if f == 0 and e >= 2:
                        act.wait_ge(S["down"], nth(c, E, e - 1))
                    bias = vcol_f[:, VEC["eb"] + n:VEC["eb"] + n + 1]
                    act.activation(hid[:, n % 4, 0:width], ps[:, n % 4, 0:width], ACT.Gelu_apprx_tanh, bias=bias)
                    act.activation(hid_h[:, e % 2, f, 0:width], ps[:, n % 4, 0:width], ACT.Gelu_apprx_tanh, bias=bias).then_inc(S["up_done"], 1)

            with act.Fori(0, BATCH) as c:
                experts(c, TOK)
            experts(BATCH, BATCH * TXT)


N_PARAMS = 2 + 6 + 1 + 1 + 1

def kernel(**inputs):
    import numpy as np
    import concourse.bacc as bacc
    from concourse.bass_utils import run_bass_kernel_spmd

    nc = bacc.Bacc("TRN2", target_bir_lowering=False, num_devices=1)
    arrays, aps = {}, {}
    for name, value in inputs.items():
        a = np.ascontiguousarray(value)
        arrays["in_" + name] = a
        aps[name] = nc.dram_tensor("in_" + name, a.shape, mybir.dt.from_np(a.dtype), kind="ExternalInput").ap()
    out = nc.dram_tensor("out", (BATCH, T, D), F32, kind="ExternalOutput").ap()
    fusion_kernel(nc, aps, out)
    r = run_bass_kernel_spmd(nc, [arrays], core_ids=[0])
    return r.results[0]["out"]
```
